# Optimizing a Trainium2 kernel written in Bass

```python
import numpy as np
import jax
import jax.numpy as jnp

def _softmax(x, axis=-1):
    return jax.nn.softmax(x, axis=axis)

def _gelu(x):
    return jax.nn.gelu(x, approximate=True)

def _silu(x):
    return jax.nn.silu(x)

def _sigmoid(x):
    return jax.nn.sigmoid(x)

def _layernorm(x, axis=-1, eps=1e-05):
    m = jnp.mean(x, axis=axis, keepdims=True)
    v = jnp.var(x, axis=axis, keepdims=True)
    return (x - m) / jnp.sqrt(v + eps)

def _scatter_add(tgt, idx, src, axis=0):
    return tgt.at[idx].add(src)

def _segment_sum(src, seg, n):
    return jax.ops.segment_sum(src, seg, n)
kernel_name = 'mk_gnn_preln_d2_gnn_r32_77c346'

def setup_inputs(seed: int=0):
    np.random.seed(seed)
    _w = jnp.asarray

    def _rec_inputs():
        import jax
        import jax.numpy as jnp
        _gk = jax.random.key(seed)
        x = -0.000202 + 1 * jax.random.normal(jax.random.fold_in(_gk, 1), (3125, 160), jnp.float32)
        _s = jax.random.randint(jax.random.fold_in(_gk, 2), (25000,), 0, 3125, jnp.int32)
        _d = jax.random.randint(jax.random.fold_in(_gk, 3), (25000,), 0, 3125, jnp.int32)
        _loop = jnp.arange(3125, dtype=jnp.int32)
        src = jnp.concatenate([_s, _d, _loop])
        dst = jnp.concatenate([_d, _s, _loop])
        _o = jnp.argsort(dst, stable=True)
        src = src[_o]
        dst = dst[_o]
        edge_attr_4 = 0.0012443 + 1.0001 * jax.random.normal(jax.random.fold_in(_gk, 12), (53125, 4), jnp.float32)
        edge_attr_64 = 0.000127647 + 1.00004 * jax.random.normal(jax.random.fold_in(_gk, 13), (53125, 64), jnp.float32)
        node_vec1 = jax.random.uniform(jax.random.fold_in(_gk, 15), (3125, 1), jnp.float32, 0.0, 1)
        return (x, src, dst, edge_attr_4, edge_attr_64, node_vec1)
    x, src, dst, edge_attr_4, edge_attr_64, node_vec1 = _rec_inputs()

    def _L0_gnn_setup():
        import jax, jax.numpy as jnp
        import numpy as np
        N, E = (1250, 20000)
        S_IN, V_IN = (64, 32)
        S_MID, V_MID = (96, 128)
        S_OUT, V_OUT = (96, 32)
        R = 64
        FC_HID = 64
        W_NUMEL = 64 + 64 + 32 + 32 + 32
        NUM_NEIGHBORS = 16.0

        def _inv(d):
            return 1.0 / jnp.sqrt(jnp.float32(d))

        def _forward(node_features, node_attr, edge_attr, edge_scalars, lin1_ws, lin1_wv, fc_w1, fc_w2, sc_ws, sc_wv, lin2_ws, lin2_wv, edge_src, edge_dst):
            n = node_features.shape[0]
            s = node_features[:, :S_IN]
            v = node_features[:, S_IN:].reshape(n, V_IN, 3)
            a = node_attr
            sc_s = s @ sc_ws * a * _inv(S_IN)
            sc_v = jnp.einsum('nci,cd->ndi', v, sc_wv) * a[:, :, None] * _inv(V_IN)
            h_s = s @ lin1_ws * a * _inv(S_IN)
            h_v = jnp.einsum('nci,cd->ndi', v, lin1_wv) * a[:, :, None] * _inv(V_IN)
            hid = jax.nn.silu(edge_scalars @ fc_w1 * _inv(R))
            w = hid @ fc_w2 * _inv(FC_HID)
            w1, w2, w3, w4, w5 = jnp.split(w, [64, 128, 160, 192], axis=-1)
            es = h_s[edge_src]
            ev = h_v[edge_src]
            e0 = edge_attr[:, :1]
            e1 = edge_attr[:, 1:4]
            m_s1 = w1 * es * e0
            m_s2 = w4 * jnp.einsum('eci,ei->ec', ev, e1) * _inv(3)
            m_v1 = (w2 * es)[:, :, None] * e1[:, None, :]
            m_v2 = w3[:, :, None] * ev * e0[:, :, None]
            m_v3 = w5[:, :, None] * jnp.cross(ev, e1[:, None, :]) * _inv(2)
            mid_s = jnp.concatenate([m_s1, m_s2], axis=-1)
            mid_v = jnp.concatenate([m_v1, m_v2, m_v3], axis=1)
            inv_nn = 1.0 / jnp.sqrt(jnp.float32(NUM_NEIGHBORS))
            agg_s = jax.ops.segment_sum(mid_s, edge_dst, num_segments=n) * inv_nn
            agg_v = jax.ops.segment_sum(mid_v, edge_dst, num_segments=n) * inv_nn
            o_s = agg_s @ lin2_ws * a * _inv(S_MID)
            o_v = jnp.einsum('nci,cd->ndi', agg_v, lin2_wv) * a[:, :, None] * _inv(V_MID)
            pre_s = sc_s + o_s
            pre_v = sc_v + o_v
            scalars = jax.nn.silu(pre_s[:, :64])
            gates = jax.nn.sigmoid(pre_s[:, 64:96])
            gated = gates[:, :, None] * pre_v
            return jnp.concatenate([scalars, gated.reshape(n, 3 * V_OUT)], axis=-1)
        key = jax.random.key(seed)
        ks = jax.random.split(key, 13)
        return {'node_features': jax.random.normal(ks[0], (N, S_IN + 3 * V_IN), jnp.float32), 'node_attr': jnp.ones((N, 1), jnp.float32), 'edge_src': jax.random.randint(ks[1], (E,), 0, N), 'edge_dst': jax.random.randint(ks[2], (E,), 0, N), 'edge_attr': jax.random.normal(ks[3], (E, 4), jnp.float32), 'edge_scalars': jax.random.normal(ks[4], (E, R), jnp.float32), 'lin1_ws': jax.random.normal(ks[5], (S_IN, S_IN), jnp.float32), 'lin1_wv': jax.random.normal(ks[6], (V_IN, V_IN), jnp.float32), 'fc_w1': jax.random.normal(ks[7], (R, FC_HID), jnp.float32), 'fc_w2': jax.random.normal(ks[8], (FC_HID, W_NUMEL), jnp.float32), 'sc_ws': jax.random.normal(ks[9], (S_IN, S_OUT), jnp.float32), 'sc_wv': jax.random.normal(ks[10], (V_IN, V_OUT), jnp.float32), 'lin2_ws': jax.random.normal(ks[11], (S_MID, S_OUT), jnp.float32), 'lin2_wv': jax.random.normal(ks[12], (V_MID, V_OUT), jnp.float32)}
    _L0_gnn_all = _L0_gnn_setup()
    _L0_gnn_in = {k: v for k, v in _L0_gnn_all.items() if k in ('lin1_ws', 'lin1_wv', 'fc_w1', 'fc_w2', 'sc_ws', 'sc_wv', 'lin2_ws', 'lin2_wv')}
    del _L0_gnn_all

    def _L1_gnn_setup():
        import jax, jax.numpy as jnp
        import numpy as np
        MUL0, MUL1 = (64, 32)
        INV_SQRT3 = 1.0 / np.sqrt(3.0)

        def _split(x):
            return (x[:, :MUL0], x[:, MUL0:].reshape(x.shape[0], MUL1, 3))

        def _merge(o0, o1):
            return jnp.concatenate([o0, o1.reshape(o1.shape[0], -1)], axis=-1)

        def _tp(x0, x1, y0, y1, w000, w011, w101, w110):
            fan0 = x0.shape[1] * y0.shape[1] + x1.shape[1] * y1.shape[1]
            fan1 = x0.shape[1] * y1.shape[1] + x1.shape[1] * y0.shape[1]
            out0 = (jnp.einsum('eu,ev,uvw->ew', x0, y0, w000) + INV_SQRT3 * jnp.einsum('euk,evk,uvw->ew', x1, y1, w110)) / np.sqrt(fan0)
            out1 = (jnp.einsum('eu,evk,uvw->ewk', x0, y1, w011) + jnp.einsum('euk,ev,uvw->ewk', x1, y0, w101)) / np.sqrt(fan1)
            return (out0, out1)

        def _lin(x0, x1, w0, w1):
            return (x0 @ w0 / np.sqrt(x0.shape[1]), jnp.einsum('euk,uv->evk', x1, w1) / np.sqrt(x1.shape[1]))
        key = jax.random.key(seed)
        ks = jax.random.split(key, 20)
        N, E = (50000, 15625)
        inp = {'node_features': jax.random.normal(ks[0], (N, MUL0 + 3 * MUL1), dtype=jnp.float32), 'edge_index': jax.random.randint(ks[1], (2, E), 0, N, dtype=jnp.int64), 'edge_attr_tensor': jax.random.normal(ks[2], (E, 4), dtype=jnp.float32), 'node_attr_scalar_raw': jax.random.normal(ks[3], (N, 1), dtype=jnp.float32), 'wm000': jax.random.normal(ks[4], (MUL0, 1, MUL0), dtype=jnp.float32), 'wm011': jax.random.normal(ks[5], (MUL0, 1, MUL1), dtype=jnp.float32), 'wm101': jax.random.normal(ks[6], (MUL1, 1, MUL1), dtype=jnp.float32), 'wm110': jax.random.normal(ks[7], (MUL1, 1, MUL0), dtype=jnp.float32), 'lm0': jax.random.normal(ks[8], (MUL0, MUL0), dtype=jnp.float32), 'lm1': jax.random.normal(ks[9], (MUL1, MUL1), dtype=jnp.float32), 'wu000': jax.random.normal(ks[10], (MUL0, MUL0, MUL0), dtype=jnp.float32), 'wu011': jax.random.normal(ks[11], (MUL0, MUL1, MUL1), dtype=jnp.float32), 'wu101': jax.random.normal(ks[12], (MUL1, MUL0, MUL1), dtype=jnp.float32), 'wu110': jax.random.normal(ks[13], (MUL1, MUL1, MUL0), dtype=jnp.float32), 'lu0': jax.random.normal(ks[14], (MUL0, MUL0), dtype=jnp.float32), 'lu1': jax.random.normal(ks[15], (MUL1, MUL1), dtype=jnp.float32)}
        return inp
    _L1_gnn_all = _L1_gnn_setup()
    _L1_gnn_in = {k: v for k, v in _L1_gnn_all.items() if k in ('wm000', 'wm011', 'wm101', 'wm110', 'lm0', 'lm1', 'wu000', 'wu011', 'wu101', 'wu110', 'lu0', 'lu1')}
    del _L1_gnn_all
    return {'x': x, 'src': src, 'dst': dst, 'edge_attr_4': edge_attr_4, 'edge_attr_64': edge_attr_64, 'node_vec1': node_vec1, 'L0_gnn_lin1_ws': _L0_gnn_in['lin1_ws'], 'L0_gnn_lin1_wv': _L0_gnn_in['lin1_wv'], 'L0_gnn_fc_w1': _L0_gnn_in['fc_w1'], 'L0_gnn_fc_w2': _L0_gnn_in['fc_w2'], 'L0_gnn_sc_ws': _L0_gnn_in['sc_ws'], 'L0_gnn_sc_wv': _L0_gnn_in['sc_wv'], 'L0_gnn_lin2_ws': _L0_gnn_in['lin2_ws'], 'L0_gnn_lin2_wv': _L0_gnn_in['lin2_wv'], 'L1_gnn_wm000': _L1_gnn_in['wm000'], 'L1_gnn_wm011': _L1_gnn_in['wm011'], 'L1_gnn_wm101': _L1_gnn_in['wm101'], 'L1_gnn_wm110': _L1_gnn_in['wm110'], 'L1_gnn_lm0': _L1_gnn_in['lm0'], 'L1_gnn_lm1': _L1_gnn_in['lm1'], 'L1_gnn_wu000': _L1_gnn_in['wu000'], 'L1_gnn_wu011': _L1_gnn_in['wu011'], 'L1_gnn_wu101': _L1_gnn_in['wu101'], 'L1_gnn_wu110': _L1_gnn_in['wu110'], 'L1_gnn_lu0': _L1_gnn_in['lu0'], 'L1_gnn_lu1': _L1_gnn_in['lu1']}

def reference(x, src, dst, edge_attr_4, edge_attr_64, node_vec1, L0_gnn_lin1_ws, L0_gnn_lin1_wv, L0_gnn_fc_w1, L0_gnn_fc_w2, L0_gnn_sc_ws, L0_gnn_sc_wv, L0_gnn_lin2_ws, L0_gnn_lin2_wv, L1_gnn_wm000, L1_gnn_wm011, L1_gnn_wm101, L1_gnn_wm110, L1_gnn_lm0, L1_gnn_lm1, L1_gnn_wu000, L1_gnn_wu011, L1_gnn_wu101, L1_gnn_wu110, L1_gnn_lu0, L1_gnn_lu1):
    import jax
    import jax.numpy as jnp

    def _L0_gnn_ref(node_features, node_attr, edge_src, edge_dst, edge_attr, edge_scalars, lin1_ws, lin1_wv, fc_w1, fc_w2, sc_ws, sc_wv, lin2_ws, lin2_wv):
        import jax, jax.numpy as jnp
        import numpy as np
        N, E = (1250, 20000)
        S_IN, V_IN = (64, 32)
        S_MID, V_MID = (96, 128)
        S_OUT, V_OUT = (96, 32)
        R = 64
        FC_HID = 64
        W_NUMEL = 64 + 64 + 32 + 32 + 32
        NUM_NEIGHBORS = 16.0

        def _inv(d):
            return 1.0 / jnp.sqrt(jnp.float32(d))

        def _forward(node_features, node_attr, edge_attr, edge_scalars, lin1_ws, lin1_wv, fc_w1, fc_w2, sc_ws, sc_wv, lin2_ws, lin2_wv, edge_src, edge_dst):
            n = node_features.shape[0]
            s = node_features[:, :S_IN]
            v = node_features[:, S_IN:].reshape(n, V_IN, 3)
            a = node_attr
            sc_s = s @ sc_ws * a * _inv(S_IN)
            sc_v = jnp.einsum('nci,cd->ndi', v, sc_wv) * a[:, :, None] * _inv(V_IN)
            h_s = s @ lin1_ws * a * _inv(S_IN)
            h_v = jnp.einsum('nci,cd->ndi', v, lin1_wv) * a[:, :, None] * _inv(V_IN)
            hid = jax.nn.silu(edge_scalars @ fc_w1 * _inv(R))
            w = hid @ fc_w2 * _inv(FC_HID)
            w1, w2, w3, w4, w5 = jnp.split(w, [64, 128, 160, 192], axis=-1)
            es = h_s[edge_src]
            ev = h_v[edge_src]
            e0 = edge_attr[:, :1]
            e1 = edge_attr[:, 1:4]
            m_s1 = w1 * es * e0
            m_s2 = w4 * jnp.einsum('eci,ei->ec', ev, e1) * _inv(3)
            m_v1 = (w2 * es)[:, :, None] * e1[:, None, :]
            m_v2 = w3[:, :, None] * ev * e0[:, :, None]
            m_v3 = w5[:, :, None] * jnp.cross(ev, e1[:, None, :]) * _inv(2)
            mid_s = jnp.concatenate([m_s1, m_s2], axis=-1)
            mid_v = jnp.concatenate([m_v1, m_v2, m_v3], axis=1)
            inv_nn = 1.0 / jnp.sqrt(jnp.float32(NUM_NEIGHBORS))
            agg_s = jax.ops.segment_sum(mid_s, edge_dst, num_segments=n) * inv_nn
            agg_v = jax.ops.segment_sum(mid_v, edge_dst, num_segments=n) * inv_nn
            o_s = agg_s @ lin2_ws * a * _inv(S_MID)
            o_v = jnp.einsum('nci,cd->ndi', agg_v, lin2_wv) * a[:, :, None] * _inv(V_MID)
            pre_s = sc_s + o_s
            pre_v = sc_v + o_v
            scalars = jax.nn.silu(pre_s[:, :64])
            gates = jax.nn.sigmoid(pre_s[:, 64:96])
            gated = gates[:, :, None] * pre_v
            return jnp.concatenate([scalars, gated.reshape(n, 3 * V_OUT)], axis=-1)
        return _forward(node_features, node_attr, edge_attr, edge_scalars, lin1_ws, lin1_wv, fc_w1, fc_w2, sc_ws, sc_wv, lin2_ws, lin2_wv, edge_src, edge_dst)

    def _L1_gnn_ref(node_features, edge_index, edge_attr_tensor, node_attr_scalar_raw, wm000, wm011, wm101, wm110, lm0, lm1, wu000, wu011, wu101, wu110, lu0, lu1):
        import jax, jax.numpy as jnp
        import numpy as np
        MUL0, MUL1 = (64, 32)
        INV_SQRT3 = 1.0 / np.sqrt(3.0)

        def _split(x):
            return (x[:, :MUL0], x[:, MUL0:].reshape(x.shape[0], MUL1, 3))

        def _merge(o0, o1):
            return jnp.concatenate([o0, o1.reshape(o1.shape[0], -1)], axis=-1)

        def _tp(x0, x1, y0, y1, w000, w011, w101, w110):
            fan0 = x0.shape[1] * y0.shape[1] + x1.shape[1] * y1.shape[1]
            fan1 = x0.shape[1] * y1.shape[1] + x1.shape[1] * y0.shape[1]
            out0 = (jnp.einsum('eu,ev,uvw->ew', x0, y0, w000) + INV_SQRT3 * jnp.einsum('euk,evk,uvw->ew', x1, y1, w110)) / np.sqrt(fan0)
            out1 = (jnp.einsum('eu,evk,uvw->ewk', x0, y1, w011) + jnp.einsum('euk,ev,uvw->ewk', x1, y0, w101)) / np.sqrt(fan1)
            return (out0, out1)

        def _lin(x0, x1, w0, w1):
            return (x0 @ w0 / np.sqrt(x0.shape[1]), jnp.einsum('euk,uv->evk', x1, w1) / np.sqrt(x1.shape[1]))
        N = node_features.shape[0]
        row, col = (edge_index[0], edge_index[1])
        r_vec = edge_attr_tensor[:, :3]
        dist = edge_attr_tensor[:, 3:4]
        e0 = dist
        e1 = r_vec[:, None, :]
        xj0, xj1 = _split(node_features[col])
        m0, m1 = _tp(xj0, xj1, e0, e1, wm000, wm011, wm101, wm110)
        d0, d1 = _lin(xj0, xj1, lm0, lm1)
        msgs = _merge(m0 + d0, m1 + d1)
        agg = jax.ops.segment_sum(msgs, row, num_segments=N)
        a0, a1 = _split(agg)
        x0, x1 = _split(node_features)
        u0, u1 = _tp(x0, x1, a0, a1, wu000, wu011, wu101, wu110)
        ud0, ud1 = _lin(x0, x1, lu0, lu1)
        return node_features + _merge(u0 + ud0, u1 + ud1)
    edge_index = jnp.stack([src, dst])
    h = jnp.maximum(_layernorm(x, axis=-1), 0.0)
    x = x + _L0_gnn_ref(h, node_vec1, src, dst, edge_attr_4, edge_attr_64, L0_gnn_lin1_ws, L0_gnn_lin1_wv, L0_gnn_fc_w1, L0_gnn_fc_w2, L0_gnn_sc_ws, L0_gnn_sc_wv, L0_gnn_lin2_ws, L0_gnn_lin2_wv)
    h = jnp.maximum(_layernorm(x, axis=-1), 0.0)
    x = x + _L1_gnn_ref(h, edge_index, edge_attr_4, node_vec1, L1_gnn_wm000, L1_gnn_wm011, L1_gnn_wm101, L1_gnn_wm110, L1_gnn_lm0, L1_gnn_lm1, L1_gnn_wu000, L1_gnn_wu011, L1_gnn_wu101, L1_gnn_wu110, L1_gnn_lu0, L1_gnn_lu1)
    return x

_drawn_inputs = setup_inputs


def setup_inputs(seed=0):
    import zlib

    import numpy as np

    out = dict(_drawn_inputs(seed))
    spreads = {}
    factors = {}
    for name, (base, spread) in spreads.items():
        noise = np.random.default_rng([zlib.crc32(name.encode()), seed]).standard_normal(out[name].shape)
        drawn = base * np.exp(spread * noise) if base else spread * noise
        out[name] = jnp.asarray(drawn.astype(out[name].dtype))
    for name, factor in factors.items():
        out[name] = (out[name] * factor).astype(out[name].dtype)
    return out
```

```python
import concourse.bass as bass
from concourse import mybir
from contextlib import ExitStack

P = 128
N_NODES, N_EDGES = 3125, 53125
S_CH, V_CH = 64, 32
D = S_CH + 3 * V_CH
NODE_TILES = 2 * (-(-N_NODES // (2 * P)))
N_PAD = NODE_TILES * P
EDGE_TILES = 8
ITEM = EDGE_TILES * P
ITEMS = -(-N_EDGES // ITEM)
assert ITEMS % 2 == 0 and NODE_TILES % 2 == 0
E_PAD = (ITEMS + 1) * ITEM
V3 = 3 * V_CH
FC = 64
W_COLS = 2 * S_CH + 3 * V_CH
AGG = (S_CH + V_CH) + 3 * (S_CH + V_CH + 2 * V_CH)
GROUP = S_CH + 3 * V_CH
T1_COLS = 2 * D + V_CH + V3
MSG = D + V_CH
TABLES = 4
TRASH = N_PAD
T_PAD = N_PAD + P
EPS = 1e-5


def weights_into(w):
    r = lambda n: float(n) ** -0.5
    f96 = r(S_CH + V_CH)
    return [
        (w["lin1s"][:, :], r(S_CH)), (w["lin1v"][:, :], r(V_CH)), (w["fc2"][:, :], r(FC)),
        (w["scs"][:, :], r(S_CH)), (w["scv"][:, :], r(V_CH)),
        (w["l2s"][0:S_CH, :], r(96) / 4), (w["l2s"][S_CH:96, :], r(96) * r(3) / 4),
        (w["l2v"][0:96, :], r(128) / 4), (w["l2v"][96:128, :], r(128) * r(2) / 4),
        (w["r1s"][:, 0:64], f96), (w["r1s"][:, 64:128], r(S_CH)), (w["r1s"][:, 128:160], f96),
        (w["r1v"][:, 0:V3], f96), (w["r1v"][:, V3:2 * V3], r(V_CH)),
        (w["wa"][S_CH:96, :], f96 * r(3)),
        (w["u000"][:, :], r(5120)), (w["u110"][:, :], r(5120) * r(3)),
        (w["u011"][:, :], r(4096)), (w["u101"][:, :], r(4096)),
        (w["lu0"][:, :], r(S_CH)), (w["lu1"][:, :], r(V_CH)),
    ]


def build(nc, x_in, a_in, dst_in, dstrow_in, src_in, srcrow_in, ea_in, es_in, ident_in, iota_in,
          cols_in, win_in, lin1_ws, lin1_wv, fc_w1, fc_w2, sc_ws, sc_wv, lin2_ws, lin2_wv,
          wm000, wm011, wm101, wm110, lm0, lm1, wu000, wu011, wu101, wu110, lu0, lu1, out):
    f32, i32 = mybir.dt.float32, mybir.dt.int32
    ALU, ACT, AX = mybir.AluOpType, mybir.ActivationFunctionType, mybir.AxisListType
    ds = bass.ds
    UN = NODE_TILES // 2

    ctx = ExitStack()
    with ctx:
        def sb(name, shape, dt=f32):
            return ctx.enter_context(nc.sbuf_tensor(name, shape, dt))

        def sem(name):
            return ctx.enter_context(nc.semaphore(name))

        def two(name):
            return [sem(f"{name}{s}") for s in range(2)]

        h0_tab = nc.dram_tensor("h0_tab", [N_PAD, D], f32, kind="Internal").ap()
        agg0 = nc.dram_tensor("agg0", [N_PAD, AGG], f32, kind="Internal").ap()
        t1_tab = nc.dram_tensor("t1_tab", [N_PAD, T1_COLS], f32, kind="Internal").ap()
        agg1 = [nc.dram_tensor(f"agg1_{k}", [T_PAD, MSG], f32, kind="Internal").ap() for k in range(TABLES)]

        ident = sb("ident", [P, P])
        iota = sb("iota", [P, P])
        cols = sb("cols", [P, 4])
        win = sb("win", [P, NODE_TILES + 1])
        ones = sb("ones", [P, P])
        zero = sb("zero", [P, (T_PAD // P) * MSG // 2])
        w = {"lin1s": sb("w_lin1s", [64, 64]), "lin1v": sb("w_lin1v", [96, 96]),
             "fc1": sb("w_fc1", [64, 64]), "fc2": sb("w_fc2", [64, W_COLS]),
             "scs": sb("w_scs", [64, 96]), "scv": sb("w_scv", [96, 96]),
             "l2s": sb("w_l2s", [96, 96]), "l2v": sb("w_l2v", [128, 32]),
             "r1s": sb("w_r1s", [64, 160]), "r1v": sb("w_r1v", [96, 2 * V3]),
             "wa": sb("w_wa", [96, 64]), "u000": sb("w_u000", [P, 32 * 64]),
             "u110": sb("w_u110", [P, 8 * 64]), "u011": sb("w_u011", [64, 1024]),
             "u101": sb("w_u101", [64, 1024]), "lu0": sb("w_lu0", [64, 64]), "lu1": sb("w_lu1", [96, 96])}

        X = sb("X", [P, NODE_TILES * D])
        X1 = sb("X1", [P, (NODE_TILES + 1) * D])
        A1 = sb("A1", [P, (NODE_TILES + 1) * D])
        attr = sb("attr", [P, NODE_TILES])
        dsti = sb("dsti", [P, (ITEMS + 1) * EDGE_TILES], i32)
        dstf = sb("dstf", [P, (ITEMS + 1) * EDGE_TILES])
        basef = sb("basef", [P, ITEMS + 1])
        rel_all = sb("rel_all", [P, (ITEMS + 1) * EDGE_TILES])
        out_of = sb("out_of", [P, (ITEMS + 1) * EDGE_TILES])
        far = sb("far", [P, 1])
        flag = sb("flag", [1, 1], i32)
        bn6 = sb("bn6", [P, 2, 6])
        bn2 = sb("bn2", [P, 2, 2])
        moments = sb("moments", [P, NODE_TILES, 2])
        vareps = sb("vareps", [P, NODE_TILES])
        std = sb("std", [P, NODE_TILES])
        rstd = [sb(f"rstd{l}", [P, NODE_TILES + 1]) for l in range(2)]
        shift = [sb(f"shift{l}", [P, NODE_TILES + 1]) for l in range(2)]

        hs = sb("hs", [P, 2, D])
        hts = sb("hts", [64, 2, P])
        htv = sb("htv", [96, 2, P])
        h0s = sb("h0s", [P, 2, D])
        aggt = sb("aggt", [P, 2, AGG])
        crs = sb("crs", [P, 2, 3, V_CH])
        midts = sb("midts", [96, 2, P])
        midtv = sb("midtv", [P, 2, 3 * P])
        sig = sb("sig", [P, 2, 96])
        gat = sb("gat", [P, 2, D])
        t1s = sb("t1s", [P, 2, T1_COLS])
        tabs = sb("tabs", [P, 2, TABLES, MSG])
        half = sb("half", [P, 2, 2, MSG])
        mt = sb("mt", [P, 2, 96])
        mtt = sb("mtt", [96, 2, P])
        a_s = sb("a_s", [P, 2, D])
        ats = sb("ats", [64, 2, P])
        sum2 = sb("sum2", [P, V3])
        ys = sb("ys", [P, 2, D])
        yt = sb("yt", [P, D])

        arena = sb("arena", [P, 14336])

        def carve(*shapes):
            at, views = 0, []
            for shape in shapes:
                n = 1
                for d in shape[1:]:
                    n *= d
                v = arena[0:shape[0], at:at + n]
                names = "abcd"[:len(shape) - 1]
                views.append(v.rearrange(f"p ({' '.join(names)}) -> p {' '.join(names)}",
                                         **dict(zip(names, shape[1:]))) if len(names) > 1 else v)
                at += n
            assert at <= 14336
            return views

        srci = sb("srci", [P, 2, EDGE_TILES], i32)
        ea = sb("ea", [P, 2, EDGE_TILES, 4])
        est, hid, gath, sel, xw, aggs = carve(
            [64, 2, ITEM], [64, 2, ITEM], [P, 2, EDGE_TILES, D], [P, 2, 4, P], [P, 2, 2 * S_CH + 3 * V3],
            [P, 2, AGG])
        rel = sb("rel", [P, 2, EDGE_TILES])
        dstrow, srcrow, t1w, pick, same, msg, tz, tx, outm = carve(
            [P, 2, ITEM], [P, 2, ITEM], [P, 2, T1_COLS], [P, 2, ITEM], [P, 2, ITEM], [P, 2, 2, MSG],
            [P, 2, 2, 3 * V_CH], [P, 2, 2, 3 * V_CH], [P, 2, EDGE_TILES, MSG])
        dstrow, srcrow = dstrow.bitcast(i32), srcrow.bitcast(i32)
        tz = tz.rearrange("p q i (k c) -> p q i k c", k=3)
        tx = tx.rearrange("p q i (k c) -> p q i k c", k=3)
        prod, prod2, gz, zout, zt = carve(
            [P, 3, 1024], [P, 3, 1024], [P, 3, 1024], [P, 2, 1024], [P, 2, 512])
        srcf = sb("srcf", [P, 2, EDGE_TILES])
        nodeid = sb("nodeid", [P, 2])
        again = sb("again", [P, EDGE_TILES])
        away = sb("away", [P, EDGE_TILES])
        moved = sb("moved", [P, EDGE_TILES])
        scidx = sb("scidx", [P, 2, EDGE_TILES], i32)

        PS = ctx.enter_context(nc.psum_tensor("PS", [P, 8, 512], f32))

        loaded = sem("loaded")
        loaded_bd = sem("loaded_bd")
        zeroed = sem("zeroed")
        scaled = sem("scaled")
        cleared = sem("cleared")
        setup = sem("setup")
        base_mm = sem("base_mm")
        far_mm = sem("far_mm")
        flag_ready = sem("flag_ready")
        stats = sem("stats")
        eps_ready = sem("eps_ready")
        std_ready = sem("std_ready")
        norm_ready = sem("norm_ready")
        n0_h, n0_tr, n0_cp, n0_mm, n0_out = (sem(f"n0_{k}") for k in ("h", "tr", "cp", "mm", "out"))
        n0_stored = two("n0_stored")
        l0_loaded = two("l0_loaded")
        gathered = [[sem(f"gathered{s}_{j}") for j in range(EDGE_TILES)] for s in range(2)]
        rel_ready = sem("rel_ready")
        hid_mm, hid_ready, w_done, x_ready, scat_done, agg_evac = (
            sem(k) for k in ("hid_mm", "hid_ready", "w_done", "x_ready", "scat_done", "agg_evac"))
        agg_added = two("agg_added")
        l0_done = sem("l0_done")
        n1_loaded = two("n1_loaded")
        n1_h, n1_crs, n1_mid, n1_tr, n1_cp, n1_mm, n1_sig, n1_g, n1_x = (
            sem(f"n1_{k}") for k in ("h", "crs", "mid", "tr", "cp", "mm", "sig", "g", "x"))
        stats1, eps1_ready, std1_ready, norm1_ready = (
            sem(k) for k in ("stats1", "eps1_ready", "std1_ready", "norm1_ready"))
        n1b_h, n1b_tr, n1b_cp, n1b_mm, n1b_out = (sem(f"n1b_{k}") for k in ("h", "tr", "cp", "mm", "out"))
        n1b_stored = two("n1b_stored")
        l1_loaded = two("l1_loaded")
        prep_a, pick_ready, rank_mm, idx_step, idx_ready = (
            sem(k) for k in ("prep_a", "pick_ready", "rank_mm", "idx_step", "idx_ready"))
        gath_mm, v_ready, parts_ready, msg_ready, ded_done, out_ready = (
            sem(k) for k in ("gath_mm", "v_ready", "parts_ready", "msg_ready", "ded_done", "out_ready"))
        scattered = [two(f"scattered{k}_") for k in range(TABLES)]
        l1_done = sem("l1_done")
        n2_loaded = two("n2_loaded")
        n2a_half, n2a_sum, n2a_tr, n2a_cp, n2a_mm, n2a_out = (
            sem(f"n2a_{k}") for k in ("half", "sum", "tr", "cp", "mm", "out"))
        n2_h, n2_tr, n2_cp, n2_t, n2_p, n2_id, n2_z, n2_half, n2_ev, n2_main, n2_g, n2_r, n2_yt, n2_y = (
            sem(f"n2_{k}") for k in ("h", "tr", "cp", "t", "p", "id", "z", "half", "ev", "main",
                                     "g", "r", "yt", "y"))
        stored = two("stored")
        CREDITS = [(n0_tr, 2), (n0_cp, 2), (n0_mm, 2), (n0_out, 2),
                   (hid_mm, 4), (hid_ready, 2), (w_done, 16), (x_ready, 16), (scat_done, 2), (agg_evac, 2),
                   (n1_tr, 2), (n1_cp, 2), (n1_mm, 2), (n1_g, 2), (n1_x, 2),
                   (n1b_tr, 2), (n1b_cp, 2), (n1b_mm, 2), (n1b_out, 2),
                   (gath_mm, 8), (msg_ready, 8), (ded_done, 8), (out_ready, 2), (idx_ready, 2),
                   (n2a_tr, 2), (n2a_cp, 2), (n2a_mm, 2), (n2a_out, 2),
                   (n2_cp, 1), (n2_p, 2), (n2_id, 1), (n2_half, 10), (n2_ev, 2), (n2_main, 2), (n2_y, 2)]

        block = ctx.enter_context(nc.Block())

        def settle(eng):
            eng.nop(nofuse=True)

        def v3(ap):
            return ap.rearrange("p (c k) -> p k c", k=3)

        def by3(ap):
            return ap.rearrange("p (k c) -> p k c", k=3)

        def items(eng, body, general):
            if not general:
                with eng.Fori(0, ITEMS // 2) as u:
                    for s in range(2):
                        body(u, s, 2 * u + s, None)
            else:
                with eng.Fori(0, ITEMS) as i:
                    with eng.Fori(0, NODE_TILES // 2) as q:
                        for s in range(2):
                            body(i * (NODE_TILES // 2) + q, s, i, 2 * q + s)

        def uses(general):
            return ITEMS * NODE_TILES if general else ITEMS

        def by_input(eng, part):
            eng.wait_ge(flag_ready, 1)
            bad = eng.value_load(flag[0:1, 0:1], min_val=0, max_val=E_PAD)
            with eng.If(bad < 1):
                part(False)
            with eng.Else():
                part(True)

        @block.sync
        def _(sp):
            for sm, n in CREDITS:
                sp.sem_inc(sm, n)
            loads = [
                (X[:, :].rearrange("p (t d) -> p t d", d=D), x_in.rearrange("(t p) d -> p t d", p=P)),
                (attr[:, :], a_in), (dsti[:, :], dst_in), (ident[:, :], ident_in), (iota[:, :], iota_in),
                (cols[:, :], cols_in), (win[:, :], win_in),
                (w["lin1s"][:, :], lin1_ws), (w["fc1"][:, :], fc_w1),
                (w["fc2"][:, 0:64], fc_w2[:, 64:128]), (w["fc2"][:, 64:128], fc_w2[:, 0:64]),
                (w["fc2"][:, 128:W_COLS], fc_w2[:, 128:W_COLS]),
                (w["scs"][:, :], sc_ws), (w["l2s"][:, :], lin2_ws), (w["l2v"][:, :], lin2_wv),
                (w["r1s"][:, 0:64], wm000.rearrange("u o w -> u (o w)")), (w["r1s"][:, 64:128], lm0),
                (w["r1s"][:, 128:160], wm011.rearrange("u o w -> u (o w)")),
                (w["wa"][0:64, :], ident_in[0:64, 0:64]),
                (w["wa"][64:96, :], wm110.rearrange("u o w -> u (o w)")),
                (w["u000"][:, :].rearrange("p (b w) -> p b w", w=64),
                 wu000.rearrange("(b i) v w -> (i v) b w", i=2)),
                (w["u110"][:, :].rearrange("p (b w) -> p b w", w=64),
                 wu110.rearrange("(b i) v w -> (i v) b w", i=4)),
                (w["u011"][:, :], wu011.rearrange("u v w -> u (v w)")),
                (w["u101"][:, :].rearrange("v (u w) -> v u w", w=32), wu101.rearrange("u v w -> v u w")),
                (w["lu0"][:, :], lu0),
            ]
            assert len(loads) == N_LOADS
            for dst, src in loads:
                sp.dma_start(dst, src).then_inc(loaded, 16)
            sp.wait_ge(zeroed, 2)
            blocks = [("lin1v", 0, lin1_wv), ("scv", 0, sc_wv), ("r1v", 0, wm101.rearrange("u o w -> u (o w)")),
                      ("r1v", V3, lm1), ("lu1", 0, lu1)]
            for name, c0, src in blocks:
                for k in range(3):
                    sp.dma_start(w[name][32 * k:32 * k + 32, c0 + 32 * k:c0 + 32 * k + 32], src)\
                        .then_inc(loaded_bd, 16)
            for table, width in [(agg0, NODE_TILES * AGG // 6)] + [(a, T_PAD // P * MSG // 2) for a in agg1]:
                flat = table.rearrange("(p r) c -> p (r c)", p=P)
                for c in range(0, flat.shape[1], width):
                    sp.dma_start(flat[:, c:c + width], zero[:, 0:width]).then_inc(cleared, 16)

            with sp.Fori(0, UN) as u:
                for s in range(2):
                    t = 2 * u + s
                    sp.wait_ge(n0_out, t + 3)
                    sp.dma_start(h0_tab[ds(t * P, P), :], h0s[:, s, :]).then_inc(n0_stored[s], 16)

            def load0(u, s, item, window):
                n = 2 * u + s
                sp.wait_ge(x_ready, 8 * n + 8)
                sp.wait_ge(hid_mm, 2 * n + 2)
                sp.dma_start(srci[:, s, :], src_in[ds(item, 1), :, :].rearrange("i p j -> (i p) j"))\
                    .then_inc(l0_loaded[s], 16)
                sp.dma_start(ea[:, s, :, :].rearrange("p j c -> p (j c)"),
                             ea_in[ds(item, 1), :, :].rearrange("i p j -> (i p) j")).then_inc(l0_loaded[s], 16)
                sp.dma_start(est[:, s, :], es_in[ds(item, 1), :, :].rearrange("i p j -> (i p) j"))\
                    .then_inc(l0_loaded[s], 16)

            def layer0(general):
                items(sp, load0, general)
                load0(uses(general) // 2, 0, ITEMS, None)
            by_input(sp, layer0)

            sp.wait_ge(l0_done, 1)
            with sp.Fori(0, UN) as u:
                for s in range(2):
                    t = 2 * u + s
                    sp.wait_ge(n1_tr, t + 1)
                    sp.dma_start(aggt[:, s, :], agg0[ds(t * P, P), :]).then_inc(n1_loaded[s], 16)
            with sp.Fori(0, UN) as u:
                for s in range(2):
                    t = 2 * u + s
                    sp.wait_ge(n1b_out, t + 3)
                    sp.dma_start(t1_tab[ds(t * P, P), :], t1s[:, s, :]).then_inc(n1b_stored[s], 16)
            for s in range(2):
                sp.wait_ge(n1b_stored[s], 16 * UN)

            def load1(u, s, item, window):
                n = 2 * u + s
                sp.wait_ge(gath_mm, 4 * n + 4)
                sp.wait_ge(msg_ready, 4 * n + 4)
                if window is None:
                    base = sp.value_load(dsti[0:1, ds(item * EDGE_TILES, 1)], min_val=0, max_val=N_NODES)
                else:
                    base = window * P
                sp.dma_start(t1w[:, s, :], t1_tab[ds(base, P), :]).then_inc(l1_loaded[s], 16)
                sp.dma_start(srci[:, s, :], src_in[ds(item, 1), :, :].rearrange("i p j -> (i p) j"))\
                    .then_inc(l1_loaded[s], 16)
                sp.dma_start(ea[:, s, :, :].rearrange("p j c -> p (j c)"),
                             ea_in[ds(item, 1), :, :].rearrange("i p j -> (i p) j")).then_inc(l1_loaded[s], 16)
                sp.dma_start(dstrow[:, s, :], dstrow_in[ds(item, 1), :].to_broadcast([P, ITEM]))\
                    .then_inc(l1_loaded[s], 16)
                sp.dma_start(srcrow[:, s, :], srcrow_in[ds(item, 1), :].to_broadcast([P, ITEM]))\
                    .then_inc(l1_loaded[s], 16)

            def layer1(general):
                items(sp, load1, general)
                load1(uses(general) // 2, 0, ITEMS, 0 if general else None)
            by_input(sp, layer1)

            sp.wait_ge(l1_done, 1)
            with sp.Fori(0, UN) as u:
                for s in range(2):
                    t = 2 * u + s
                    sp.wait_ge(n2a_tr, t + 1)
                    for k in range(TABLES):
                        sp.dma_start(tabs[:, s, k, :], agg1[k][ds(t * P, P), :]).then_inc(n2_loaded[s], 16)
            with sp.Fori(0, UN) as u:
                for s in range(2):
                    t = 2 * u + s
                    sp.wait_ge(n2_y, t + 3)
                    sp.dma_start(out[ds(t * P, P), :], ys[:, s, :]).then_inc(stored[s], 16)
            for s in range(2):
                sp.wait_ge(stored[s], 16 * UN)

        @block.gpsimd
        def _(pool):
            pool.memset(zero[:, :], 0.0).then_inc(zeroed, 1)

            for s in range(2):
                pool.wait_ge(n0_stored[s], 16 * UN)
            pool.wait_ge(cleared, 16 * N_CLEAR)

            def gather0(u, s):
                n = 2 * u + s
                pool.wait_ge(l0_loaded[s], 48 * (u + 1))
                for j in range(EDGE_TILES):
                    pool.wait_ge(x_ready, 8 * n + j + 1)
                    settle(pool)
                    pool.indirect_dma_start(
                        out=gath[:, s, j, :], out_offset=None, in_=h0_tab,
                        in_offset=bass.IndirectOffsetOnAxis(ap=srci[:, s, j:j + 1], axis=0),
                    ).then_inc(gathered[s][j], 16)

            def item0(u, s, item, window):
                n = 2 * u + s
                gather0(u + s, 1 - s)
                if window is None:
                    base = pool.value_load(dsti[0:1, ds(item * EDGE_TILES, 1)], min_val=0, max_val=N_NODES)
                else:
                    base = window * P
                pool.wait_ge(agg_evac, n + 3)
                pool.wait_ge(agg_added[1 - s], 16 * (u + s))
                pool.dma_start(agg0[ds(base, P), :], aggs[:, s, :], accum_op=ALU.add).then_inc(agg_added[s], 16)

            def layer0(general):
                gather0(0, 0)
                items(pool, item0, general)
                for s in range(2):
                    pool.wait_ge(agg_added[s], 8 * uses(general))
                for j in range(EDGE_TILES):
                    pool.wait_ge(gathered[0][j], 8 * uses(general) + 16)
                pool.sem_inc(l0_done, 1)
            by_input(pool, layer0)

            def item1(u, s, item, window):
                n = 2 * u + s
                pool.wait_ge(idx_ready, n + 3)
                for j in range(EDGE_TILES):
                    k = j % TABLES
                    if j % 2 == 0:
                        pool.wait_ge(out_ready, 4 * n + j // 2 + 3)
                    if j < TABLES:
                        pool.wait_ge(scattered[k][1 - s], 32 * (u + s))
                    else:
                        pool.wait_ge(scattered[k][s], 32 * u + 16)
                    settle(pool)
                    pool.indirect_dma_start(
                        out=agg1[k], out_offset=bass.IndirectOffsetOnAxis(ap=scidx[:, s, j:j + 1], axis=0),
                        in_=outm[:, s, j, :], in_offset=None, compute_op=ALU.add,
                    ).then_inc(scattered[k][s], 16)

            def layer1(general):
                items(pool, item1, general)
                for k in range(TABLES):
                    for s in range(2):
                        pool.wait_ge(scattered[k][s], 16 * uses(general))
                pool.sem_inc(l1_done, 1)
            by_input(pool, layer1)

            with pool.Fori(0, UN) as uu:
                for s in range(2):
                    t = 2 * uu + s
                    pool.wait_ge(n2_h, t + 1)
                    pool.wait_ge(n2_half, 10 * t + 10)
                    for k in range(3):
                        lo = S_CH + 32 * k
                        pool.tensor_tensor(
                            gz[:, k, :].rearrange("p (u v) -> p u v", v=32),
                            hs[:, s, lo:lo + 32].unsqueeze(2).to_broadcast([P, 32, 32]),
                            a_s[:, s, lo:lo + 32].unsqueeze(1).to_broadcast([P, 32, 32]), ALU.mult)\
                            .then_inc(n2_g, 1)
                    pool.wait_ge(n2_g, 5 * t + 3)
                    pool.tensor_tensor(gz[:, 1, :], gz[:, 1, :], gz[:, 2, :], ALU.add).then_inc(n2_g, 1)
                    pool.wait_ge(n2_g, 5 * t + 4)
                    pool.tensor_tensor(gz[:, 0, :], gz[:, 0, :], gz[:, 1, :], ALU.add).then_inc(n2_g, 1)

        @block.scalar
        def _(act):
            def normed(x_tiles, layer, t, s):
                act.activation(hs[:, s, 0:S_CH], x_tiles[:, ds(t * D, S_CH)], ACT.Relu,
                               scale=rstd[layer][:, ds(t, 1)], bias=shift[layer][:, ds(t, 1)])
                return act.activation(by3(hs[:, s, S_CH:D]), v3(x_tiles[:, ds(t * D + S_CH, V3)]), ACT.Relu,
                                      scale=rstd[layer][:, ds(t, 1)], bias=shift[layer][:, ds(t, 1)])

            act.wait_ge(loaded, 16 * N_LOADS)
            act.wait_ge(eps_ready, 1)
            act.activation(std[:, :], vareps[:, :], ACT.Sqrt).then_inc(std_ready, 1)
            act.wait_ge(norm_ready, 1)
            with act.Fori(0, UN) as u:
                for s in range(2):
                    t = 2 * u + s
                    act.wait_ge(n0_tr, t + 1)
                    normed(X, 0, t, s).then_inc(n0_h, 1)
                    act.wait_ge(n0_mm, t + 3)
                    act.wait_ge(n0_stored[s], 16 * u)
                    act.activation(h0s[:, s, :], PS[:, 2 + s, 0:D], ACT.Copy,
                                   scale=attr[:, ds(t, 1)]).then_inc(n0_out, 1)

            def silu(u, s):
                n = 2 * u + s
                act.wait_ge(w_done, 8 * n + 8)
                for h in range(2):
                    act.wait_ge(hid_mm, 2 * n + h + 5)
                    act.activation(hid[:, s, h * 512:(h + 1) * 512], PS[0:64, 2 + h, :], ACT.Silu,
                                   scale=float(FC) ** -0.5).then_inc(hid_ready, 1)

            def item0(u, s, item, window):
                n = 2 * u + s
                silu(u + s, 1 - s)
                act.wait_ge(scat_done, 8 * n + 10)
                act.wait_ge(agg_added[s], 16 * u)
                ba, bb = 4 + 2 * s, 5 + 2 * s
                groups = aggs[:, s, 96:AGG].rearrange("p (k g) -> p k g", k=3)
                act.activation(aggs[:, s, 0:64], PS[:, ba, 0:64], ACT.Copy)
                act.activation(aggs[:, s, 64:96], PS[:, ba, 352:384], ACT.Copy)
                act.activation(groups[:, :, 0:64], by3(PS[:, ba, 160:352]), ACT.Copy)
                act.activation(groups[:, :, 64:96], by3(PS[:, ba, 64:160]), ACT.Copy)
                act.activation(groups[:, :, 96:160], by3(PS[:, bb, 0:192]), ACT.Copy).then_inc(agg_evac, 1)

            def layer0(general):
                silu(0, 0)
                items(act, item0, general)
            by_input(act, layer0)

            act.wait_ge(l0_done, 1)
            with act.Fori(0, UN) as u:
                for s in range(2):
                    t = 2 * u + s
                    act.wait_ge(n1_tr, t + 1)
                    normed(X, 0, t, s).then_inc(n1_h, 1)
                    act.wait_ge(n1_mm, t + 3)
                    act.wait_ge(n1_x, t + 1)
                    act.activation(sig[:, s, :], PS[:, 4 + s, 0:96], ACT.Sigmoid,
                                   scale=attr[:, ds(t, 1)]).then_inc(n1_sig, 1)
            act.wait_ge(eps1_ready, 1)
            act.activation(std[:, :], vareps[:, :], ACT.Sqrt).then_inc(std1_ready, 1)
            act.wait_ge(norm1_ready, 1)
            with act.Fori(0, UN) as u:
                for s in range(2):
                    t = 2 * u + s
                    act.wait_ge(n1b_tr, t + 1)
                    act.wait_ge(n1b_out, t + 1)
                    normed(X1, 1, t, s).then_inc(n1b_h, 1)
                    act.wait_ge(n1b_mm, t + 3)
                    act.wait_ge(n1b_stored[s], 16 * u)
                    uv = t1s[:, s, 0:2 * D].rearrange("p (g d) -> p g d", g=2)
                    act.activation(uv[:, :, 0:V3], PS[:, 2 + s, 160:352].rearrange("p (g d) -> p g d", g=2), ACT.Copy)
                    act.activation(uv[:, :, V3:D], PS[:, 2 + s, 0:128].rearrange("p (g d) -> p g d", g=2), ACT.Copy)
                    act.activation(t1s[:, s, 2 * D:2 * D + 32], PS[:, 2 + s, 128:160], ACT.Copy)
                    act.wait_ge(n1b_h, t + 1)
                    act.activation(t1s[:, s, 2 * D + 32:T1_COLS], hs[:, s, S_CH:D], ACT.Copy).then_inc(n1b_out, 1)

            def vcopy(u, s, m):
                q = m % 2
                pair = 8 * u + 4 * s + m
                act.wait_ge(gath_mm, pair + 9)
                act.wait_ge(ded_done, pair + 7)
                act.activation(msg[:, q, :, 0:D], PS[:, 2 * q:2 * q + 2, D:2 * D], ACT.Copy).then_inc(v_ready, 1)

            def item1(u, s, item, window):
                for m in range(4):
                    pair = 8 * u + 4 * s + m
                    if m < 3:
                        vcopy(u, s, m + 1)
                    else:
                        vcopy(u + s, 1 - s, 0)
                    act.wait_ge(ded_done, pair + 9)
                    if m == 0:
                        for k in range(TABLES):
                            act.wait_ge(scattered[k][s], 32 * u)
                    act.activation(outm[:, s, 2 * m:2 * m + 2, :],
                                   PS[:, 4 + m % 2, 0:2 * MSG].rearrange("p (i d) -> p i d", i=2),
                                   ACT.Copy).then_inc(out_ready, 1)

            def layer1(general):
                vcopy(0, 0, 0)
                items(act, item1, general)
            by_input(act, layer1)

            act.wait_ge(l1_done, 1)
            with act.Fori(0, UN) as u:
                for s in range(2):
                    t = 2 * u + s
                    act.wait_ge(n2a_mm, t + 3)
                    act.activation(A1[:, ds(t * D, S_CH)], PS[:, 2 + s, 0:64], ACT.Copy).then_inc(n2a_out, 1)

            def head(t, s):
                act.wait_ge(n2_y, t + 1)
                act.activation(a_s[:, s, :], A1[:, ds(t * D, D)], ACT.Copy)
                normed(X1, 1, t, s).then_inc(n2_h, 1)

            act.wait_ge(n2a_out, NODE_TILES + 2)
            head(0, 0)
            with act.Fori(0, UN) as u:
                for s in range(2):
                    t = 2 * u + s
                    head(t + 1, 1 - s)
                    for e in range(10):
                        act.wait_ge(n2_half, 10 * t + e + 11)
                        act.wait_ge(n2_main, 10 * t + e + 1)
                        act.activation(zt[:, e % 2, :], PS[:, 5 + e % 2, :], ACT.Copy).then_inc(n2_ev, 1)

        @block.vector
        def _(dve):
            steps = [0]

            def step(ins):
                steps[0] += 1
                ins.then_inc(setup, 1)
                dve.wait_ge(setup, steps[0])

            def tile_stats(x_tiles, t, s, counted):
                settle(dve)
                dve.bn_stats(bn6[:, s, :], x_tiles[:, ds(t * D, D)]).then_inc(counted, 1)
                dve.wait_ge(counted, 3 * t + 1)
                settle(dve)
                dve.bn_aggr(bn2[:, s, :], bn6[:, s, :]).then_inc(counted, 1)
                dve.wait_ge(counted, 3 * t + 2)
                dve.tensor_copy(moments[:, ds(t, 1), :].rearrange("p o m -> p (o m)"), bn2[:, s, :])\
                    .then_inc(counted, 1)

            def layernorm(x_tiles, layer, counted, eps_sem, std_sem, norm_sem, first):
                if first:
                    with dve.Fori(0, UN) as u:
                        for s in range(2):
                            t = 2 * u + s
                            tile_stats(x_tiles, t, s, counted)
                dve.wait_ge(counted, 3 * NODE_TILES)
                mean = moments[:, :, 0:1].rearrange("p t o -> p (t o)")
                var = moments[:, :, 1:2].rearrange("p t o -> p (t o)")
                dve.tensor_scalar(vareps[:, :], var, EPS, None, ALU.add).then_inc(eps_sem, 1)
                dve.wait_ge(std_sem, 1)
                step(dve.reciprocal(rstd[layer][:, 0:NODE_TILES], std[:, :]))
                dve.scalar_tensor_tensor(out=shift[layer][:, 0:NODE_TILES], in0=mean, scalar=-1.0,
                                         in1=rstd[layer][:, 0:NODE_TILES], op0=ALU.mult, op1=ALU.mult)\
                    .then_inc(norm_sem, 1)

            for name in ("lin1v", "scv", "r1v"):
                dve.memset(w[name][:, :], 0.0)
            dve.memset(w["lu1"][:, :], 0.0).then_inc(zeroed, 1)
            dve.memset(X1[:, NODE_TILES * D:], 0.0)
            dve.memset(A1[:, NODE_TILES * D:], 0.0)
            for l in range(2):
                dve.memset(rstd[l][:, NODE_TILES:], 0.0)
                dve.memset(shift[l][:, NODE_TILES:], 0.0)
            step(dve.memset(ones[:, :], 1.0))
            dve.wait_ge(loaded, 16 * N_LOADS)
            dve.wait_ge(loaded_bd, 16 * 15)
            for ap, factor in weights_into(w):
                last = dve.tensor_scalar(ap, ap, factor, None, ALU.mult)
            last.then_inc(scaled, 1)
            step(dve.tensor_copy(dstf[:, :], dsti[:, :]))
            dve.sem_inc(base_mm, 1)
            dve.wait_ge(base_mm, 2)
            step(dve.tensor_copy(basef[:, :], PS[:, 0, 0:ITEMS + 1]))
            step(dve.tensor_tensor(rel_all[:, :].rearrange("p (i j) -> p i j", j=EDGE_TILES),
                                   dstf[:, :].rearrange("p (i j) -> p i j", j=EDGE_TILES),
                                   basef[:, :].unsqueeze(2).to_broadcast([P, ITEMS + 1, EDGE_TILES]), ALU.subtract))
            step(dve.tensor_scalar(out_of[:, :], rel_all[:, :], 0.0, None, ALU.is_lt))
            step(dve.scalar_tensor_tensor(out=out_of[:, :], in0=rel_all[:, :], scalar=float(P - 1),
                                          in1=out_of[:, :], op0=ALU.is_gt, op1=ALU.add))
            step(dve.tensor_reduce(far[:, :], out_of[:, :], AX.X, ALU.add))
            dve.sem_inc(far_mm, 1)
            dve.wait_ge(far_mm, 2)
            dve.tensor_copy(flag[0:1, 0:1], PS[0:1, 1, 0:1]).then_inc(flag_ready, 1)
            layernorm(X, 0, stats, eps_ready, std_ready, norm_ready, True)
            with dve.Fori(0, UN) as u:
                for s in range(2):
                    t = 2 * u + s
                    dve.wait_ge(n0_tr, t + 3)
                    dve.wait_ge(n0_mm, t + 1)
                    dve.tensor_copy(hts[:, s, :], PS[0:64, s, 0:128])
                    dve.tensor_copy(htv[:, s, :], PS[0:96, s, 128:256]).then_inc(n0_cp, 1)

            def item0(u, s, item, window):
                n = 2 * u + s
                dve.wait_ge(l0_loaded[s], 48 * (u + 1))
                base = basef[:, ds(item, 1)] if window is None else win[:, ds(window, 1)]
                dve.tensor_scalar(rel[:, s, :], dstf[:, ds(item * EDGE_TILES, EDGE_TILES)], base, None,
                                  ALU.subtract).then_inc(rel_ready, 1)
                dve.wait_ge(rel_ready, n + 1)
                for j in range(EDGE_TILES):
                    b = j % 2
                    tile = 8 * n + j
                    dve.wait_ge(scat_done, tile + 1)
                    for k in range(4):
                        dve.tensor_scalar(sel[:, b, k, :], iota[:, :], rel[:, s, j:j + 1], ea[:, s, j, k:k + 1],
                                          ALU.is_equal, ALU.mult)
                    dve.wait_ge(w_done, tile + 17)
                    dve.wait_ge(gathered[s][j], 16 * (u + 1))
                    dve.tensor_tensor(xw[:, b, 0:128].rearrange("p (i c) -> p i c", i=2),
                                      PS[:, b, 0:128].rearrange("p (i c) -> p i c", i=2),
                                      gath[:, s, j, 0:64].unsqueeze(1).to_broadcast([P, 2, 64]), ALU.mult)
                    dve.tensor_tensor(xw[:, b, 128:].rearrange("p (i k c) -> p i k c", i=3, k=3),
                                      PS[:, b, 128:224].rearrange("p (i c) -> p i c", i=3).unsqueeze(2)
                                      .to_broadcast([P, 3, 3, 32]),
                                      by3(gath[:, s, j, 64:160]).unsqueeze(1).to_broadcast([P, 3, 3, 32]),
                                      ALU.mult).then_inc(x_ready, 1)

            by_input(dve, lambda general: items(dve, item0, general))

            dve.wait_ge(l0_done, 1)
            with dve.Fori(0, UN) as u:
                for s in range(2):
                    t = 2 * u + s
                    dve.wait_ge(n1_loaded[s], 16 * (u + 1))
                    q = lambda g, i: aggt[:, s, 96 + GROUP * g + 96 + 32 * i:96 + GROUP * g + 128 + 32 * i]
                    dve.tensor_tensor(crs[:, s, 0, :], q(2, 1), q(1, 1), ALU.subtract)
                    dve.tensor_tensor(crs[:, s, 1, :], q(0, 1), q(2, 0), ALU.subtract)
                    dve.tensor_tensor(crs[:, s, 2, :], q(1, 0), q(0, 0), ALU.subtract).then_inc(n1_crs, 1)
                    dve.wait_ge(n1_crs, t + 1)
                    dve.tensor_copy(aggt[:, s, 96:AGG].rearrange("p (k g) -> p k g", k=3)[:, :, 96:128],
                                    crs[:, s, :, :]).then_inc(n1_mid, 1)
                    dve.wait_ge(n1_tr, t + 3)
                    dve.wait_ge(n1_mm, t + 1)
                    dve.tensor_copy(hts[:, s, :], PS[0:64, s, 0:128])
                    dve.tensor_copy(htv[:, s, :], PS[0:96, s, 128:256])
                    dve.tensor_copy(midts[:, s, :], PS[0:96, s, 256:384])
                    dve.tensor_copy(midtv[:, s, :], PS[:, 2 + s, 0:384]).then_inc(n1_cp, 1)
                    dve.wait_ge(n1_sig, t + 1)
                    dve.scalar_tensor_tensor(out=gat[:, s, 0:64], in0=PS[:, 4 + s, 0:64], scalar=attr[:, ds(t, 1)],
                                             in1=sig[:, s, 0:64], op0=ALU.mult, op1=ALU.mult)
                    dve.scalar_tensor_tensor(out=by3(gat[:, s, 64:160]), in0=by3(PS[:, 4 + s, 96:192]),
                                             scalar=attr[:, ds(t, 1)],
                                             in1=sig[:, s, 64:96].unsqueeze(1).to_broadcast([P, 3, 32]),
                                             op0=ALU.mult, op1=ALU.mult).then_inc(n1_g, 1)
                    dve.wait_ge(n1_g, t + 3)
                    dve.tensor_tensor(X1[:, ds(t * D, 64)], X[:, ds(t * D, 64)], gat[:, s, 0:64], ALU.add)
                    dve.tensor_tensor(v3(X1[:, ds(t * D + 64, V3)]), v3(X[:, ds(t * D + 64, V3)]),
                                      by3(gat[:, s, 64:160]), ALU.add).then_inc(n1_x, 1)
                    dve.wait_ge(n1_x, t + 3)
                    tile_stats(X1, t, s, stats1)
            layernorm(X1, 1, stats1, eps1_ready, std1_ready, norm1_ready, False)
            with dve.Fori(0, UN) as u:
                for s in range(2):
                    t = 2 * u + s
                    dve.wait_ge(n1b_tr, t + 3)
                    dve.wait_ge(n1b_mm, t + 1)
                    dve.tensor_copy(hts[:, s, :], PS[0:64, s, 0:128])
                    dve.tensor_copy(htv[:, s, :], PS[0:96, s, 128:256]).then_inc(n1b_cp, 1)

            def prepare(u, s, item, window):
                n = 2 * u + s
                base = basef[:, ds(item, 1)] if window is None else win[:, ds(window, 1)]
                dve.wait_ge(l1_loaded[s], 80 * (u + 1))
                dve.tensor_copy(srcf[:, s, :], srci[:, s, :])
                dve.tensor_tensor(nodeid[:, s:s + 1], base, cols[:, 0:1], ALU.add).then_inc(prep_a, 1)
                dve.wait_ge(prep_a, n + 1)
                dve.wait_ge(gath_mm, 4 * n + 4)
                dve.wait_ge(ded_done, 4 * n + 4)
                dve.tensor_scalar(pick[:, s, :], dstrow[:, s, :], nodeid[:, s:s + 1], None, ALU.is_equal)
                dve.tensor_tensor(same[:, s, :].rearrange("p (j f) -> p j f", j=EDGE_TILES),
                                  srcrow[:, s, :].rearrange("p (j f) -> p j f", j=EDGE_TILES),
                                  srcf[:, s, :].unsqueeze(2).to_broadcast([P, EDGE_TILES, P]), ALU.is_equal)\
                    .then_inc(pick_ready, 1)

            def indices(u, s):
                n = 2 * u + s
                dve.wait_ge(rank_mm, n + 1)
                for k in range(TABLES):
                    dve.wait_ge(scattered[k][s], 32 * u)
                dve.tensor_scalar(again[:, :], PS[:, 6, 8 * s:8 * s + 8], cols[:, 2:3], 2.5, ALU.mult, ALU.is_gt)
                dve.tensor_scalar(away[:, :], srcf[:, s, :], -1.0, cols[:, 3:4], ALU.mult, ALU.add)\
                    .then_inc(idx_step, 1)
                dve.wait_ge(idx_step, 2 * n + 1)
                dve.tensor_tensor(moved[:, :], again[:, :], away[:, :], ALU.mult).then_inc(idx_step, 1)
                dve.wait_ge(idx_step, 2 * n + 2)
                dve.tensor_tensor(scidx[:, s, :], moved[:, :], srcf[:, s, :], ALU.add).then_inc(idx_ready, 1)

            def item1(u, s, item, window):
                for m in range(4):
                    q = m % 2
                    pair = 8 * u + 4 * s + m
                    e = ea[:, s, 2 * m:2 * m + 2, :]
                    g = PS[:, 2 * q:2 * q + 2, :]
                    ek = e[:, :, 0:3].unsqueeze(3).to_broadcast([P, 2, 3, V_CH])
                    dve.wait_ge(v_ready, pair + 1)
                    dve.tensor_tensor(tx[:, q, :, :, :], g[:, :, 352:448].rearrange("p i (k c) -> p i k c", k=3), ek,
                                      ALU.mult)
                    dve.tensor_tensor(tz[:, q, :, :, :],
                                      g[:, :, 320:352].unsqueeze(2).to_broadcast([P, 2, 3, V_CH]), ek, ALU.mult)
                    for i in range(2):
                        last = dve.scalar_tensor_tensor(out=msg[:, q, i, 0:D], in0=g[:, i, 0:D], scalar=e[:, i, 3:4],
                                                        in1=msg[:, q, i, 0:D], op0=ALU.mult, op1=ALU.add)
                    last.then_inc(parts_ready, 1)
                    dve.wait_ge(parts_ready, pair + 1)
                    dve.tensor_reduce(msg[:, q, :, D:MSG], tx[:, q, :, :, :].rearrange("p i k c -> p i c k"),
                                      AX.X, ALU.add)
                    dve.tensor_tensor(msg[:, q, :, 0:V3].rearrange("p i (k c) -> p i k c", k=3),
                                      msg[:, q, :, 0:V3].rearrange("p i (k c) -> p i k c", k=3),
                                      tz[:, q, :, :, :], ALU.add).then_inc(msg_ready, 1)
                    if m == 1:
                        prepare_next(u, s, item, window)
                    if m == 3:
                        indices(u + s, 1 - s)

            def prepare_next(u, s, item, window):
                if window is None:
                    prepare(u + s, 1 - s, item + 1, None)
                elif s == 0:
                    prepare(u, 1, item, window + 1)
                else:
                    prepare(u + 1, 0, item, window + 1)

            def layer1(general):
                prepare(0, 0, 0, 0 if general else None)
                indices(0, 0)
                items(dve, item1, general)
            by_input(dve, layer1)

            dve.wait_ge(l1_done, 1)
            with dve.Fori(0, UN) as u:
                for s in range(2):
                    t = 2 * u + s
                    dve.wait_ge(n2_loaded[s], 16 * TABLES * (u + 1))
                    dve.tensor_tensor(half[:, s, :, :], tabs[:, s, 0:2, :], tabs[:, s, 2:4, :], ALU.add)\
                        .then_inc(n2a_half, 1)
                    dve.wait_ge(n2a_half, t + 1)
                    dve.wait_ge(n2a_tr, t + 1)
                    dve.tensor_tensor(A1[:, ds(t * D + S_CH, V3)], half[:, s, 0, 0:V3], half[:, s, 1, 0:V3], ALU.add)
                    dve.tensor_tensor(mt[:, s, :], half[:, s, 0, V3:MSG], half[:, s, 1, V3:MSG], ALU.add)\
                        .then_inc(n2a_sum, 1)
                    dve.wait_ge(n2a_tr, t + 3)
                    dve.wait_ge(n2a_mm, t + 1)
                    dve.tensor_copy(mtt[:, s, :], PS[0:96, s, 0:128]).then_inc(n2a_cp, 1)

            def copies(t, s):
                dve.wait_ge(n2_tr, t + 1)
                dve.tensor_copy(hts[:, s, :], PS[0:64, 0, 0:128])
                dve.tensor_copy(htv[:, s, :], PS[0:96, 0, 128:256])
                dve.tensor_copy(ats[:, s, :], PS[0:64, 0, 256:384]).then_inc(n2_cp, 1)

            def times(out_ap, banks, by):
                return dve.tensor_tensor(
                    out_ap.rearrange("p k (i w) -> p k i w", w=32),
                    banks.rearrange("p b (i w) -> p (b i) w", w=32).unsqueeze(1).to_broadcast([P, 3, 32, 32]),
                    by3(by).unsqueeze(3).to_broadcast([P, 3, 32, 32]), ALU.mult)

            copies(0, 0)
            with dve.Fori(0, UN) as u:
                for s in range(2):
                    t = 2 * u + s
                    for c in range(4):
                        dve.wait_ge(n2_half, 10 * t + 2 * c + (8 if c >= 2 else 6))
                        dve.wait_ge(n2_h, t + 1)
                        dve.tensor_tensor(zout[:, c % 2, :].rearrange("p (u v) -> p u v", v=64),
                                          hs[:, s, 16 * c:16 * c + 16].unsqueeze(2).to_broadcast([P, 16, 64]),
                                          a_s[:, s, 0:64].unsqueeze(1).to_broadcast([P, 16, 64]), ALU.mult)\
                            .then_inc(n2_z, 1)
                    dve.wait_ge(n2_t, 2 * t + 1)
                    dve.wait_ge(n2_id, t + 1)
                    times(prod[:, :, :], PS[:, 1:3, :], a_s[:, s, 64:160]).then_inc(n2_p, 1)
                    dve.wait_ge(n2_t, 2 * t + 2)
                    times(prod2[:, :, :], PS[:, 3:5, :], hs[:, s, 64:160]).then_inc(n2_p, 1)
                    dve.wait_ge(n2_p, 2 * t + 4)
                    dve.tensor_reduce(by3(sum2[:, :]), prod2[:, :, :].rearrange("p k (i w) -> p k w i", w=32),
                                      AX.X, ALU.add).then_inc(n2_r, 1)
                    copies(t + 1, 1 - s)
                    dve.wait_ge(n2_r, t + 1)
                    dve.wait_ge(n2_main, 10 * t + 12)
                    dve.tensor_tensor(yt[:, :], PS[:, 7, 0:D], hs[:, s, :], ALU.add).then_inc(n2_yt, 1)
                    dve.wait_ge(n2_yt, 3 * t + 1)
                    dve.tensor_tensor(yt[:, 64:D], yt[:, 64:D], sum2[:, :], ALU.add).then_inc(n2_yt, 1)
                    dve.wait_ge(n2_yt, 3 * t + 2)
                    dve.wait_ge(stored[s], 16 * u)
                    dve.tensor_tensor(ys[:, s, 0:64], yt[:, 0:64], X1[:, ds(t * D, 64)], ALU.add).then_inc(n2_yt, 1)
                    dve.tensor_tensor(v3(ys[:, s, 64:160]), by3(yt[:, 64:160]), v3(X1[:, ds(t * D + 64, V3)]),
                                      ALU.add).then_inc(n2_y, 1)

        @block.tensor
        def _(pe):
            def mm(o, l, r, start=True, stop=True):
                return pe.matmul(o, l, r, start=start, stop=stop, skip_group_check=True)

            def turn(o, src):
                return pe.transpose(o, src, ident[:, :])

            pe.wait_ge(setup, 1)
            pe.wait_ge(loaded, 16 * N_LOADS)
            pe.wait_ge(base_mm, 1)
            mm(PS[:, 0, 0:ITEMS + 1], ones[0:1, :],
               dstf[0:1, :].rearrange("p (i j) -> p i j", j=EDGE_TILES)[:, :, 0]).then_inc(base_mm, 1)
            pe.wait_ge(far_mm, 1)
            mm(PS[0:1, 1, 0:1], far[:, :], ones[:, 0:1]).then_inc(far_mm, 1)
            pe.wait_ge(scaled, 1)
            pe.wait_ge(flag_ready, 1)
            with pe.Fori(0, UN) as u:
                for s in range(2):
                    t = 2 * u + s
                    pe.wait_ge(n0_h, t + 1)
                    pe.wait_ge(n0_cp, t + 1)
                    turn(PS[0:96, s, 128:256], hs[:, s, 64:160])
                    turn(PS[0:64, s, 0:128], hs[:, s, 0:64]).then_inc(n0_tr, 1)
                    pe.wait_ge(n0_cp, t + 3)
                    pe.wait_ge(n0_out, t + 1)
                    mm(PS[:, 2 + s, 0:64], hts[:, s, :], w["lin1s"][:, :])
                    mm(PS[:, 2 + s, 64:160], htv[:, s, :], w["lin1v"][:, :]).then_inc(n0_mm, 1)

            def hidden(u, s):
                n = 2 * u + s
                pe.wait_ge(l0_loaded[s], 48 * (u + 1))
                for h in range(2):
                    pe.wait_ge(hid_ready, 2 * n + h + 1)
                    settle(pe)
                    mm(PS[0:64, 2 + h, :], w["fc1"][:, :], est[:, s, h * 512:(h + 1) * 512]).then_inc(hid_mm, 1)

            def radial(u, s, j):
                n = 2 * u + s
                pe.wait_ge(x_ready, 8 * n + j + 15)
                if j % 4 == 0:
                    pe.wait_ge(hid_ready, 2 * n + j // 4 + 3)
                mm(PS[:, j % 2, 0:W_COLS], hid[:, s, j * P:(j + 1) * P], w["fc2"][:, :]).then_inc(w_done, 1)

            def item0(u, s, item, window):
                n = 2 * u + s
                ba, bb = 4 + 2 * s, 5 + 2 * s
                for j in range(EDGE_TILES):
                    b = j % 2
                    first, last = j == 0, j == EDGE_TILES - 1
                    if first:
                        pe.wait_ge(agg_evac, n + 1)
                    pe.wait_ge(x_ready, 8 * n + j + 17)
                    mm(PS[:, ba, 0:160], sel[:, b, 0, :], xw[:, b, 64:224], first, last)
                    for k in range(3):
                        o = sel[:, b, 1 + k, :]
                        mm(PS[:, ba, 160 + 64 * k:224 + 64 * k], o, xw[:, b, 0:64], False, last)
                        mm(PS[:, ba, 352:384], o, xw[:, b, 224 + 32 * k:256 + 32 * k], False, last)
                        f = xw[:, b, 320:416].rearrange("p (j c) -> p j c", j=3)
                        f = (f[:, 1:3, :], f[:, 0:3:2, :], f[:, 0:2, :])[k]
                        done = mm(PS[:, bb, 64 * k:64 * k + 64].rearrange("p (j c) -> p j c", j=2), o, f,
                                  first and k == 0, last)
                    done.then_inc(scat_done, 1)
                    if j < 6:
                        radial(u, s, j + 2)
                    else:
                        radial(u + s, 1 - s, j - 6)
                    if j == 3:
                        hidden(u + s, 1 - s)

            def layer0(general):
                hidden(0, 0)
                radial(0, 0, 0)
                radial(0, 0, 1)
                items(pe, item0, general)
            by_input(pe, layer0)

            pe.wait_ge(l0_done, 1)
            with pe.Fori(0, UN) as u:
                for s in range(2):
                    t = 2 * u + s
                    pe.wait_ge(n1_h, t + 1)
                    pe.wait_ge(n1_mid, t + 1)
                    pe.wait_ge(n1_cp, t + 1)
                    turn(PS[0:96, s, 128:256], hs[:, s, 64:160])
                    turn(PS[0:64, s, 0:128], hs[:, s, 0:64])
                    turn(PS[0:96, s, 256:384], aggt[:, s, 0:96])
                    for k in range(3):
                        last = turn(PS[:, 2 + s, P * k:P * k + P], aggt[:, s, 96 + GROUP * k:96 + GROUP * k + P])
                    last.then_inc(n1_tr, 1)
                    pe.wait_ge(n1_cp, t + 3)
                    pe.wait_ge(n1_g, t + 1)
                    o = PS[:, 4 + s, :]
                    mm(o[:, 0:96], hts[:, s, :], w["scs"][:, :], True, False)
                    mm(o[:, 0:96], midts[:, s, :], w["l2s"][:, :], False, True)
                    mm(o[:, 96:192], htv[:, s, :], w["scv"][:, :], False, False)
                    for k in range(3):
                        last = mm(o[:, 96 + 32 * k:128 + 32 * k], midtv[:, s, P * k:P * k + P], w["l2v"][:, :],
                                  False, True)
                    last.then_inc(n1_mm, 1)
            with pe.Fori(0, UN) as u:
                for s in range(2):
                    t = 2 * u + s
                    pe.wait_ge(n1b_h, t + 1)
                    pe.wait_ge(n1b_cp, t + 1)
                    turn(PS[0:96, s, 128:256], hs[:, s, 64:160])
                    turn(PS[0:64, s, 0:128], hs[:, s, 0:64]).then_inc(n1b_tr, 1)
                    pe.wait_ge(n1b_cp, t + 3)
                    pe.wait_ge(n1b_out, t + 1)
                    mm(PS[:, 2 + s, 0:160], hts[:, s, :], w["r1s"][:, :])
                    mm(PS[:, 2 + s, 160:352], htv[:, s, :], w["r1v"][:, :]).then_inc(n1b_mm, 1)

            def pickup(u, s, m):
                pair = 8 * u + 4 * s + m
                q = m % 2
                if m == 0:
                    pe.wait_ge(l1_loaded[s], 80 * (u + 1))
                    pe.wait_ge(pick_ready, 2 * u + s + 1)
                pe.wait_ge(msg_ready, pair + 7)
                for i in range(2):
                    j = 2 * m + i
                    last = mm(PS[:, 2 * q + i, 0:T1_COLS], pick[:, s, j * P:(j + 1) * P], t1w[:, s, :])
                last.then_inc(gath_mm, 1)

            def rank(u, s):
                n = 2 * u + s
                pe.wait_ge(pick_ready, n + 1)
                pe.wait_ge(idx_ready, n + 1)
                for j in range(EDGE_TILES):
                    last = mm(PS[:, 6, 8 * s + j:8 * s + j + 1], same[:, s, j * P:(j + 1) * P], cols[:, 1:2])
                last.then_inc(rank_mm, 1)

            def item1(u, s, item, window):
                for m in range(4):
                    pair = 8 * u + 4 * s + m
                    q = m % 2
                    if m < 3:
                        pickup(u, s, m + 1)
                    else:
                        pickup(u + s, 1 - s, 0)
                    pe.wait_ge(msg_ready, pair + 9)
                    pe.wait_ge(out_ready, pair + 1)
                    for i in range(2):
                        j = 2 * m + i
                        last = mm(PS[:, 4 + q, MSG * i:MSG * (i + 1)], same[:, s, j * P:(j + 1) * P], msg[:, q, i, :])
                    last.then_inc(ded_done, 1)
                    if m == 2:
                        rank(u + s, 1 - s)

            def layer1(general):
                rank(0, 0)
                pickup(0, 0, 0)
                items(pe, item1, general)
            by_input(pe, layer1)

            pe.wait_ge(l1_done, 1)
            with pe.Fori(0, UN) as u:
                for s in range(2):
                    t = 2 * u + s
                    pe.wait_ge(n2a_sum, t + 1)
                    pe.wait_ge(n2a_cp, t + 1)
                    turn(PS[0:96, s, 0:128], mt[:, s, :]).then_inc(n2a_tr, 1)
                    pe.wait_ge(n2a_cp, t + 3)
                    pe.wait_ge(n2a_out, t + 1)
                    mm(PS[:, 2 + s, 0:64], mtt[:, s, :], w["wa"][:, :]).then_inc(n2a_mm, 1)

            def head(t, s):
                pe.wait_ge(n2_h, t + 1)
                pe.wait_ge(n2_cp, t + 1)
                turn(PS[0:96, 0, 128:256], hs[:, s, 64:160])
                turn(PS[0:64, 0, 0:128], hs[:, s, 0:64])
                turn(PS[0:64, 0, 256:384], a_s[:, s, 0:64]).then_inc(n2_tr, 1)

            def tables(t, s):
                pe.wait_ge(n2_cp, t + 2)
                for i, (l, r) in enumerate(((hts, "u011"), (ats, "u101"))):
                    pe.wait_ge(n2_p, 2 * t + i + 1)
                    for h in range(2):
                        last = mm(PS[:, 1 + 2 * i + h, :], l[:, s, :], w[r][:, 512 * h:512 * (h + 1)])
                    last.then_inc(n2_t, 1)

            def turn4(t, e):
                c, h = divmod(e, 2)
                if h == 0 and c < 4:
                    pe.wait_ge(n2_z, 4 * t + c + 1)
                if h == 0 and c == 4:
                    pe.wait_ge(n2_g, 5 * t + 5)
                pe.wait_ge(n2_ev, 10 * t + e + 1)
                z = zout[:, c % 2, :] if c < 4 else gz[:, 0, :]
                for i in range(4):
                    last = turn(PS[:, 5 + h, P * i:P * i + P], z[:, 512 * h + P * i:512 * h + P * i + P])
                last.then_inc(n2_half, 1)

            def main4(t, e):
                pe.wait_ge(n2_ev, 10 * t + e + 3)
                wt, b0 = ("u000", 4 * e) if e < 8 else ("u110", 4 * (e - 8))
                for i in range(4):
                    last = mm(PS[:, 7, 0:64], zt[:, e % 2, P * i:P * i + P],
                              w[wt][:, 64 * (b0 + i):64 * (b0 + i + 1)], False, e == 9 and i == 3)
                last.then_inc(n2_main, 1)

            head(0, 0)
            tables(0, 0)
            with pe.Fori(0, UN) as u:
                for s in range(2):
                    t = 2 * u + s
                    pe.wait_ge(n2_y, t + 2)
                    mm(PS[:, 7, 0:64], hts[:, s, :], w["lu0"][:, :], True, False)
                    mm(PS[:, 7, 64:160], htv[:, s, :], w["lu1"][:, :], False, False)
                    turn4(t, 0)
                    for e in range(7):
                        turn4(t, e + 1)
                        main4(t, e)
                    main4(t, 7)
                    pe.wait_ge(n2_p, 2 * t + 3)
                    for i in range(32):
                        last = mm(by3(PS[:, 7, 64:160]), ident[:, :], prod[:, :, 32 * i:32 * i + 32], False, i == 31)
                    last.then_inc(n2_id, 1)
                    head(t + 1, 1 - s)
                    turn4(t, 8)
                    turn4(t, 9)
                    main4(t, 8)
                    main4(t, 9)
                    tables(t + 1, 1 - s)


N_LOADS = 25
N_CLEAR = 6 + 2 * TABLES


def kernel(**inputs):
    import numpy as np
    import concourse.bacc as bacc
    from concourse.bass_utils import run_bass_kernel_spmd

    src, dst = np.asarray(inputs["src"]), np.asarray(inputs["dst"])
    x, attr = np.asarray(inputs["x"]), np.asarray(inputs["node_vec1"])
    ea, es = np.asarray(inputs["edge_attr_4"]), np.asarray(inputs["edge_attr_64"])

    def padded(a, n, value=0):
        return np.concatenate([a, np.full((n - a.shape[0],) + a.shape[1:], value, a.dtype)])

    src, dst = padded(src, E_PAD, N_NODES), padded(dst, E_PAD, N_NODES)
    ea, es = padded(ea, E_PAD), padded(es, E_PAD)
    n = ITEMS + 1
    p = np.arange(P)
    cols = np.stack([p, 2.0 ** (64 - p), 2.0 ** (p - 64), TRASH + p], 1).astype(np.float32)
    arrays = {
        "x_in": padded(x, N_PAD),
        "a_in": padded(attr, N_PAD).reshape(NODE_TILES, P).T,
        "dst_in": dst.reshape(n * EDGE_TILES, P).T,
        "dstrow_in": dst.reshape(n, ITEM),
        "src_in": src.reshape(n, EDGE_TILES, P).transpose(0, 2, 1),
        "srcrow_in": src.reshape(n, ITEM),
        "ea_in": ea.reshape(n, EDGE_TILES, P, 4).transpose(0, 2, 1, 3).reshape(n, P, EDGE_TILES * 4),
        "es_in": es.reshape(n, ITEM, es.shape[1]).transpose(0, 2, 1),
        "ident_in": np.eye(P, dtype=np.float32),
        "iota_in": np.tile(p.astype(np.float32), (P, 1)),
        "cols_in": cols,
        "win_in": np.tile(np.append(P * np.arange(NODE_TILES), 0).astype(np.float32), (P, 1)),
    }
    for name in ("L0_gnn_lin1_ws", "L0_gnn_lin1_wv", "L0_gnn_fc_w1", "L0_gnn_fc_w2", "L0_gnn_sc_ws", "L0_gnn_sc_wv",
                 "L0_gnn_lin2_ws", "L0_gnn_lin2_wv", "L1_gnn_wm000", "L1_gnn_wm011", "L1_gnn_wm101",
                 "L1_gnn_wm110", "L1_gnn_lm0", "L1_gnn_lm1", "L1_gnn_wu000", "L1_gnn_wu011", "L1_gnn_wu101",
                 "L1_gnn_wu110", "L1_gnn_lu0", "L1_gnn_lu1"):
        arrays[name] = np.asarray(inputs[name])
    arrays = {k: np.ascontiguousarray(v) for k, v in arrays.items()}

    nc = bacc.Bacc("TRN2", target_bir_lowering=False, num_devices=1)
    args = [nc.dram_tensor(k, v.shape, mybir.dt.from_np(v.dtype), kind="ExternalInput").ap()
            for k, v in arrays.items()]
    out = nc.dram_tensor("out", (N_PAD, D), mybir.dt.float32, kind="ExternalOutput").ap()
    build(nc, *args, out)
    r = run_bass_kernel_spmd(nc, [arrays], core_ids=[0])
    return r.results[0]["out"][:N_NODES]
```

```python
import concourse.bass as bass
from concourse import mybir
from contextlib import ExitStack

P = 128
N_NODES, N_EDGES = 3125, 53125
S_CH, V_CH = 64, 32
D = S_CH + 3 * V_CH
NODE_TILES = 2 * (-(-N_NODES // (2 * P)))
N_PAD = NODE_TILES * P
EDGE_TILES = 8
ITEM = EDGE_TILES * P
ITEMS = -(-N_EDGES // ITEM)
assert ITEMS % 2 == 0 and NODE_TILES % 2 == 0
E_PAD = (ITEMS + 1) * ITEM
V3 = 3 * V_CH
FC = 64
W_COLS = 2 * S_CH + 4 * V_CH
H0 = D + 2 * V_CH
X_STEP = 2 * S_CH + 4 * 3 * V_CH
AGG = S_CH + 3 * V_CH + 3 * (S_CH + V_CH + 2 * V_CH)
G0 = S_CH + 3 * V_CH
GROUP = S_CH + 3 * V_CH
T1_COLS = 2 * D + V_CH + V3
MSG = D + V_CH
TABLES = 4
TRASH = N_PAD
T_PAD = N_PAD + P
EPS = 1e-5


def weights_into(w):
    r = lambda n: float(n) ** -0.5
    f96 = r(S_CH + V_CH)
    return [
        (w["lin1s"][:, :], r(S_CH)), (w["lin1v"][:, :], r(V_CH)), (w["fc2"][:, :], r(FC)),
        (w["scs"][:, :], r(S_CH)), (w["scv"][:, :], r(V_CH)),
        (w["l2s"][0:S_CH, :], r(96) / 4), (w["l2s"][S_CH:96, :], r(96) * r(3) / 4),
        (w["l2v"][0:96, :], r(128) / 4), (w["l2v"][96:128, :], r(128) * r(2) / 4),
        (w["r1s"][:, 0:64], f96), (w["r1s"][:, 64:128], r(S_CH)), (w["r1s"][:, 128:160], f96),
        (w["r1v"][:, 0:V3], f96), (w["r1v"][:, V3:2 * V3], r(V_CH)),
        (w["wa"][S_CH:96, :], f96 * r(3)),
        (w["u000"][:, :], r(5120)), (w["u110"][:, :], r(5120) * r(3)),
        (w["u011"][:, :], r(4096)), (w["u101"][:, :], r(4096)),
        (w["lu0"][:, :], r(S_CH)), (w["lu1"][:, :], r(V_CH)),
    ]


def build(nc, x_in, a_in, dst_in, dstrow_in, src_in, srcrow_in, ea_in, es_in, ident_in, iota_in,
          cols_in, win_in, lin1_ws, lin1_wv, fc_w1, fc_w2, sc_ws, sc_wv, lin2_ws, lin2_wv,
          wm000, wm011, wm101, wm110, lm0, lm1, wu000, wu011, wu101, wu110, lu0, lu1, out):
    f32, i32 = mybir.dt.float32, mybir.dt.int32
    ALU, ACT, AX = mybir.AluOpType, mybir.ActivationFunctionType, mybir.AxisListType
    ds = bass.ds
    UN = NODE_TILES // 2

    ctx = ExitStack()
    with ctx:
        def sb(name, shape, dt=f32):
            return ctx.enter_context(nc.sbuf_tensor(name, shape, dt))

        def sem(name):
            return ctx.enter_context(nc.semaphore(name))

        def two(name):
            return [sem(f"{name}{s}") for s in range(2)]

        h0_tab = nc.dram_tensor("h0_tab", [N_PAD, H0], f32, kind="Internal").ap()
        agg0 = nc.dram_tensor("agg0", [N_PAD, AGG], f32, kind="Internal").ap()
        t1_tab = nc.dram_tensor("t1_tab", [N_PAD, T1_COLS], f32, kind="Internal").ap()
        agg1 = [nc.dram_tensor(f"agg1_{k}", [T_PAD, MSG], f32, kind="Internal").ap() for k in range(TABLES)]

        ident = sb("ident", [P, P])
        iota = sb("iota", [P, P])
        cols = sb("cols", [P, 4])
        win = sb("win", [P, NODE_TILES + 1])
        ones = sb("ones", [P, P])
        zero = sb("zero", [P, NODE_TILES * AGG // 8])
        w = {"lin1s": sb("w_lin1s", [64, 64]), "lin1v": sb("w_lin1v", [96, 160]),
             "fc1": sb("w_fc1", [64, 64]), "fc2": sb("w_fc2", [64, W_COLS]),
             "scs": sb("w_scs", [64, 96]), "scv": sb("w_scv", [96, 96]),
             "l2s": sb("w_l2s", [96, 96]), "l2v": sb("w_l2v", [128, 32]),
             "r1s": sb("w_r1s", [64, 160]), "r1v": sb("w_r1v", [96, 2 * V3]),
             "wa": sb("w_wa", [96, 64]), "u000": sb("w_u000", [P, 32 * 64]),
             "u110": sb("w_u110", [P, 8 * 64]), "u011": sb("w_u011", [64, 1024]),
             "u101": sb("w_u101", [64, 1024]), "lu0": sb("w_lu0", [64, 64]), "lu1": sb("w_lu1", [96, 96])}

        X = sb("X", [P, NODE_TILES * D])
        X1 = sb("X1", [P, (NODE_TILES + 1) * D])
        A1 = sb("A1", [P, (NODE_TILES + 1) * D])
        attr = sb("attr", [P, NODE_TILES])
        dsti = sb("dsti", [P, (ITEMS + 1) * EDGE_TILES], i32)
        dstf = sb("dstf", [P, (ITEMS + 1) * EDGE_TILES])
        basef = sb("basef", [P, ITEMS + 1])
        rel_all = sb("rel_all", [P, (ITEMS + 1) * EDGE_TILES])
        out_of = sb("out_of", [P, (ITEMS + 1) * EDGE_TILES])
        far = sb("far", [P, 1])
        flag = sb("flag", [1, 1], i32)
        bn6 = sb("bn6", [P, 2, 6])
        bn2 = sb("bn2", [P, 2, 2])
        moments = sb("moments", [P, NODE_TILES, 2])
        vareps = sb("vareps", [P, NODE_TILES])
        std = sb("std", [P, NODE_TILES])
        rstd = [sb(f"rstd{l}", [P, NODE_TILES + 1]) for l in range(2)]
        shift = [sb(f"shift{l}", [P, NODE_TILES + 1]) for l in range(2)]

        hs = sb("hs", [P, 2, D])
        hts = sb("hts", [64, 2, P])
        htv = sb("htv", [96, 2, P])
        h0s = sb("h0s", [P, 2, H0])
        aggt = sb("aggt", [P, 2, AGG])
        crs = sb("crs", [P, 2, 4, V_CH])
        midts = sb("midts", [96, 2, P])
        midtv = sb("midtv", [P, 2, 3 * P])
        sig = sb("sig", [P, 2, 96])
        gat = sb("gat", [P, 2, D])
        t1s = sb("t1s", [P, 2, T1_COLS])
        tabs = sb("tabs", [P, 2, TABLES, MSG])
        half = sb("half", [P, 2, 2, MSG])
        mt = sb("mt", [P, 2, 96])
        mtt = sb("mtt", [96, 2, P])
        a_s = sb("a_s", [P, 2, D])
        ats = sb("ats", [64, 2, P])
        sum2 = sb("sum2", [P, V3])
        ys = sb("ys", [P, 2, D])
        yt = sb("yt", [P, D])

        arena = sb("arena", [P, 14336])

        def carve(*shapes):
            at, views = 0, []
            for shape in shapes:
                n = 1
                for d in shape[1:]:
                    n *= d
                v = arena[0:shape[0], at:at + n]
                names = "abcd"[:len(shape) - 1]
                views.append(v.rearrange(f"p ({' '.join(names)}) -> p {' '.join(names)}",
                                         **dict(zip(names, shape[1:]))) if len(names) > 1 else v)
                at += n
            assert at <= 14336
            return views

        srci = sb("srci", [P, 2, EDGE_TILES], i32)
        ea = sb("ea", [P, 2, EDGE_TILES, 4])
        est, hid, gath, sel, xw, aggs = carve(
            [64, 2, ITEM], [64, 2, ITEM], [P, 2, EDGE_TILES, H0], [P, 4, 4, P], [P, 5 * X_STEP],
            [P, 2, AGG])
        rel = sb("rel", [P, 2, EDGE_TILES])
        dstrow, srcrow, t1w, pick, same, msg, tz, tx, outm = carve(
            [P, 2, ITEM], [P, 2, ITEM], [P, 2, T1_COLS], [P, 2, ITEM], [P, 2, ITEM], [P, 2, 2, MSG + 1],
            [P, 2, 2, 3 * V_CH], [P, 2, 2, 3 * V_CH], [P, 2, EDGE_TILES, MSG + 1])
        dstrow, srcrow = dstrow.bitcast(i32), srcrow.bitcast(i32)
        tz = tz.rearrange("p q i (k c) -> p q i k c", k=3)
        tx = tx.rearrange("p q i (k c) -> p q i k c", k=3)
        prod, prod2, gz, zout, zt = carve(
            [P, 3, 1024], [P, 3, 1024], [P, 3, 1024], [P, 2, 1024], [P, 2, 512])
        srcf = sb("srcf", [P, 2, EDGE_TILES])
        nodeid = sb("nodeid", [P, 2])
        away = sb("away", [P, 2, EDGE_TILES])
        moved = sb("moved", [P, EDGE_TILES])
        scidx = sb("scidx", [P, 2, EDGE_TILES], i32)

        PS = ctx.enter_context(nc.psum_tensor("PS", [P, 8, 512], f32))

        loaded = sem("loaded")
        loaded_bd = sem("loaded_bd")
        zeroed = sem("zeroed")
        scaled = sem("scaled")
        cleared = sem("cleared")
        setup = sem("setup")
        base_mm = sem("base_mm")
        far_mm = sem("far_mm")
        flag_ready = sem("flag_ready")
        stats = sem("stats")
        eps_ready = sem("eps_ready")
        std_ready = sem("std_ready")
        norm_ready = sem("norm_ready")
        n0_h, n0_tr, n0_cp, n0_mm, n0_out = (sem(f"n0_{k}") for k in ("h", "tr", "cp", "mm", "out"))
        n0_stored = two("n0_stored")
        l0_loaded = two("l0_loaded")
        gathered = [[sem(f"gathered{s}_{j}") for j in range(EDGE_TILES)] for s in range(2)]
        rel_ready = sem("rel_ready")
        hid_mm, hid_ready, w_done, x_ready, scat_done, agg_evac = (
            sem(k) for k in ("hid_mm", "hid_ready", "w_done", "x_ready", "scat_done", "agg_evac"))
        agg_added = two("agg_added")
        l0_done = sem("l0_done")
        n1_loaded = two("n1_loaded")
        n1_h, n1_crs, n1_mid, n1_tr, n1_cp, n1_mm, n1_sig, n1_g, n1_x = (
            sem(f"n1_{k}") for k in ("h", "crs", "mid", "tr", "cp", "mm", "sig", "g", "x"))
        stats1, eps1_ready, std1_ready, norm1_ready = (
            sem(k) for k in ("stats1", "eps1_ready", "std1_ready", "norm1_ready"))
        n1b_h, n1b_tr, n1b_cp, n1b_mm, n1b_out = (sem(f"n1b_{k}") for k in ("h", "tr", "cp", "mm", "out"))
        n1b_stored = two("n1b_stored")
        l1_loaded = two("l1_loaded")
        l1_rows = two("l1_rows")
        same_ready = sem("same_ready")
        prep_a, pick_ready, idx_step, idx_ready = (
            sem(k) for k in ("prep_a", "pick_ready", "idx_step", "idx_ready"))
        gath_mm, v_ready, parts_ready, msg_ready, ded_done, out_ready = (
            sem(k) for k in ("gath_mm", "v_ready", "parts_ready", "msg_ready", "ded_done", "out_ready"))
        scattered = [two(f"scattered{k}_") for k in range(TABLES)]
        l1_done = sem("l1_done")
        n2_loaded = two("n2_loaded")
        n2a_half, n2a_sum, n2a_tr, n2a_cp, n2a_mm, n2a_out = (
            sem(f"n2a_{k}") for k in ("half", "sum", "tr", "cp", "mm", "out"))
        n2_h, n2_tr, n2_cp, n2_t, n2_p, n2_id, n2_z, n2_half, n2_ev, n2_main, n2_g, n2_r, n2_yt, n2_y = (
            sem(f"n2_{k}") for k in ("h", "tr", "cp", "t", "p", "id", "z", "half", "ev", "main",
                                     "g", "r", "yt", "y"))
        stored = two("stored")
        CREDITS = [(n0_tr, 2), (n0_cp, 2), (n0_mm, 2), (n0_out, 2),
                   (hid_mm, 4), (hid_ready, 2), (w_done, 16), (x_ready, 16), (scat_done, 4), (agg_evac, 2),
                   (n1_tr, 2), (n1_cp, 2), (n1_mm, 2), (n1_g, 2), (n1_x, 2),
                   (n1b_tr, 2), (n1b_cp, 2), (n1b_mm, 2), (n1b_out, 2),
                   (gath_mm, 8), (msg_ready, 8), (ded_done, 8), (same_ready, 5), (out_ready, 2), 
                   (n2a_tr, 2), (n2a_cp, 2), (n2a_mm, 2), (n2a_out, 2),
                   (n2_cp, 1), (n2_p, 2), (n2_id, 1), (n2_half, 10), (n2_ev, 2), (n2_main, 2), (n2_y, 2)]
        CREDITS += [(sm, 1) for pair in (n0_stored, n1b_stored, stored) for sm in pair]

        block = ctx.enter_context(nc.Block())

        def settle(eng):
            eng.nop(nofuse=True)

        def v3(ap):
            return ap.rearrange("p (c k) -> p k c", k=3)

        def by3(ap):
            return ap.rearrange("p (k c) -> p k c", k=3)

        def sliding(ap):
            part, k, c = ap.ap
            return bass.AP(ap.tensor, ap.offset, [list(part), list(k), list(k), list(c)])

        SUM_K = 320

        def clearing(table, part, parts):
            flat = table.rearrange("(p r) c -> p (r c)", p=P)
            width = flat.shape[1] // parts
            assert width * parts == flat.shape[1] and width <= zero.shape[1]
            return flat[:, part * width:(part + 1) * width], zero[:, 0:width]

        def items(eng, body, general):
            if not general:
                with eng.Fori(0, ITEMS // 2) as u:
                    for s in range(2):
                        body(u, s, 2 * u + s, None)
            else:
                with eng.Fori(0, ITEMS) as i:
                    with eng.Fori(0, NODE_TILES // 2) as q:
                        for s in range(2):
                            body(i * (NODE_TILES // 2) + q, s, i, 2 * q + s)

        def uses(general):
            return ITEMS * NODE_TILES if general else ITEMS

        def by_input(eng, part):
            eng.wait_ge(flag_ready, 1)
            bad = eng.value_load(flag[0:1, 0:1], min_val=0, max_val=E_PAD)
            with eng.If(bad < 1):
                part(False)
            with eng.Else():
                part(True)

        @block.sync
        def _(sp):
            for sm, n in CREDITS:
                sp.sem_inc(sm, n)
            loads = [
                (X[:, :].rearrange("p (t d) -> p t d", d=D), x_in.rearrange("(t p) d -> p t d", p=P)),
                (attr[:, :], a_in), (dsti[:, :], dst_in), (ident[:, :], ident_in), (iota[:, :], iota_in),
                (cols[:, :], cols_in), (win[:, :], win_in),
                (w["lin1s"][:, :], lin1_ws), (w["fc1"][:, :], fc_w1),
                (w["fc2"][:, 0:64], fc_w2[:, 64:128]), (w["fc2"][:, 64:128], fc_w2[:, 0:64]),
                (w["fc2"][:, 128:224], fc_w2[:, 128:224]), (w["fc2"][:, 224:256], fc_w2[:, 192:224]),
                (w["scs"][:, :], sc_ws), (w["l2s"][:, :], lin2_ws), (w["l2v"][:, :], lin2_wv),
                (w["r1s"][:, 0:64], wm000.rearrange("u o w -> u (o w)")), (w["r1s"][:, 64:128], lm0),
                (w["r1s"][:, 128:160], wm011.rearrange("u o w -> u (o w)")),
                (w["wa"][0:64, :], ident_in[0:64, 0:64]),
                (w["wa"][64:96, :], wm110.rearrange("u o w -> u (o w)")),
                (w["u000"][:, :].rearrange("p (b w) -> p b w", w=64),
                 wu000.rearrange("(b i) v w -> (i v) b w", i=2)),
                (w["u110"][:, :].rearrange("p (b w) -> p b w", w=64),
                 wu110.rearrange("(b i) v w -> (i v) b w", i=4)),
                (w["u011"][:, :], wu011.rearrange("u v w -> u (v w)")),
                (w["u101"][:, :].rearrange("v (u w) -> v u w", w=32), wu101.rearrange("u v w -> v u w")),
                (w["lu0"][:, :], lu0),
            ]
            assert len(loads) == N_LOADS
            for dst, src in loads:
                sp.dma_start(dst, src).then_inc(loaded, 16)
            sp.wait_ge(zeroed, 2)
            blocks = [("lin1v", 0, lin1_wv), ("scv", 0, sc_wv), ("r1v", 0, wm101.rearrange("u o w -> u (o w)")),
                      ("r1v", V3, lm1), ("lu1", 0, lu1)]
            for name, c0, src in blocks:
                for k in range(3):
                    sp.dma_start(w[name][32 * k:32 * k + 32, c0 + 32 * k:c0 + 32 * k + 32], src)\
                        .then_inc(loaded_bd, 16)
            for k in range(2):
                sp.dma_start(w["lin1v"][32 * k:32 * k + 32, V3 + 32 * k:V3 + 32 * k + 32], lin1_wv)\
                    .then_inc(loaded_bd, 16)
            for part in range(2, 8):
                sp.dma_start(*clearing(agg0, part, 8)).then_inc(cleared, 16)

            with sp.Fori(0, UN) as u:
                for s in range(2):
                    t = 2 * u + s
                    sp.wait_ge(n0_out, t + 3)
                    sp.dma_start(h0_tab[ds(t * P, P), :], h0s[:, s, :]).then_inc(n0_stored[s], 16)

            def load0(u, s, item, window):
                n = 2 * u + s
                sp.wait_ge(x_ready, 8 * n + 8)
                sp.wait_ge(hid_mm, 2 * n + 2)
                sp.dma_start(srci[:, s, :], src_in[ds(item, 1), :, :].rearrange("i p j -> (i p) j"))\
                    .then_inc(l0_loaded[s], 16)
                sp.dma_start(ea[:, s, :, :].rearrange("p j c -> p (j c)"),
                             ea_in[ds(item, 1), :, :].rearrange("i p j -> (i p) j")).then_inc(l0_loaded[s], 16)
                sp.dma_start(est[:, s, :], es_in[ds(item, 1), :, :].rearrange("i p j -> (i p) j"))\
                    .then_inc(l0_loaded[s], 16)

            def layer0(general):
                items(sp, load0, general)
                load0(uses(general) // 2, 0, ITEMS, None)
            by_input(sp, layer0)

            sp.wait_ge(l0_done, 1)
            with sp.Fori(0, UN) as u:
                for s in range(2):
                    t = 2 * u + s
                    sp.wait_ge(n1_tr, t + 1)
                    sp.dma_start(aggt[:, s, :], agg0[ds(t * P, P), :]).then_inc(n1_loaded[s], 16)
            with sp.Fori(0, UN) as u:
                for s in range(2):
                    t = 2 * u + s
                    sp.wait_ge(n1b_out, t + 3)
                    sp.dma_start(t1_tab[ds(t * P, P), :], t1s[:, s, :]).then_inc(n1b_stored[s], 16)
            for s in range(2):
                sp.wait_ge(n1b_stored[s], 16 * UN + 1)

            def load_rows(u, s, item):
                sp.wait_ge(same_ready, 8 * u + 4 * s + 1)
                sp.dma_start(srci[:, s, :], src_in[ds(item, 1), :, :].rearrange("i p j -> (i p) j"))\
                    .then_inc(l1_rows[s], 16)
                sp.dma_start(dstrow[:, s, :], dstrow_in[ds(item, 1), :].to_broadcast([P, ITEM]))\
                    .then_inc(l1_rows[s], 16)
                sp.dma_start(srcrow[:, s, :], srcrow_in[ds(item, 1), :].to_broadcast([P, ITEM]))\
                    .then_inc(l1_rows[s], 16)

            def load1(u, s, item, window):
                n = 2 * u + s
                sp.wait_ge(gath_mm, 4 * n + 4)
                sp.wait_ge(msg_ready, 4 * n + 4)
                if window is None:
                    base = sp.value_load(dsti[0:1, ds(item * EDGE_TILES, 1)], min_val=0, max_val=N_NODES)
                else:
                    base = window * P
                sp.dma_start(t1w[:, s, :], t1_tab[ds(base, P), :]).then_inc(l1_loaded[s], 16)
                sp.dma_start(ea[:, s, :, :].rearrange("p j c -> p (j c)"),
                             ea_in[ds(item, 1), :, :].rearrange("i p j -> (i p) j")).then_inc(l1_loaded[s], 16)

            def loads1(u, s, item, window):
                if window is None:
                    load1(u, s, item, None)
                    load_rows(u + s, 1 - s, item + 1)
                else:
                    load_rows(u, s, item)
                    load1(u, s, item, window)

            def layer1(general):
                end = uses(general) // 2
                if not general:
                    load_rows(0, 0, 0)
                items(sp, loads1, general)
                if general:
                    load_rows(end, 0, ITEMS)
                load1(end, 0, ITEMS, 0 if general else None)
            by_input(sp, layer1)

            sp.wait_ge(l1_done, 1)
            with sp.Fori(0, UN) as u:
                for s in range(2):
                    t = 2 * u + s
                    sp.wait_ge(n2a_tr, t + 1)
                    for k in range(TABLES):
                        sp.dma_start(tabs[:, s, k, :], agg1[k][ds(t * P, P), :]).then_inc(n2_loaded[s], 16)
            with sp.Fori(0, UN) as u:
                for s in range(2):
                    t = 2 * u + s
                    sp.wait_ge(n2_y, t + 3)
                    sp.dma_start(out[ds(t * P, P), :], ys[:, s, :]).then_inc(stored[s], 16)
            for s in range(2):
                sp.wait_ge(stored[s], 16 * UN + 1)

        @block.gpsimd
        def _(pool):
            pool.memset(zero[:, :], 0.0).then_inc(zeroed, 1)
            pool.wait_ge(zeroed, 2)
            for s in range(2):
                pool.dma_start(*clearing(agg0, s, 8)).then_inc(agg_added[s], 16)

            for s in range(2):
                pool.wait_ge(n0_stored[s], 16 * UN + 1)

            def gather0(u, s):
                n = 2 * u + s
                pool.wait_ge(l0_loaded[s], 48 * (u + 1))
                for j in range(EDGE_TILES):
                    pool.wait_ge(x_ready, 8 * n + j + 1)
                    settle(pool)
                    pool.indirect_dma_start(
                        out=gath[:, s, j, :], out_offset=None, in_=h0_tab,
                        in_offset=bass.IndirectOffsetOnAxis(ap=srci[:, s, j:j + 1], axis=0),
                    ).then_inc(gathered[s][j], 16)

            def item0(u, s, item, window):
                n = 2 * u + s
                gather0(u + s, 1 - s)
                if window is None:
                    base = pool.value_load(dsti[0:1, ds(item * EDGE_TILES, 1)], min_val=0, max_val=N_NODES)
                else:
                    base = window * P
                pool.wait_ge(agg_evac, n + 3)
                pool.wait_ge(agg_added[1 - s], 16 * (u + s) + 16)
                pool.dma_start(agg0[ds(base, P), :], aggs[:, s, :], accum_op=ALU.add).then_inc(agg_added[s], 16)

            def layer0(general):
                gather0(0, 0)
                pool.wait_ge(cleared, 16 * 6)
                for s in range(2):
                    pool.wait_ge(agg_added[s], 16)
                items(pool, item0, general)
                for s in range(2):
                    pool.wait_ge(agg_added[s], 8 * uses(general) + 16)
                for j in range(EDGE_TILES):
                    pool.wait_ge(gathered[0][j], 8 * uses(general) + 16)
                pool.sem_inc(l0_done, 1)
            by_input(pool, layer0)

            for part in range(6):
                for k in range(TABLES):
                    if part >= 2:
                        pool.wait_ge(scattered[k][part % 2], 16 * (part // 2))
                    pool.dma_start(*clearing(agg1[k], part, 6)).then_inc(scattered[k][part % 2], 16)

            def item1(u, s, item, window):
                n = 2 * u + s
                pool.wait_ge(idx_ready, n + 2)
                for j in range(EDGE_TILES):
                    k = j % TABLES
                    if j < TABLES:
                        pool.wait_ge(scattered[k][1 - s], 32 * (u + s) + 48)
                    else:
                        pool.wait_ge(scattered[k][s], 32 * u + 64)
                    settle(pool)
                    pool.indirect_dma_start(
                        out=agg1[k], out_offset=bass.IndirectOffsetOnAxis(ap=scidx[:, s, j:j + 1], axis=0),
                        in_=outm[:, s, j, 0:MSG], in_offset=None, compute_op=ALU.add,
                    ).then_inc(scattered[k][s], 16)

            def layer1(general):
                for k in range(TABLES):
                    for s in range(2):
                        pool.wait_ge(scattered[k][s], 48)
                items(pool, item1, general)
                for k in range(TABLES):
                    for s in range(2):
                        pool.wait_ge(scattered[k][s], 16 * uses(general) + 48)
                pool.sem_inc(l1_done, 1)
            by_input(pool, layer1)

            with pool.Fori(0, UN) as uu:
                for s in range(2):
                    t = 2 * uu + s
                    pool.wait_ge(n2_h, t + 1)
                    pool.wait_ge(n2_half, 10 * t + 10)
                    for k in range(3):
                        lo = S_CH + 32 * k
                        pool.tensor_tensor(
                            gz[:, k, :].rearrange("p (u v) -> p u v", v=32),
                            hs[:, s, lo:lo + 32].unsqueeze(2).to_broadcast([P, 32, 32]),
                            a_s[:, s, lo:lo + 32].unsqueeze(1).to_broadcast([P, 32, 32]), ALU.mult)\
                            .then_inc(n2_g, 1)
                    pool.wait_ge(n2_g, 5 * t + 3)
                    pool.tensor_tensor(gz[:, 1, :], gz[:, 1, :], gz[:, 2, :], ALU.add).then_inc(n2_g, 1)
                    pool.wait_ge(n2_g, 5 * t + 4)
                    pool.tensor_tensor(gz[:, 0, :], gz[:, 0, :], gz[:, 1, :], ALU.add).then_inc(n2_g, 1)

        @block.scalar
        def _(act):
            def normed(x_tiles, layer, t, s):
                act.activation(hs[:, s, 0:S_CH], x_tiles[:, ds(t * D, S_CH)], ACT.Relu,
                               scale=rstd[layer][:, ds(t, 1)], bias=shift[layer][:, ds(t, 1)])
                return act.activation(by3(hs[:, s, S_CH:D]), v3(x_tiles[:, ds(t * D + S_CH, V3)]), ACT.Relu,
                                      scale=rstd[layer][:, ds(t, 1)], bias=shift[layer][:, ds(t, 1)])

            act.wait_ge(loaded, 16 * N_LOADS)
            act.wait_ge(eps_ready, 1)
            act.activation(std[:, :], vareps[:, :], ACT.Sqrt).then_inc(std_ready, 1)
            act.wait_ge(norm_ready, 1)
            with act.Fori(0, UN) as u:
                for s in range(2):
                    t = 2 * u + s
                    act.wait_ge(n0_tr, t + 1)
                    normed(X, 0, t, s).then_inc(n0_h, 1)
                    act.wait_ge(n0_mm, t + 3)
                    act.wait_ge(n0_stored[s], 16 * u + 1)
                    act.activation(h0s[:, s, :], PS[:, 2 + s, 0:H0], ACT.Copy,
                                   scale=attr[:, ds(t, 1)]).then_inc(n0_out, 1)

            def silu(u, s):
                n = 2 * u + s
                act.wait_ge(w_done, 8 * n + 8)
                for h in range(2):
                    act.wait_ge(hid_mm, 2 * n + h + 5)
                    act.activation(hid[:, s, h * 512:(h + 1) * 512], PS[0:64, 2 + h, :], ACT.Silu,
                                   scale=float(FC) ** -0.5).then_inc(hid_ready, 1)

            def item0(u, s, item, window):
                n = 2 * u + s
                silu(u + s, 1 - s)
                act.wait_ge(scat_done, 8 * n + 12)
                act.wait_ge(agg_added[s], 16 * u + 16)
                sums = PS[:, 4 + 2 * s:6 + 2 * s, :].rearrange("p b c -> p (b c)")
                parts = sums[:, SUM_K:SUM_K + 3 * 192].rearrange("p (k g) -> p k g", k=3)
                groups = aggs[:, s, G0:AGG].rearrange("p (k g) -> p k g", k=3)
                act.activation(aggs[:, s, 0:64], sums[:, 0:64], ACT.Copy)
                act.activation(by3(aggs[:, s, 64:G0]), parts[:, :, 96:128], ACT.Copy)
                act.activation(groups[:, :, 0:64], parts[:, :, 0:64], ACT.Copy)
                act.activation(groups[:, :, 64:96], by3(sums[:, 64:160]), ACT.Copy)
                act.activation(groups[:, :, 96:160], parts[:, :, 128:192], ACT.Copy).then_inc(agg_evac, 1)

            def layer0(general):
                silu(0, 0)
                items(act, item0, general)
            by_input(act, layer0)

            act.wait_ge(l0_done, 1)
            with act.Fori(0, UN) as u:
                for s in range(2):
                    t = 2 * u + s
                    act.wait_ge(n1_tr, t + 1)
                    normed(X, 0, t, s).then_inc(n1_h, 1)
                    act.wait_ge(n1_mm, t + 3)
                    act.wait_ge(n1_x, t + 1)
                    act.activation(sig[:, s, :], PS[:, 4 + s, 0:96], ACT.Sigmoid,
                                   scale=attr[:, ds(t, 1)]).then_inc(n1_sig, 1)
            act.wait_ge(eps1_ready, 1)
            act.activation(std[:, :], vareps[:, :], ACT.Sqrt).then_inc(std1_ready, 1)
            act.wait_ge(norm1_ready, 1)
            with act.Fori(0, UN) as u:
                for s in range(2):
                    t = 2 * u + s
                    act.wait_ge(n1b_tr, t + 1)
                    act.wait_ge(n1b_out, t + 1)
                    normed(X1, 1, t, s).then_inc(n1b_h, 1)
                    act.wait_ge(n1b_mm, t + 3)
                    act.wait_ge(n1b_stored[s], 16 * u + 1)
                    uv = t1s[:, s, 0:2 * D].rearrange("p (g d) -> p g d", g=2)
                    act.activation(uv[:, :, 0:V3], PS[:, 2 + s, 160:352].rearrange("p (g d) -> p g d", g=2), ACT.Copy)
                    act.activation(uv[:, :, V3:D], PS[:, 2 + s, 0:128].rearrange("p (g d) -> p g d", g=2), ACT.Copy)
                    act.activation(t1s[:, s, 2 * D:2 * D + 32], PS[:, 2 + s, 128:160], ACT.Copy)
                    act.wait_ge(n1b_h, t + 1)
                    act.activation(t1s[:, s, 2 * D + 32:T1_COLS], hs[:, s, S_CH:D], ACT.Copy).then_inc(n1b_out, 1)

            def vcopy(u, s, m):
                q = m % 2
                pair = 8 * u + 4 * s + m
                act.wait_ge(gath_mm, pair + 9)
                act.wait_ge(ded_done, pair + 7)
                act.activation(msg[:, q, :, 0:D], PS[:, 2 * q:2 * q + 2, D:2 * D], ACT.Copy).then_inc(v_ready, 1)

            def item1(u, s, item, window):
                for m in range(4):
                    pair = 8 * u + 4 * s + m
                    if m < 3:
                        vcopy(u, s, m + 1)
                    else:
                        vcopy(u + s, 1 - s, 0)
                    act.wait_ge(ded_done, pair + 9)
                    if m == 0:
                        for k in range(TABLES):
                            act.wait_ge(scattered[k][s], 32 * u + 48)
                    act.activation(outm[:, s, 2 * m:2 * m + 2, :],
                                   PS[:, 4 + m % 2, 0:2 * (MSG + 1)].rearrange("p (i d) -> p i d", i=2),
                                   ACT.Copy).then_inc(out_ready, 1)

            def layer1(general):
                vcopy(0, 0, 0)
                items(act, item1, general)
            by_input(act, layer1)

            act.wait_ge(l1_done, 1)
            with act.Fori(0, UN) as u:
                for s in range(2):
                    t = 2 * u + s
                    act.wait_ge(n2a_mm, t + 3)
                    act.activation(A1[:, ds(t * D, S_CH)], PS[:, 2 + s, 0:64], ACT.Copy).then_inc(n2a_out, 1)

            def head(t, s):
                act.wait_ge(n2_y, t + 1)
                act.activation(a_s[:, s, :], A1[:, ds(t * D, D)], ACT.Copy)
                normed(X1, 1, t, s).then_inc(n2_h, 1)

            act.wait_ge(n2a_out, NODE_TILES + 2)
            head(0, 0)
            with act.Fori(0, UN) as u:
                for s in range(2):
                    t = 2 * u + s
                    head(t + 1, 1 - s)
                    for e in range(10):
                        act.wait_ge(n2_half, 10 * t + e + 11)
                        act.wait_ge(n2_main, 10 * t + e + 1)
                        act.activation(zt[:, e % 2, :], PS[:, 5 + e % 2, :], ACT.Copy).then_inc(n2_ev, 1)

        @block.vector
        def _(dve):
            steps = [0]

            def step(ins):
                steps[0] += 1
                ins.then_inc(setup, 1)
                dve.wait_ge(setup, steps[0])

            def tile_stats(x_tiles, t, s, counted):
                settle(dve)
                dve.bn_stats(bn6[:, s, :], x_tiles[:, ds(t * D, D)]).then_inc(counted, 1)
                dve.wait_ge(counted, 3 * t + 1)
                settle(dve)
                dve.bn_aggr(bn2[:, s, :], bn6[:, s, :]).then_inc(counted, 1)
                dve.wait_ge(counted, 3 * t + 2)
                dve.tensor_copy(moments[:, ds(t, 1), :].rearrange("p o m -> p (o m)"), bn2[:, s, :])\
                    .then_inc(counted, 1)

            def layernorm(x_tiles, layer, counted, eps_sem, std_sem, norm_sem, first):
                if first:
                    with dve.Fori(0, UN) as u:
                        for s in range(2):
                            t = 2 * u + s
                            tile_stats(x_tiles, t, s, counted)
                dve.wait_ge(counted, 3 * NODE_TILES)
                mean = moments[:, :, 0:1].rearrange("p t o -> p (t o)")
                var = moments[:, :, 1:2].rearrange("p t o -> p (t o)")
                dve.tensor_scalar(vareps[:, :], var, EPS, None, ALU.add).then_inc(eps_sem, 1)
                dve.wait_ge(std_sem, 1)
                step(dve.reciprocal(rstd[layer][:, 0:NODE_TILES], std[:, :]))
                dve.scalar_tensor_tensor(out=shift[layer][:, 0:NODE_TILES], in0=mean, scalar=-1.0,
                                         in1=rstd[layer][:, 0:NODE_TILES], op0=ALU.mult, op1=ALU.mult)\
                    .then_inc(norm_sem, 1)

            for name in ("lin1v", "scv", "r1v"):
                dve.memset(w[name][:, :], 0.0)
            dve.memset(w["lu1"][:, :], 0.0).then_inc(zeroed, 1)
            dve.memset(X1[:, NODE_TILES * D:], 0.0)
            dve.memset(A1[:, NODE_TILES * D:], 0.0)
            for l in range(2):
                dve.memset(rstd[l][:, NODE_TILES:], 0.0)
                dve.memset(shift[l][:, NODE_TILES:], 0.0)
            step(dve.memset(ones[:, :], 1.0))
            dve.wait_ge(loaded, 16 * N_LOADS)
            dve.wait_ge(loaded_bd, 16 * 17)
            for ap, factor in weights_into(w):
                last = dve.tensor_scalar(ap, ap, factor, None, ALU.mult)
            last.then_inc(scaled, 1)
            step(dve.tensor_copy(dstf[:, :], dsti[:, :]))
            dve.sem_inc(base_mm, 1)
            dve.wait_ge(base_mm, 2)
            step(dve.tensor_copy(basef[:, :], PS[:, 0, 0:ITEMS + 1]))
            step(dve.tensor_tensor(rel_all[:, :].rearrange("p (i j) -> p i j", j=EDGE_TILES),
                                   dstf[:, :].rearrange("p (i j) -> p i j", j=EDGE_TILES),
                                   basef[:, :].unsqueeze(2).to_broadcast([P, ITEMS + 1, EDGE_TILES]), ALU.subtract))
            step(dve.tensor_scalar(out_of[:, :], rel_all[:, :], 0.0, None, ALU.is_lt))
            step(dve.scalar_tensor_tensor(out=out_of[:, :], in0=rel_all[:, :], scalar=float(P - 1),
                                          in1=out_of[:, :], op0=ALU.is_gt, op1=ALU.add))
            step(dve.tensor_reduce(far[:, :], out_of[:, :], AX.X, ALU.add))
            dve.sem_inc(far_mm, 1)
            dve.wait_ge(far_mm, 2)
            dve.tensor_copy(flag[0:1, 0:1], PS[0:1, 1, 0:1]).then_inc(flag_ready, 1)
            layernorm(X, 0, stats, eps_ready, std_ready, norm_ready, True)
            with dve.Fori(0, UN) as u:
                for s in range(2):
                    t = 2 * u + s
                    dve.wait_ge(n0_tr, t + 3)
                    dve.wait_ge(n0_mm, t + 1)
                    dve.tensor_copy(hts[:, s, :], PS[0:64, s, 0:128])
                    dve.tensor_copy(htv[:, s, :], PS[0:96, s, 128:256]).then_inc(n0_cp, 1)

            def item0(u, s, item, window):
                n = 2 * u + s
                dve.wait_ge(l0_loaded[s], 48 * (u + 1))
                base = basef[:, ds(item, 1)] if window is None else win[:, ds(window, 1)]
                dve.tensor_scalar(rel[:, s, :], dstf[:, ds(item * EDGE_TILES, EDGE_TILES)], base, None,
                                  ALU.subtract).then_inc(rel_ready, 1)
                dve.wait_ge(rel_ready, n + 1)
                for m in range(EDGE_TILES // 2):
                    j, b = 2 * m, 2 * (m % 2)
                    tile = 8 * n + j
                    dve.wait_ge(scat_done, tile + 2)
                    for i in range(2):
                        for k in range(4):
                            dve.tensor_scalar(sel[:, b + i, k, :], iota[:, :], rel[:, s, j + i:j + i + 1],
                                              ea[:, s, j + i, k:k + 1], ALU.is_equal, ALU.mult)
                    dve.wait_ge(w_done, tile + 18)
                    for i in range(2):
                        dve.wait_ge(gathered[s][j + i], 16 * (u + 1))
                    wt = PS[:, m % 2, :].rearrange("p (t w) -> p t w", t=2)
                    x = xw[:, b * X_STEP:(b + 2) * X_STEP].rearrange("p (t c) -> p t c", t=2)
                    dve.tensor_tensor(x[:, :, 0:128].rearrange("p t (i c) -> p t i c", i=2),
                                      wt[:, :, 0:128].rearrange("p t (i c) -> p t i c", i=2),
                                      gath[:, s, j:j + 2, 0:64].unsqueeze(2).to_broadcast([P, 2, 2, 64]), ALU.mult)
                    dve.tensor_tensor(x[:, :, 128:224].rearrange("p t (k c) -> p t k c", k=3),
                                      wt[:, :, 128:160].unsqueeze(2).to_broadcast([P, 2, 3, V_CH]),
                                      gath[:, s, j:j + 2, 64:160].rearrange("p t (k c) -> p t k c", k=3), ALU.mult)
                    for i in range(2):
                        dve.tensor_tensor(x[:, i, 224:X_STEP].rearrange("p (k m c) -> p k m c", k=3, m=3),
                                          wt[:, i, 160:256].rearrange("p (m c) -> p m c", m=3).unsqueeze(1)
                                          .to_broadcast([P, 3, 3, V_CH]),
                                          sliding(by3(gath[:, s, j + i, 64:160])), ALU.mult).then_inc(x_ready, 1)

            by_input(dve, lambda general: items(dve, item0, general))

            dve.wait_ge(l0_done, 1)
            with dve.Fori(0, UN) as u:
                for s in range(2):
                    t = 2 * u + s
                    dve.wait_ge(n1_loaded[s], 16 * (u + 1))
                    q = lambda g, i: aggt[:, s, G0 + GROUP * g + 96 + 32 * i:G0 + GROUP * g + 128 + 32 * i]
                    for k in range(3):
                        dve.tensor_tensor(crs[:, s, k, :], q((k + 2) % 3, 1), q((k + 1) % 3, 0), ALU.subtract)
                    dve.tensor_reduce(crs[:, s, 3, :], aggt[:, s, 64:G0].rearrange("p (k c) -> p c k", k=3),
                                      AX.X, ALU.add).then_inc(n1_crs, 1)
                    dve.wait_ge(n1_crs, t + 1)
                    dve.tensor_copy(aggt[:, s, 64:96], crs[:, s, 3, :])
                    dve.tensor_copy(aggt[:, s, G0:AGG].rearrange("p (k g) -> p k g", k=3)[:, :, 96:128],
                                    crs[:, s, 0:3, :]).then_inc(n1_mid, 1)
                    dve.wait_ge(n1_tr, t + 3)
                    dve.wait_ge(n1_mm, t + 1)
                    dve.tensor_copy(hts[:, s, :], PS[0:64, s, 0:128])
                    dve.tensor_copy(htv[:, s, :], PS[0:96, s, 128:256])
                    dve.tensor_copy(midts[:, s, :], PS[0:96, s, 256:384])
                    dve.tensor_copy(midtv[:, s, :], PS[:, 2 + s, 0:384]).then_inc(n1_cp, 1)
                    dve.wait_ge(n1_sig, t + 1)
                    dve.scalar_tensor_tensor(out=gat[:, s, 0:64], in0=PS[:, 4 + s, 0:64], scalar=attr[:, ds(t, 1)],
                                             in1=sig[:, s, 0:64], op0=ALU.mult, op1=ALU.mult)
                    dve.scalar_tensor_tensor(out=by3(gat[:, s, 64:160]), in0=by3(PS[:, 4 + s, 96:192]),
                                             scalar=attr[:, ds(t, 1)],
                                             in1=sig[:, s, 64:96].unsqueeze(1).to_broadcast([P, 3, 32]),
                                             op0=ALU.mult, op1=ALU.mult).then_inc(n1_g, 1)
                    dve.wait_ge(n1_g, t + 3)
                    dve.tensor_tensor(X1[:, ds(t * D, 64)], X[:, ds(t * D, 64)], gat[:, s, 0:64], ALU.add)
                    dve.tensor_tensor(v3(X1[:, ds(t * D + 64, V3)]), v3(X[:, ds(t * D + 64, V3)]),
                                      by3(gat[:, s, 64:160]), ALU.add).then_inc(n1_x, 1)
                    dve.wait_ge(n1_x, t + 3)
                    tile_stats(X1, t, s, stats1)
            layernorm(X1, 1, stats1, eps1_ready, std1_ready, norm1_ready, False)
            with dve.Fori(0, UN) as u:
                for s in range(2):
                    t = 2 * u + s
                    dve.wait_ge(n1b_tr, t + 3)
                    dve.wait_ge(n1b_mm, t + 1)
                    dve.tensor_copy(hts[:, s, :], PS[0:64, s, 0:128])
                    dve.tensor_copy(htv[:, s, :], PS[0:96, s, 128:256]).then_inc(n1b_cp, 1)

            def base_of(item, window):
                return basef[:, ds(item, 1)] if window is None else win[:, ds(window, 1)]

            def prepare_ids(u, s, base):
                dve.wait_ge(l1_rows[s], 48 * (u + 1))
                dve.tensor_copy(srcf[:, s, :], srci[:, s, :])
                dve.tensor_tensor(nodeid[:, s:s + 1], base, cols[:, 0:1], ALU.add).then_inc(prep_a, 1)

            def prepare_pick(u, s):
                n = 2 * u + s
                dve.wait_ge(prep_a, n + 1)
                dve.wait_ge(gath_mm, 4 * n + 4)
                dve.tensor_scalar(away[:, s, :], srcf[:, s, :], -1.0, cols[:, 3:4], ALU.mult, ALU.add)
                dve.tensor_scalar(pick[:, s, :], dstrow[:, s, :], nodeid[:, s:s + 1], None, ALU.is_equal)\
                    .then_inc(pick_ready, 1)

            def prepare_same(u, s, m):
                j = 2 * m
                dve.wait_ge(ded_done, 8 * u + 4 * s + m + 1)
                dve.tensor_tensor(same[:, s, j * P:(j + 2) * P].rearrange("p (j f) -> p j f", j=2),
                                  srcrow[:, s, j * P:(j + 2) * P].rearrange("p (j f) -> p j f", j=2),
                                  srcf[:, s, j:j + 2].unsqueeze(2).to_broadcast([P, 2, P]), ALU.is_equal)\
                    .then_inc(same_ready, 1)

            def indices(u, s):
                n = 2 * u + s
                dve.wait_ge(pick_ready, n + 1)
                dve.wait_ge(out_ready, 4 * n + 2)
                for k in range(TABLES):
                    dve.wait_ge(scattered[k][1 - s], 32 * (u + s) + 16)
                dve.scalar_tensor_tensor(out=moved[:, :], in0=outm[:, 1 - s, :, MSG], scalar=cols[:, 2:3],
                                         in1=away[:, 1 - s, :], op0=ALU.is_gt, op1=ALU.mult).then_inc(idx_step, 1)
                dve.wait_ge(idx_step, n + 1)
                dve.tensor_tensor(scidx[:, 1 - s, :], moved[:, :], srcf[:, 1 - s, :], ALU.add)\
                    .then_inc(idx_ready, 1)

            def item1(u, s, item, window):
                for m in range(4):
                    q = m % 2
                    pair = 8 * u + 4 * s + m
                    e = ea[:, s, 2 * m:2 * m + 2, :]
                    g = PS[:, 2 * q:2 * q + 2, :]
                    ek = e[:, :, 0:3].unsqueeze(3).to_broadcast([P, 2, 3, V_CH])
                    if m == 0:
                        dve.wait_ge(l1_loaded[s], 32 * (u + 1))
                    dve.wait_ge(v_ready, pair + 1)
                    dve.tensor_tensor(tx[:, q, :, :, :], g[:, :, 352:448].rearrange("p i (k c) -> p i k c", k=3), ek,
                                      ALU.mult)
                    dve.tensor_tensor(tz[:, q, :, :, :],
                                      g[:, :, 320:352].unsqueeze(2).to_broadcast([P, 2, 3, V_CH]), ek, ALU.mult)
                    for i in range(2):
                        last = dve.scalar_tensor_tensor(out=msg[:, q, i, 0:D], in0=g[:, i, 0:D], scalar=e[:, i, 3:4],
                                                        in1=msg[:, q, i, 0:D], op0=ALU.mult, op1=ALU.add)
                    last.then_inc(parts_ready, 1)
                    dve.wait_ge(parts_ready, pair + 1)
                    dve.tensor_reduce(msg[:, q, :, D:MSG], tx[:, q, :, :, :].rearrange("p i k c -> p i c k"),
                                      AX.X, ALU.add)
                    dve.tensor_tensor(msg[:, q, :, 0:V3].rearrange("p i (k c) -> p i k c", k=3),
                                      msg[:, q, :, 0:V3].rearrange("p i (k c) -> p i k c", k=3),
                                      tz[:, q, :, :, :], ALU.add).then_inc(msg_ready, 1)
                    if m == 0:
                        prepare_same(u, s, 3)
                        indices(u, s)
                        dve.wait_ge(idx_ready, 2 * u + s + 1)
                        prepare_ids(u + s, 1 - s, base_of(item + 1, None if window is None else window + 1))
                    elif m == 1:
                        prepare_pick(u + s, 1 - s)
                    elif m == 2:
                        prepare_same(u + s, 1 - s, 0)
                        prepare_same(u + s, 1 - s, 1)
                    else:
                        prepare_same(u + s, 1 - s, 2)

            def layer1(general):
                for k in range(TABLES):
                    for s in range(2):
                        dve.wait_ge(scattered[k][s], 48)
                dve.memset(outm[:, 1, :, MSG], 0.0)
                dve.memset(away[:, 1, :], 0.0)
                dve.memset(srcf[:, 1, :], 0.0)
                dve.tensor_copy(msg[:, :, :, MSG], cols[:, 1:2].unsqueeze(2).to_broadcast([P, 2, 2]))
                prepare_ids(0, 0, base_of(0, 0 if general else None))
                prepare_pick(0, 0)
                for m in range(3):
                    prepare_same(0, 0, m)
                items(dve, item1, general)
                indices(uses(general) // 2, 0)
            by_input(dve, layer1)

            dve.wait_ge(l1_done, 1)
            with dve.Fori(0, UN) as u:
                for s in range(2):
                    t = 2 * u + s
                    dve.wait_ge(n2_loaded[s], 16 * TABLES * (u + 1))
                    dve.tensor_tensor(half[:, s, :, :], tabs[:, s, 0:2, :], tabs[:, s, 2:4, :], ALU.add)\
                        .then_inc(n2a_half, 1)
                    dve.wait_ge(n2a_half, t + 1)
                    dve.wait_ge(n2a_tr, t + 1)
                    dve.tensor_tensor(A1[:, ds(t * D + S_CH, V3)], half[:, s, 0, 0:V3], half[:, s, 1, 0:V3], ALU.add)
                    dve.tensor_tensor(mt[:, s, :], half[:, s, 0, V3:MSG], half[:, s, 1, V3:MSG], ALU.add)\
                        .then_inc(n2a_sum, 1)
                    dve.wait_ge(n2a_tr, t + 3)
                    dve.wait_ge(n2a_mm, t + 1)
                    dve.tensor_copy(mtt[:, s, :], PS[0:96, s, 0:128]).then_inc(n2a_cp, 1)

            def copies(t, s):
                dve.wait_ge(n2_tr, t + 1)
                dve.tensor_copy(hts[:, s, :], PS[0:64, 0, 0:128])
                dve.tensor_copy(htv[:, s, :], PS[0:96, 0, 128:256])
                dve.tensor_copy(ats[:, s, :], PS[0:64, 0, 256:384]).then_inc(n2_cp, 1)

            def times(out_ap, banks, by):
                return dve.tensor_tensor(
                    out_ap.rearrange("p k (i w) -> p k i w", w=32),
                    banks.rearrange("p b (i w) -> p (b i) w", w=32).unsqueeze(1).to_broadcast([P, 3, 32, 32]),
                    by3(by).unsqueeze(3).to_broadcast([P, 3, 32, 32]), ALU.mult)

            copies(0, 0)
            with dve.Fori(0, UN) as u:
                for s in range(2):
                    t = 2 * u + s
                    for c in range(4):
                        dve.wait_ge(n2_half, 10 * t + 2 * c + (8 if c >= 2 else 6))
                        dve.wait_ge(n2_h, t + 1)
                        dve.tensor_tensor(zout[:, c % 2, :].rearrange("p (u v) -> p u v", v=64),
                                          hs[:, s, 16 * c:16 * c + 16].unsqueeze(2).to_broadcast([P, 16, 64]),
                                          a_s[:, s, 0:64].unsqueeze(1).to_broadcast([P, 16, 64]), ALU.mult)\
                            .then_inc(n2_z, 1)
                    dve.wait_ge(n2_t, 2 * t + 1)
                    dve.wait_ge(n2_id, t + 1)
                    times(prod[:, :, :], PS[:, 1:3, :], a_s[:, s, 64:160]).then_inc(n2_p, 1)
                    dve.wait_ge(n2_t, 2 * t + 2)
                    times(prod2[:, :, :], PS[:, 3:5, :], hs[:, s, 64:160]).then_inc(n2_p, 1)
                    dve.wait_ge(n2_p, 2 * t + 4)
                    dve.tensor_reduce(by3(sum2[:, :]), prod2[:, :, :].rearrange("p k (i w) -> p k w i", w=32),
                                      AX.X, ALU.add).then_inc(n2_r, 1)
                    copies(t + 1, 1 - s)
                    dve.wait_ge(n2_r, t + 1)
                    dve.wait_ge(n2_main, 10 * t + 12)
                    dve.tensor_tensor(yt[:, :], PS[:, 7, 0:D], hs[:, s, :], ALU.add).then_inc(n2_yt, 1)
                    dve.wait_ge(n2_yt, 3 * t + 1)
                    dve.tensor_tensor(yt[:, 64:D], yt[:, 64:D], sum2[:, :], ALU.add).then_inc(n2_yt, 1)
                    dve.wait_ge(n2_yt, 3 * t + 2)
                    dve.wait_ge(stored[s], 16 * u + 1)
                    dve.tensor_tensor(ys[:, s, 0:64], yt[:, 0:64], X1[:, ds(t * D, 64)], ALU.add).then_inc(n2_yt, 1)
                    dve.tensor_tensor(v3(ys[:, s, 64:160]), by3(yt[:, 64:160]), v3(X1[:, ds(t * D + 64, V3)]),
                                      ALU.add).then_inc(n2_y, 1)

        @block.tensor
        def _(pe):
            def mm(o, l, r, start=True, stop=True):
                return pe.matmul(o, l, r, start=start, stop=stop, skip_group_check=True)

            def turn(o, src):
                return pe.transpose(o, src, ident[:, :])

            pe.wait_ge(setup, 1)
            pe.wait_ge(loaded, 16 * N_LOADS)
            pe.wait_ge(base_mm, 1)
            mm(PS[:, 0, 0:ITEMS + 1], ones[0:1, :],
               dstf[0:1, :].rearrange("p (i j) -> p i j", j=EDGE_TILES)[:, :, 0]).then_inc(base_mm, 1)
            pe.wait_ge(far_mm, 1)
            mm(PS[0:1, 1, 0:1], far[:, :], ones[:, 0:1]).then_inc(far_mm, 1)
            pe.wait_ge(scaled, 1)
            pe.wait_ge(flag_ready, 1)
            with pe.Fori(0, UN) as u:
                for s in range(2):
                    t = 2 * u + s
                    pe.wait_ge(n0_h, t + 1)
                    pe.wait_ge(n0_cp, t + 1)
                    turn(PS[0:96, s, 128:256], hs[:, s, 64:160])
                    turn(PS[0:64, s, 0:128], hs[:, s, 0:64]).then_inc(n0_tr, 1)
                    pe.wait_ge(n0_cp, t + 3)
                    pe.wait_ge(n0_out, t + 1)
                    mm(PS[:, 2 + s, 0:64], hts[:, s, :], w["lin1s"][:, :])
                    mm(PS[:, 2 + s, 64:H0], htv[:, s, :], w["lin1v"][:, :]).then_inc(n0_mm, 1)

            def hidden(u, s):
                n = 2 * u + s
                pe.wait_ge(l0_loaded[s], 48 * (u + 1))
                for h in range(2):
                    pe.wait_ge(hid_ready, 2 * n + h + 1)
                    settle(pe)
                    mm(PS[0:64, 2 + h, :], w["fc1"][:, :], est[:, s, h * 512:(h + 1) * 512]).then_inc(hid_mm, 1)

            def radial(u, s, j):
                n = 2 * u + s
                pe.wait_ge(x_ready, 8 * n + j + 14 - j % 2)
                if j % 4 == 0:
                    pe.wait_ge(hid_ready, 2 * n + j // 4 + 3)
                mm(PS[:, j // 2 % 2, W_COLS * (j % 2):W_COLS * (j % 2 + 1)], hid[:, s, j * P:(j + 1) * P], w["fc2"][:, :]).then_inc(w_done, 1)

            def item0(u, s, item, window):
                n = 2 * u + s
                sums = PS[:, 4 + 2 * s:6 + 2 * s, :].rearrange("p b c -> p (b c)")
                for j in range(EDGE_TILES):
                    b = j % 4
                    x = b * X_STEP
                    first, last = j == 0, j == EDGE_TILES - 1
                    if first:
                        pe.wait_ge(agg_evac, n + 1)
                    pe.wait_ge(x_ready, 8 * n + j + 17)
                    mm(sums[:, 0:160], sel[:, b, 0, :], xw[:, x + 64:x + 224], first, last)
                    for k in range(3):
                        to = 224 + 96 * k
                        done = mm(sums[:, SUM_K + 192 * k:SUM_K + 192 * k + 192], sel[:, b, 1 + k, :],
                                  xw[:, x:x + 2 * to].rearrange("p (g c) -> p g c", g=2)[:, :, 0:96],
                                  first and k == 1, last)
                    done.then_inc(scat_done, 1)
                    for ahead in (j + 3, j + 4) if j % 2 else ():
                        if ahead < 8:
                            radial(u, s, ahead)
                        else:
                            radial(u + s, 1 - s, ahead - 8)
                    if j == 2:
                        hidden(u + s, 1 - s)

            def layer0(general):
                hidden(0, 0)
                for j in range(4):
                    radial(0, 0, j)
                items(pe, item0, general)
            by_input(pe, layer0)

            pe.wait_ge(l0_done, 1)
            with pe.Fori(0, UN) as u:
                for s in range(2):
                    t = 2 * u + s
                    pe.wait_ge(n1_h, t + 1)
                    pe.wait_ge(n1_mid, t + 1)
                    pe.wait_ge(n1_cp, t + 1)
                    turn(PS[0:96, s, 128:256], hs[:, s, 64:160])
                    turn(PS[0:64, s, 0:128], hs[:, s, 0:64])
                    turn(PS[0:96, s, 256:384], aggt[:, s, 0:96])
                    for k in range(3):
                        last = turn(PS[:, 2 + s, P * k:P * k + P], aggt[:, s, G0 + GROUP * k:G0 + GROUP * k + P])
                    last.then_inc(n1_tr, 1)
                    pe.wait_ge(n1_cp, t + 3)
                    pe.wait_ge(n1_g, t + 1)
                    o = PS[:, 4 + s, :]
                    mm(o[:, 0:96], hts[:, s, :], w["scs"][:, :], True, False)
                    mm(o[:, 0:96], midts[:, s, :], w["l2s"][:, :], False, True)
                    mm(o[:, 96:192], htv[:, s, :], w["scv"][:, :], False, False)
                    for k in range(3):
                        last = mm(o[:, 96 + 32 * k:128 + 32 * k], midtv[:, s, P * k:P * k + P], w["l2v"][:, :],
                                  False, True)
                    last.then_inc(n1_mm, 1)
            with pe.Fori(0, UN) as u:
                for s in range(2):
                    t = 2 * u + s
                    pe.wait_ge(n1b_h, t + 1)
                    pe.wait_ge(n1b_cp, t + 1)
                    turn(PS[0:96, s, 128:256], hs[:, s, 64:160])
                    turn(PS[0:64, s, 0:128], hs[:, s, 0:64]).then_inc(n1b_tr, 1)
                    pe.wait_ge(n1b_cp, t + 3)
                    pe.wait_ge(n1b_out, t + 1)
                    mm(PS[:, 2 + s, 0:160], hts[:, s, :], w["r1s"][:, :])
                    mm(PS[:, 2 + s, 160:352], htv[:, s, :], w["r1v"][:, :]).then_inc(n1b_mm, 1)

            def pickup(u, s, m):
                pair = 8 * u + 4 * s + m
                q = m % 2
                if m == 0:
                    pe.wait_ge(l1_loaded[s], 32 * (u + 1))
                    pe.wait_ge(pick_ready, 2 * u + s + 1)
                pe.wait_ge(msg_ready, pair + 7)
                for i in range(2):
                    j = 2 * m + i
                    last = mm(PS[:, 2 * q + i, 0:T1_COLS], pick[:, s, j * P:(j + 1) * P], t1w[:, s, :])
                last.then_inc(gath_mm, 1)

            def item1(u, s, item, window):
                for m in range(4):
                    pair = 8 * u + 4 * s + m
                    q = m % 2
                    if m < 3:
                        pickup(u, s, m + 1)
                    else:
                        pickup(u + s, 1 - s, 0)
                    pe.wait_ge(same_ready, pair + 6)
                    pe.wait_ge(msg_ready, pair + 9)
                    pe.wait_ge(out_ready, pair + 1)
                    for i in range(2):
                        j = 2 * m + i
                        last = mm(PS[:, 4 + q, (MSG + 1) * i:(MSG + 1) * (i + 1)], same[:, s, j * P:(j + 1) * P], msg[:, q, i, :])
                    last.then_inc(ded_done, 1)

            def layer1(general):
                pickup(0, 0, 0)
                items(pe, item1, general)
            by_input(pe, layer1)

            pe.wait_ge(l1_done, 1)
            with pe.Fori(0, UN) as u:
                for s in range(2):
                    t = 2 * u + s
                    pe.wait_ge(n2a_sum, t + 1)
                    pe.wait_ge(n2a_cp, t + 1)
                    turn(PS[0:96, s, 0:128], mt[:, s, :]).then_inc(n2a_tr, 1)
                    pe.wait_ge(n2a_cp, t + 3)
                    pe.wait_ge(n2a_out, t + 1)
                    mm(PS[:, 2 + s, 0:64], mtt[:, s, :], w["wa"][:, :]).then_inc(n2a_mm, 1)

            def head(t, s):
                pe.wait_ge(n2_h, t + 1)
                pe.wait_ge(n2_cp, t + 1)
                turn(PS[0:96, 0, 128:256], hs[:, s, 64:160])
                turn(PS[0:64, 0, 0:128], hs[:, s, 0:64])
                turn(PS[0:64, 0, 256:384], a_s[:, s, 0:64]).then_inc(n2_tr, 1)

            def tables(t, s):
                pe.wait_ge(n2_cp, t + 2)
                for i, (l, r) in enumerate(((hts, "u011"), (ats, "u101"))):
                    pe.wait_ge(n2_p, 2 * t + i + 1)
                    for h in range(2):
                        last = mm(PS[:, 1 + 2 * i + h, :], l[:, s, :], w[r][:, 512 * h:512 * (h + 1)])
                    last.then_inc(n2_t, 1)

            def turn4(t, e):
                c, h = divmod(e, 2)
                if h == 0 and c < 4:
                    pe.wait_ge(n2_z, 4 * t + c + 1)
                if h == 0 and c == 4:
                    pe.wait_ge(n2_g, 5 * t + 5)
                pe.wait_ge(n2_ev, 10 * t + e + 1)
                z = zout[:, c % 2, :] if c < 4 else gz[:, 0, :]
                for i in range(4):
                    last = turn(PS[:, 5 + h, P * i:P * i + P], z[:, 512 * h + P * i:512 * h + P * i + P])
                last.then_inc(n2_half, 1)

            def main4(t, e):
                pe.wait_ge(n2_ev, 10 * t + e + 3)
                wt, b0 = ("u000", 4 * e) if e < 8 else ("u110", 4 * (e - 8))
                for i in range(4):
                    last = mm(PS[:, 7, 0:64], zt[:, e % 2, P * i:P * i + P],
                              w[wt][:, 64 * (b0 + i):64 * (b0 + i + 1)], False, e == 9 and i == 3)
                last.then_inc(n2_main, 1)

            head(0, 0)
            tables(0, 0)
            with pe.Fori(0, UN) as u:
                for s in range(2):
                    t = 2 * u + s
                    pe.wait_ge(n2_y, t + 2)
                    mm(PS[:, 7, 0:64], hts[:, s, :], w["lu0"][:, :], True, False)
                    mm(PS[:, 7, 64:160], htv[:, s, :], w["lu1"][:, :], False, False)
                    turn4(t, 0)
                    for e in range(7):
                        turn4(t, e + 1)
                        main4(t, e)
                    main4(t, 7)
                    pe.wait_ge(n2_p, 2 * t + 3)
                    for i in range(32):
                        last = mm(by3(PS[:, 7, 64:160]), ident[:, :], prod[:, :, 32 * i:32 * i + 32], False, i == 31)
                    last.then_inc(n2_id, 1)
                    head(t + 1, 1 - s)
                    turn4(t, 8)
                    turn4(t, 9)
                    main4(t, 8)
                    main4(t, 9)
                    tables(t + 1, 1 - s)


N_LOADS = 26


def kernel(**inputs):
    import numpy as np
    import concourse.bacc as bacc
    from concourse.bass_utils import run_bass_kernel_spmd

    src, dst = np.asarray(inputs["src"]), np.asarray(inputs["dst"])
    x, attr = np.asarray(inputs["x"]), np.asarray(inputs["node_vec1"])
    ea, es = np.asarray(inputs["edge_attr_4"]), np.asarray(inputs["edge_attr_64"])

    def padded(a, n, value=0):
        return np.concatenate([a, np.full((n - a.shape[0],) + a.shape[1:], value, a.dtype)])

    src, dst = padded(src, E_PAD, N_NODES), padded(dst, E_PAD, N_NODES)
    ea, es = padded(ea, E_PAD), padded(es, E_PAD)
    n = ITEMS + 1
    p = np.arange(P)
    cols = np.stack([p, 2.0 ** (64 - p), 2.5 * 2.0 ** (64 - p), TRASH + p], 1).astype(np.float32)
    arrays = {
        "x_in": padded(x, N_PAD),
        "a_in": padded(attr, N_PAD).reshape(NODE_TILES, P).T,
        "dst_in": dst.reshape(n * EDGE_TILES, P).T,
        "dstrow_in": dst.reshape(n, ITEM),
        "src_in": src.reshape(n, EDGE_TILES, P).transpose(0, 2, 1),
        "srcrow_in": src.reshape(n, ITEM),
        "ea_in": ea.reshape(n, EDGE_TILES, P, 4).transpose(0, 2, 1, 3).reshape(n, P, EDGE_TILES * 4),
        "es_in": es.reshape(n, ITEM, es.shape[1]).transpose(0, 2, 1),
        "ident_in": np.eye(P, dtype=np.float32),
        "iota_in": np.tile(p.astype(np.float32), (P, 1)),
        "cols_in": cols,
        "win_in": np.tile(np.append(P * np.arange(NODE_TILES), 0).astype(np.float32), (P, 1)),
    }
    for name in ("L0_gnn_lin1_ws", "L0_gnn_lin1_wv", "L0_gnn_fc_w1", "L0_gnn_fc_w2", "L0_gnn_sc_ws", "L0_gnn_sc_wv",
                 "L0_gnn_lin2_ws", "L0_gnn_lin2_wv", "L1_gnn_wm000", "L1_gnn_wm011", "L1_gnn_wm101",
                 "L1_gnn_wm110", "L1_gnn_lm0", "L1_gnn_lm1", "L1_gnn_wu000", "L1_gnn_wu011", "L1_gnn_wu101",
                 "L1_gnn_wu110", "L1_gnn_lu0", "L1_gnn_lu1"):
        arrays[name] = np.asarray(inputs[name])
    arrays = {k: np.ascontiguousarray(v) for k, v in arrays.items()}

    nc = bacc.Bacc("TRN2", target_bir_lowering=False, num_devices=1)
    args = [nc.dram_tensor(k, v.shape, mybir.dt.from_np(v.dtype), kind="ExternalInput").ap()
            for k, v in arrays.items()]
    out = nc.dram_tensor("out", (N_PAD, D), mybir.dt.float32, kind="ExternalOutput").ap()
    build(nc, *args, out)
    r = run_bass_kernel_spmd(nc, [arrays], core_ids=[0])
    return r.results[0]["out"][:N_NODES]
```

```python
import concourse.bass as bass
from concourse import mybir
from contextlib import ExitStack

P = 128
N_NODES, N_EDGES = 3125, 53125
S_CH, V_CH = 64, 32
D = S_CH + 3 * V_CH
NODE_TILES = 2 * (-(-N_NODES // (2 * P)))
N_PAD = NODE_TILES * P
EDGE_TILES = 8
ITEM = EDGE_TILES * P
ITEMS = -(-N_EDGES // ITEM)
assert ITEMS % 2 == 0 and NODE_TILES % 2 == 0
E_PAD = (ITEMS + 1) * ITEM
V3 = 3 * V_CH
FC = 64
W_COLS = 2 * S_CH + 3 * V_CH
H0 = D + 2 * V_CH
X_COLS = 5 * 192
AGG = S_CH + 3 * V_CH + 3 * (S_CH + V_CH + 2 * V_CH)
G0 = S_CH + 3 * V_CH
GROUP = S_CH + 3 * V_CH
T1_COLS = 2 * D + V_CH + V3
MSG = D + V_CH
TABLES = 4
TRASH = N_PAD
T_PAD = N_PAD + P
EPS = 1e-5


def weights_into(w):
    r = lambda n: float(n) ** -0.5
    f96 = r(S_CH + V_CH)
    return [
        (w["l0s"][:, :], r(S_CH)), (w["l0v"][:, :], r(V_CH)), (w["fc2"][:, :], r(FC)),
        (w["l2s"][0:S_CH, :], r(96) / 4), (w["l2s"][S_CH:96, :], r(96) * r(3) / 4),
        (w["l2v"][0:96, :], r(128) / 4), (w["l2v"][96:128, :], r(128) * r(2) / 4),
        (w["r1s"][:, 0:64], f96), (w["r1s"][:, 64:128], r(S_CH)), (w["r1s"][:, 128:160], f96),
        (w["r1v"][:, 0:V3], f96), (w["r1v"][:, V3:2 * V3], r(V_CH)),
        (w["wa"][S_CH:96, :], f96 * r(3)),
        (w["u000"][:, :], r(5120)), (w["u110"][:, :], r(5120) * r(3)),
        (w["u011"][:, :], r(4096)), (w["u101"][:, :], r(4096)),
        (w["lu0"][:, :], r(S_CH)), (w["lu1"][:, :], r(V_CH)),
    ]


def build(nc, x_in, a_in, dst_in, dstrow_in, src_in, srcrow_in, ea_in, es_in, ident_in, iota_in,
          cols_in, win_in, lin1_ws, lin1_wv, fc_w1, fc_w2, sc_ws, sc_wv, lin2_ws, lin2_wv,
          wm000, wm011, wm101, wm110, lm0, lm1, wu000, wu011, wu101, wu110, lu0, lu1, out):
    f32, i32 = mybir.dt.float32, mybir.dt.int32
    ALU, ACT, AX = mybir.AluOpType, mybir.ActivationFunctionType, mybir.AxisListType
    ds = bass.ds
    UN = NODE_TILES // 2

    ctx = ExitStack()
    with ctx:
        def sb(name, shape, dt=f32):
            return ctx.enter_context(nc.sbuf_tensor(name, shape, dt))

        def sem(name):
            return ctx.enter_context(nc.semaphore(name))

        def two(name):
            return [sem(f"{name}{s}") for s in range(2)]

        h0_tab = nc.dram_tensor("h0_tab", [N_PAD, H0], f32, kind="Internal").ap()
        agg0 = nc.dram_tensor("agg0", [N_PAD, AGG], f32, kind="Internal").ap()
        t1_tab = nc.dram_tensor("t1_tab", [N_PAD, T1_COLS], f32, kind="Internal").ap()
        agg1 = [nc.dram_tensor(f"agg1_{k}", [T_PAD, MSG], f32, kind="Internal").ap() for k in range(TABLES)]

        ident = sb("ident", [P, P])
        iota = sb("iota", [P, P])
        cols = sb("cols", [P, 4])
        win = sb("win", [P, NODE_TILES + 1])
        ones = sb("ones", [P, P])
        zero = sb("zero", [P, NODE_TILES * AGG // 8])
        w = {"l0s": sb("w_l0s", [64, 96 + 64]), "l0v": sb("w_l0v", [96, 160 + V3]),
             "fc1": sb("w_fc1", [P, P]), "fc2": sb("w_fc2", [P, W_COLS]),
             "l2s": sb("w_l2s", [96, 96]), "l2v": sb("w_l2v", [128, 32]),
             "r1s": sb("w_r1s", [64, 160]), "r1v": sb("w_r1v", [96, 2 * V3]),
             "wa": sb("w_wa", [96, 64]), "u000": sb("w_u000", [P, 32 * 64]),
             "u110": sb("w_u110", [P, 8 * 64]), "u011": sb("w_u011", [64, 1024]),
             "u101": sb("w_u101", [64, 1024]), "lu0": sb("w_lu0", [64, 64]), "lu1": sb("w_lu1", [96, 96])}

        X = sb("X", [P, (NODE_TILES + 1) * D])
        X1 = sb("X1", [P, (NODE_TILES + 1) * D])
        Y0 = sb("Y0", [P, NODE_TILES * 2 * V3])
        A1 = Y0[:, 0:(NODE_TILES + 1) * D]
        attr = sb("attr", [P, NODE_TILES])
        dsti = sb("dsti", [P, (ITEMS + 1) * EDGE_TILES], i32)
        dstf = sb("dstf", [P, (ITEMS + 1) * EDGE_TILES])
        basef = sb("basef", [P, ITEMS + 1])
        rel_all = sb("rel_all", [P, (ITEMS + 1) * EDGE_TILES])
        out_of = sb("out_of", [P, (ITEMS + 1) * EDGE_TILES])
        far = sb("far", [P, 1])
        flag = sb("flag", [1, 1], i32)
        total = sb("total", [P, NODE_TILES])
        negmean = sb("negmean", [P, NODE_TILES])
        squares = sb("squares", [P, NODE_TILES])
        vareps = sb("vareps", [P, NODE_TILES])
        std = sb("std", [P, NODE_TILES])
        rstd = [sb(f"rstd{l}", [P, NODE_TILES + 1]) for l in range(2)]
        shift = [sb(f"shift{l}", [P, NODE_TILES + 1]) for l in range(2)]

        hs = sb("hs", [P, 2, D])
        hts = sb("hts", [64, 2, P])
        htv = sb("htv", [96, 2, P])
        h0s = sb("h0s", [P, 2, H0])
        aggt = sb("aggt", [P, 2, AGG])
        mid = sb("mid", [P, 2, 96 + 3 * P])
        midts = sb("midts", [96, 2, P])
        midtv = sb("midtv", [P, 2, 3 * P])
        t1s = sb("t1s", [P, 2, T1_COLS])
        tabs = sb("tabs", [P, 2, TABLES, MSG])
        half = sb("half", [P, 2, 2, MSG])
        mt = sb("mt", [P, 2, 96])
        mtt = sb("mtt", [96, 2, P])
        a_s = sb("a_s", [P, 2, D])
        ats = sb("ats", [64, 2, P])
        sum1 = sb("sum1", [P, V3])
        sum2 = sb("sum2", [P, V3])
        acc = sb("acc", [P, 2, D])
        ys = sb("ys", [P, 2, D])
        yt = sb("yt", [P, V3])

        arena = sb("arena", [P, 14592])

        def carve(*shapes):
            at, views = 0, []
            for shape in shapes:
                n = 1
                for d in shape[1:]:
                    n *= d
                v = arena[0:shape[0], at:at + n]
                names = "abcd"[:len(shape) - 1]
                views.append(v.rearrange(f"p ({' '.join(names)}) -> p {' '.join(names)}",
                                         **dict(zip(names, shape[1:]))) if len(names) > 1 else v)
                at += n
            assert at <= 14592
            return views

        srci = sb("srci", [P, 2, EDGE_TILES], i32)
        ea = sb("ea", [P, 2, EDGE_TILES, 4])
        est, hid, gath, sel, xw, aggs = carve(
            [P, 2, ITEM // 2], [P, 2, ITEM // 2], [P, 2, EDGE_TILES, H0], [P, 4, 4, P], [P, 4, X_COLS],
            [P, 2, AGG])
        rel = sb("rel", [P, 2, EDGE_TILES])
        dstrow, srcrow, t1w, pick, same, msg, tz, tx, outm = carve(
            [P, 2, ITEM], [P, 2, ITEM], [P, 2, T1_COLS], [P, 2, ITEM], [P, 2, ITEM], [P, 4, 2, MSG + 1],
            [P, 2, 2, 3 * V_CH], [P, 2, 2, 3 * V_CH], [P, 2, EDGE_TILES, MSG + 1])
        dstrow, srcrow = dstrow.bitcast(i32), srcrow.bitcast(i32)
        tz = tz.rearrange("p q i (k c) -> p q i k c", k=3)
        tx = tx.rearrange("p q i (k c) -> p q i k c", k=3)
        centered, sig = carve([P, NODE_TILES * D], [P, NODE_TILES, 96])
        prod, prod2, gz, gsum, zout, zt = carve(
            [P, 3, 1024], [P, 3, 1024], [P, 3, 1024], [P, 2, 1024], [P, 2, 1024], [P, 2, 512])
        srcf = sb("srcf", [P, 2, EDGE_TILES])
        nodeid = sb("nodeid", [P, 2])
        src_kept = sb("src_kept", [P, 2, EDGE_TILES])
        away = sb("away", [P, 2, EDGE_TILES])
        moved = sb("moved", [P, EDGE_TILES])
        scidx = sb("scidx", [P, 2, EDGE_TILES], i32)

        PS = ctx.enter_context(nc.psum_tensor("PS", [P, 8, 512], f32))

        loaded_x = sem("loaded_x")
        loaded_n = sem("loaded_n")
        loaded = sem("loaded")
        loaded_late = sem("loaded_late")
        zeroed = sem("zeroed")
        weighted = sem("weighted")
        scaled = sem("scaled")
        cleared = sem("cleared")
        cleared1 = sem("cleared1")
        setup = sem("setup")
        base_mm = sem("base_mm")
        far_mm = sem("far_mm")
        flag_ready = sem("flag_ready")
        centered_ready = sem("centered_ready")
        squared = sem("squared")
        eps_ready = sem("eps_ready")
        std_ready = sem("std_ready")
        norm_ready = sem("norm_ready")
        n0_h, n0_tr, n0_cp, n0_mm, n0_out = (sem(f"n0_{k}") for k in ("h", "tr", "cp", "mm", "out"))
        n0_stored = two("n0_stored")
        l0_loaded = two("l0_loaded")
        gathered = [[sem(f"gathered{s}_{j}") for j in range(EDGE_TILES)] for s in range(2)]
        rel_ready = sem("rel_ready")
        hid_mm, hid_ready, w_done, x_ready, scat_done, agg_evac = (
            sem(k) for k in ("hid_mm", "hid_ready", "w_done", "x_ready", "scat_done", "agg_evac"))
        agg_added = two("agg_added")
        l0_done = sem("l0_done")
        n1_loaded = two("n1_loaded")
        n1_copied, n1_mid, n1_tr, n1_cp, n1_mm, n1_y, n1_sig = (
            sem(f"n1_{k}") for k in ("copied", "mid", "tr", "cp", "mm", "y", "sig"))
        eps1_ready, std1_ready, norm1_ready = (
            sem(k) for k in ("eps1_ready", "std1_ready", "norm1_ready"))
        n1b_h, n1b_x, n1b_tr, n1b_cp, n1b_mm, n1b_out = (sem(f"n1b_{k}") for k in ("h", "x", "tr", "cp", "mm", "out"))
        n1b_stored = two("n1b_stored")
        l1_loaded = two("l1_loaded")
        l1_rows = two("l1_rows")
        same_ready = sem("same_ready")
        prep_a, pick_ready, idx_step, idx_ready = (
            sem(k) for k in ("prep_a", "pick_ready", "idx_step", "idx_ready"))
        gath_mm, u_ready, parts_ready, msg_ready, ded_done, out_ready = (
            sem(k) for k in ("gath_mm", "u_ready", "parts_ready", "msg_ready", "ded_done", "out_ready"))
        scattered = [two(f"scattered{k}_") for k in range(TABLES)]
        l1_done = sem("l1_done")
        n2_loaded = two("n2_loaded")
        n2a_half, n2a_sum, n2a_tr, n2a_cp, n2a_mm, n2a_out = (
            sem(f"n2a_{k}") for k in ("half", "sum", "tr", "cp", "mm", "out"))
        n2_h, n2_tr, n2_cp, n2_t, n2_p, n2_fold, n2_z, n2_half, n2_ev, n2_main, n2_g, n2_r, n2_acc, n2_yt, n2_y = (
            sem(f"n2_{k}") for k in ("h", "tr", "cp", "t", "p", "fold", "z", "half", "ev", "main",
                                     "g", "r", "acc", "yt", "y"))
        stored = two("stored")
        CREDITS = [(n0_tr, 2), (n0_cp, 2), (n0_mm, 2), (n0_out, 2),
                   (hid_mm, 2), (hid_ready, 2), (w_done, 16), (x_ready, 16), (scat_done, 4), (agg_evac, 2),
                   (n1_copied, 2), (n1_mid, 2), (n1_tr, 2), (n1_cp, 2), (n1_mm, 2), (n1_y, 2),
                   (n1b_x, 2), (n1b_tr, 2), (n1b_cp, 2), (n1b_mm, 2), (n1b_out, 2),
                   (gath_mm, 8), (parts_ready, 8), (msg_ready, 8), (ded_done, 8), (same_ready, 5), (out_ready, 2),
                   (n2a_half, 2), (n2a_tr, 2), (n2a_cp, 2), (n2a_mm, 2), (n2a_out, 2),
                   (n2_cp, 1), (n2_p, 4), (n2_r, 2), (n2_acc, 2), (n2_half, 10), (n2_ev, 2), (n2_main, 2), (n2_y, 2)]
        CREDITS += [(sm, 1) for pair in (n0_stored, n1b_stored, stored) for sm in pair]

        block = ctx.enter_context(nc.Block())

        def settle(eng):
            eng.nop(nofuse=True)

        def v3(ap):
            return ap.rearrange("p (c k) -> p k c", k=3)

        def rows(ap):
            return ap.rearrange("u o w -> u (o w)")

        def by3(ap):
            return ap.rearrange("p (k c) -> p k c", k=3)

        def next_two(ap):
            part, k, c = ap.ap
            return bass.AP(ap.tensor, ap.offset + k[0], [list(part), list(k), [k[0], 2], list(c)])

        SUM_0 = 512

        def clearing(table, part, parts):
            flat = table.rearrange("(p r) c -> p (r c)", p=P)
            width = flat.shape[1] // parts
            assert width * parts == flat.shape[1] and width <= zero.shape[1]
            return flat[:, part * width:(part + 1) * width], zero[:, 0:width]

        def half_of(ap, h):
            return ap[:, UN * D * h:UN * D * (h + 1)].rearrange("p (t d) -> p t d", d=D)

        def items(eng, body, general):
            if not general:
                with eng.Fori(0, ITEMS // 2) as u:
                    for s in range(2):
                        body(u, s, 2 * u + s, None)
            else:
                with eng.Fori(0, ITEMS) as i:
                    with eng.Fori(0, NODE_TILES // 2) as q:
                        for s in range(2):
                            body(i * (NODE_TILES // 2) + q, s, i, 2 * q + s)

        def over_tiles(eng, *stages):
            furthest = max(lead for lead, _ in stages)
            for t in range(-furthest, 0):
                for lead, f in stages:
                    if t + lead >= 0:
                        f((t + lead) // 2, (t + lead) % 2)
            with eng.Fori(0, UN - 1) as u:
                for s in range(2):
                    for lead, f in stages:
                        f(u + (s + lead) // 2, (s + lead) % 2)
            for s in range(2):
                for lead, f in stages:
                    if s + lead < 2:
                        f(UN - 1, s + lead)

        def uses(general):
            return ITEMS * NODE_TILES if general else ITEMS

        def by_input(eng, part):
            eng.wait_ge(flag_ready, 1)
            bad = eng.value_load(flag[0:1, 0:1], min_val=0, max_val=E_PAD)
            with eng.If(bad < 1):
                part(False)
            with eng.Else():
                part(True)

        @block.sync
        def _(sp):
            for sm, n in CREDITS:
                sp.sem_inc(sm, n)
            sp.dma_start(X[:, 0:NODE_TILES * D].rearrange("p (t d) -> p t d", d=D),
                         x_in.rearrange("(t p) d -> p t d", p=P)).then_inc(loaded_x, 16)
            first = [(ident[:, :], ident_in), (attr[:, :], a_in),
                     (w["l0s"][:, 0:96], sc_ws), (w["l0s"][:, 96:160], lin1_ws)]
            assert len(first) == N_FIRST
            for dst, src in first:
                sp.dma_start(dst, src).then_inc(loaded_n, 16)
            sp.wait_ge(zeroed, 2)
            for k in range(3):
                r = slice(32 * k, 32 * k + 32)
                places = [(32 * k, lin1_wv), (160 + 32 * k, sc_wv)] + ([(V3 + 32 * k, lin1_wv)] if k < 2 else [])
                for c, src in places:
                    sp.dma_start(w["l0v"][r, c:c + 32], src).then_inc(loaded_n, 16)
            loads = [(dsti[:, :], dst_in), (iota[:, :], iota_in), (cols[:, :], cols_in), (win[:, :], win_in),
                     (w["fc1"][0:64, 0:64], fc_w1), (w["fc1"][64:128, 64:128], fc_w1)]
            for r in (slice(0, 64), slice(64, 128)):
                for c, c_in, n in ((0, 64, 64), (64, 0, 64), (128, 160, 32), (160, 128, 32), (192, 192, 32)):
                    loads.append((w["fc2"][r, c:c + n], fc_w2[:, c_in:c_in + n]))
            assert len(loads) == N_LOADS
            for dst, src in loads:
                sp.dma_start(dst, src).then_inc(loaded, 16)

            with sp.Fori(0, UN) as u:
                for s in range(2):
                    t = 2 * u + s
                    sp.wait_ge(n0_out, t + 3)
                    sp.dma_start(h0_tab[ds(t * P, P), :], h0s[:, s, :]).then_inc(n0_stored[s], 16)

            def load0(u, s, item, window):
                n = 2 * u + s
                sp.wait_ge(x_ready, 8 * n + 8)
                settle(sp)
                sp.wait_ge(hid_mm, n + 1)
                sp.dma_start(srci[:, s, :], src_in[ds(item, 1), :, :].rearrange("i p j -> (i p) j"))\
                    .then_inc(l0_loaded[s], 16)
                sp.dma_start(ea[:, s, :, :].rearrange("p j c -> p (j c)"),
                             ea_in[ds(item, 1), :, :].rearrange("i p j -> (i p) j")).then_inc(l0_loaded[s], 16)
                sp.dma_start(est[:, s, :], es_in[ds(item, 1), :, :].rearrange("i p j -> (i p) j"))\
                    .then_inc(l0_loaded[s], 16)

            def layer0(general):
                items(sp, load0, general)
                load0(uses(general) // 2, 0, ITEMS, None)
            by_input(sp, layer0)

            sp.wait_ge(l0_done, 1)
            with sp.Fori(0, UN) as u:
                for s in range(2):
                    t = 2 * u + s
                    sp.wait_ge(n1_copied, t + 1)
                    sp.wait_ge(n1_mid, t + 1)
                    sp.dma_start(aggt[:, s, :], agg0[ds(t * P, P), :]).then_inc(n1_loaded[s], 16)
            with sp.Fori(0, UN) as u:
                for s in range(2):
                    t = 2 * u + s
                    sp.wait_ge(n1b_x, t + 3)
                    sp.wait_ge(n1b_out, t + 3)
                    sp.dma_start(t1_tab[ds(t * P, P), :], t1s[:, s, :]).then_inc(n1b_stored[s], 16)
            for s in range(2):
                sp.wait_ge(n1b_stored[s], 16 * UN + 1)

            def load_rows(u, s, item):
                sp.wait_ge(same_ready, 8 * u + 4 * s + 1)
                sp.dma_start(srci[:, s, :], src_in[ds(item, 1), :, :].rearrange("i p j -> (i p) j"))\
                    .then_inc(l1_rows[s], 16)
                sp.dma_start(dstrow[:, s, :], dstrow_in[ds(item, 1), :].to_broadcast([P, ITEM]))\
                    .then_inc(l1_rows[s], 16)
                sp.dma_start(srcrow[:, s, :], srcrow_in[ds(item, 1), :].to_broadcast([P, ITEM]))\
                    .then_inc(l1_rows[s], 16)

            def load1(u, s, item, window):
                n = 2 * u + s
                sp.wait_ge(gath_mm, 4 * n + 4)
                sp.wait_ge(msg_ready, 4 * n + 4)
                if window is None:
                    base = sp.value_load(dsti[0:1, ds(item * EDGE_TILES, 1)], min_val=0, max_val=N_NODES)
                else:
                    base = window * P
                sp.dma_start(t1w[:, s, :], t1_tab[ds(base, P), :]).then_inc(l1_loaded[s], 16)
                sp.dma_start(ea[:, s, :, :].rearrange("p j c -> p (j c)"),
                             ea_in[ds(item, 1), :, :].rearrange("i p j -> (i p) j")).then_inc(l1_loaded[s], 16)

            def loads1(u, s, item, window):
                if window is None:
                    load1(u, s, item, None)
                    load_rows(u + s, 1 - s, item + 1)
                else:
                    load_rows(u, s, item)
                    load1(u, s, item, window)

            def layer1(general):
                end = uses(general) // 2
                if not general:
                    load_rows(0, 0, 0)
                items(sp, loads1, general)
                if general:
                    load_rows(end, 0, ITEMS)
                load1(end, 0, ITEMS, 0 if general else None)
            by_input(sp, layer1)

            sp.wait_ge(l1_done, 1)
            with sp.Fori(0, UN) as u:
                for s in range(2):
                    t = 2 * u + s
                    sp.wait_ge(n2a_half, t + 1)
                    for k in range(TABLES):
                        sp.dma_start(tabs[:, s, k, :], agg1[k][ds(t * P, P), :]).then_inc(n2_loaded[s], 16)
            with sp.Fori(0, UN) as u:
                for s in range(2):
                    t = 2 * u + s
                    sp.wait_ge(n2_y, t + 3)
                    sp.dma_start(out[ds(t * P, P), :], ys[:, s, :]).then_inc(stored[s], 16)
            for s in range(2):
                sp.wait_ge(stored[s], 16 * UN + 1)

        @block.gpsimd
        def _(pool):
            pool.memset(zero[:, :], 0.0).then_inc(zeroed, 1)
            pool.wait_ge(zeroed, 2)
            for s in range(2):
                pool.dma_start(*clearing(agg0, s, 8)).then_inc(agg_added[s], 16)
            pool.wait_ge(loaded_n, 16 * (N_FIRST + 8))
            for part in range(2, 8):
                pool.dma_start(*clearing(agg0, part, 8)).then_inc(cleared, 16)

            for s in range(2):
                pool.wait_ge(n0_stored[s], 16 * UN + 1)

            def gather0(u, s):
                n = 2 * u + s
                pool.wait_ge(l0_loaded[s], 48 * (u + 1))
                for j in range(EDGE_TILES):
                    pool.wait_ge(x_ready, 8 * n + j + 1)
                    settle(pool)
                    pool.indirect_dma_start(
                        out=gath[:, s, j, :], out_offset=None, in_=h0_tab,
                        in_offset=bass.IndirectOffsetOnAxis(ap=srci[:, s, j:j + 1], axis=0),
                    ).then_inc(gathered[s][j], 16)

            def item0(u, s, item, window):
                n = 2 * u + s
                gather0(u + s, 1 - s)
                if window is None:
                    base = pool.value_load(dsti[0:1, ds(item * EDGE_TILES, 1)], min_val=0, max_val=N_NODES)
                else:
                    base = window * P
                pool.wait_ge(agg_evac, n + 3)
                pool.wait_ge(agg_added[1 - s], 16 * (u + s) + 16)
                pool.dma_start(agg0[ds(base, P), :], aggs[:, s, :], accum_op=ALU.add).then_inc(agg_added[s], 16)

            def layer0(general):
                gather0(0, 0)
                pool.wait_ge(cleared, 16 * 6)
                for s in range(2):
                    pool.wait_ge(agg_added[s], 16)
                items(pool, item0, general)
                for s in range(2):
                    pool.wait_ge(agg_added[s], 8 * uses(general) + 16)
                for j in range(EDGE_TILES):
                    pool.wait_ge(gathered[0][j], 8 * uses(general) + 16)
                pool.sem_inc(l0_done, 1)
            by_input(pool, layer0)

            for turn in range(3):
                for s in range(2):
                    for k in range(TABLES):
                        if turn > 0:
                            pool.wait_ge(scattered[k][s], 16 * turn)
                        pool.dma_start(agg1[k][TRASH + 64 * s:TRASH + 64 * s + 64, :], zero[0:64, 0:MSG])\
                            .then_inc(scattered[k][s], 16)

            def item1(u, s, item, window):
                n = 2 * u + s
                pool.wait_ge(idx_ready, n + 2)
                for j in range(EDGE_TILES):
                    k = j % TABLES
                    if j < TABLES:
                        pool.wait_ge(scattered[k][1 - s], 32 * (u + s) + 48)
                    else:
                        pool.wait_ge(scattered[k][s], 32 * u + 64)
                    settle(pool)
                    pool.indirect_dma_start(
                        out=agg1[k], out_offset=bass.IndirectOffsetOnAxis(ap=scidx[:, s, j:j + 1], axis=0),
                        in_=outm[:, s, j, 0:MSG], in_offset=None, compute_op=ALU.add,
                    ).then_inc(scattered[k][s], 16)

            def layer1(general):
                pool.wait_ge(cleared1, 16 * TABLES * ITEMS // 2)
                for k in range(TABLES):
                    for s in range(2):
                        pool.wait_ge(scattered[k][s], 48)
                items(pool, item1, general)
                for k in range(TABLES):
                    for s in range(2):
                        pool.wait_ge(scattered[k][s], 16 * uses(general) + 48)
                pool.sem_inc(l1_done, 1)
            by_input(pool, layer1)

            with pool.Fori(0, UN) as uu:
                for s in range(2):
                    t = 2 * uu + s
                    pool.wait_ge(n2_h, t + 1)
                    pool.wait_ge(n2_half, 10 * t + 1)
                    for k in range(3):
                        lo = S_CH + 32 * k
                        pool.tensor_tensor(
                            gz[:, k, :].rearrange("p (u v) -> p u v", v=32),
                            hs[:, s, lo:lo + 32].unsqueeze(2).to_broadcast([P, 32, 32]),
                            a_s[:, s, lo:lo + 32].unsqueeze(1).to_broadcast([P, 32, 32]), ALU.mult)\
                            .then_inc(n2_g, 1)
                    pool.wait_ge(n2_g, 5 * t + 3)
                    pool.tensor_tensor(gz[:, 1, :], gz[:, 1, :], gz[:, 2, :], ALU.add).then_inc(n2_g, 1)
                    pool.wait_ge(n2_g, 5 * t + 4)
                    pool.tensor_tensor(gsum[:, s, :], gz[:, 0, :], gz[:, 1, :], ALU.add).then_inc(n2_g, 1)
                    for i, width in enumerate((512, 256)):
                        if i == 0:
                            pool.wait_ge(n2_p, 4 * t + 6)
                        else:
                            pool.wait_ge(n2_fold, 2 * t + 1)
                        pool.tensor_tensor(prod[:, :, 0:width], prod[:, :, 0:width], prod[:, :, width:2 * width],
                                           ALU.add).then_inc(n2_fold, 1)

        @block.scalar
        def _(act):
            def normed(x_tiles, layer, t, s):
                act.activation(hs[:, s, 0:S_CH], x_tiles[:, ds(t * D, S_CH)], ACT.Relu,
                               scale=rstd[layer][:, ds(t, 1)], bias=shift[layer][:, ds(t, 1)])
                return act.activation(by3(hs[:, s, S_CH:D]), v3(x_tiles[:, ds(t * D + S_CH, V3)]), ACT.Relu,
                                      scale=rstd[layer][:, ds(t, 1)], bias=shift[layer][:, ds(t, 1)])

            def square(layer):
                for h in range(2):
                    act.wait_ge(centered_ready, 2 * layer + h + 1)
                    act.activation(half_of(centered, h), half_of(centered, h), ACT.Square).then_inc(squared, 1)

            square(0)
            act.wait_ge(loaded_n, 16 * (N_FIRST + 8))
            act.wait_ge(eps_ready, 1)
            act.activation(std[:, :], vareps[:, :], ACT.Sqrt).then_inc(std_ready, 1)
            act.wait_ge(norm_ready, 1)

            def head0(u, s):
                t = 2 * u + s
                act.wait_ge(n0_tr, t + 1)
                normed(X, 0, t, s).then_inc(n0_h, 1)

            over_tiles(act, (0, head0))

            act.wait_ge(zeroed, 2)
            loads = [
                (w["l2s"][:, :], lin2_ws), (w["l2v"][:, :], lin2_wv),
                (w["r1s"][:, 0:64], rows(wm000)), (w["r1s"][:, 64:128], lm0), (w["r1s"][:, 128:160], rows(wm011)),
                (w["wa"][0:64, :], ident_in[0:64, 0:64]), (w["wa"][64:96, :], rows(wm110)),
                (w["u000"][:, :].rearrange("p (b w) -> p b w", w=64),
                 wu000.rearrange("(b i) v w -> (i v) b w", i=2)),
                (w["u110"][:, :].rearrange("p (b w) -> p b w", w=64),
                 wu110.rearrange("(b i) v w -> (i v) b w", i=4)),
                (w["u011"][:, :], wu011.rearrange("u v w -> u (v w)")),
                (w["u101"][:, :].rearrange("v (u w) -> v u w", w=32), wu101.rearrange("u v w -> v u w")),
                (w["lu0"][:, :], lu0),
            ]
            for name, c0, src in (("r1v", 0, rows(wm101)), ("r1v", V3, lm1), ("lu1", 0, lu1)):
                for k in range(3):
                    loads.append((w[name][32 * k:32 * k + 32, c0 + 32 * k:c0 + 32 * k + 32], src))
            assert len(loads) == N_LATE
            for dst, src in loads:
                act.dma_start(dst, src).then_inc(loaded_late, 16)

            def clear1(u, s):
                for k in range(2 * s, 2 * s + 2):
                    flat = agg1[k][0:N_PAD, :].rearrange("(p r) c -> p (r c)", p=P)
                    act.dma_start(flat[:, ds(u * MSG, MSG)], zero[:, 0:MSG]).then_inc(cleared1, 16)

            def silu(u, s):
                n = 2 * u + s
                act.wait_ge(w_done, 8 * n + 8)
                act.wait_ge(hid_mm, n + 3)
                act.activation(hid[:, s, :], PS[:, 2 + s, :], ACT.Silu, scale=float(FC) ** -0.5)\
                    .then_inc(hid_ready, 1)

            def item0(u, s, item, window):
                n = 2 * u + s
                silu(u + s, 1 - s)
                if window is None:
                    clear1(u, s)
                act.wait_ge(scat_done, 8 * n + 12)
                act.wait_ge(agg_added[s], 16 * u + 16)
                sums = PS[:, 4 + 2 * s:6 + 2 * s, :].rearrange("p b c -> p (b c)")
                parts = sums[:, 0:3 * GROUP].rearrange("p (k g) -> p k g", k=3)
                groups = aggs[:, s, G0:AGG].rearrange("p (k g) -> p k g", k=3)
                act.activation(aggs[:, s, 0:64], sums[:, SUM_0 + 96:SUM_0 + 160], ACT.Copy)
                act.activation(by3(aggs[:, s, 64:G0]), parts[:, :, 64:96], ACT.Copy)
                act.activation(groups[:, :, 0:64], parts[:, :, 0:64], ACT.Copy)
                act.activation(groups[:, :, 64:96], by3(sums[:, SUM_0:SUM_0 + 96]), ACT.Copy)
                act.activation(groups[:, :, 96:160], parts[:, :, 96:160], ACT.Copy).then_inc(agg_evac, 1)

            assert ITEMS // 2 == N_PAD // P
            act.wait_ge(zeroed, 2)

            def layer0(general):
                if general:
                    with act.Fori(0, ITEMS // 2) as u:
                        for s in range(2):
                            clear1(u, s)
                silu(0, 0)
                items(act, item0, general)
            by_input(act, layer0)

            act.wait_ge(l0_done, 1)
            with act.Fori(0, UN) as u:
                for s in range(2):
                    t = 2 * u + s
                    act.wait_ge(n1_loaded[s], 16 * (u + 1))
                    act.wait_ge(n1_tr, t + 1)
                    act.activation(mid[:, s, 0:64], aggt[:, s, 0:64], ACT.Copy)
                    act.activation(mid[:, s, 96:].rearrange("p (k g) -> p k g", k=3)[:, :, 0:96],
                                   aggt[:, s, G0:AGG].rearrange("p (k g) -> p k g", k=3)[:, :, 0:96],
                                   ACT.Copy).then_inc(n1_copied, 1)
            act.wait_ge(n1_y, NODE_TILES + 2)
            act.activation(sig[:, :, :], Y0[:, :].rearrange("p (t d) -> p t d", t=NODE_TILES)[:, :, 0:96],
                           ACT.Sigmoid).then_inc(n1_sig, 1)
            square(1)
            act.wait_ge(eps1_ready, 1)
            act.activation(std[:, :], vareps[:, :], ACT.Sqrt).then_inc(std1_ready, 1)
            act.wait_ge(norm1_ready, 1)

            def head1(u, s):
                t = 2 * u + s
                act.wait_ge(n1b_tr, t + 1)
                act.wait_ge(n1b_x, t + 1)
                normed(X1, 1, t, s).then_inc(n1b_h, 1)

            def own_vectors(u, s):
                t = 2 * u + s
                act.wait_ge(n1b_stored[s], 16 * u + 1)
                act.wait_ge(n1b_h, t + 1)
                act.activation(t1s[:, s, 2 * D + 32:T1_COLS], hs[:, s, S_CH:D], ACT.Copy).then_inc(n1b_x, 1)

            def projected(u, s):
                act.wait_ge(n1b_mm, 2 * u + s + 3)
                uv = t1s[:, s, 0:2 * D].rearrange("p (g d) -> p g d", g=2)
                act.activation(uv[:, :, 0:V3], PS[:, 2 + s, 160:352].rearrange("p (g d) -> p g d", g=2), ACT.Copy)
                act.activation(uv[:, :, V3:D], PS[:, 2 + s, 0:128].rearrange("p (g d) -> p g d", g=2), ACT.Copy)
                act.activation(t1s[:, s, 2 * D:2 * D + 32], PS[:, 2 + s, 128:160], ACT.Copy).then_inc(n1b_out, 1)

            over_tiles(act, (0, own_vectors), (2, head1), (0, projected))

            def scaled_u(u, s, m):
                q = m % 2
                pair = 8 * u + 4 * s + m
                act.wait_ge(gath_mm, pair + 9)
                act.wait_ge(ded_done, pair + 5)
                for i in range(2):
                    last = act.activation(msg[:, m, i, 0:D], PS[:, 2 * q + i, 0:D], ACT.Copy,
                                          scale=ea[:, s, 2 * m + i, 3:4])
                last.then_inc(u_ready, 1)

            def item1(u, s, item, window):
                for m in range(4):
                    pair = 8 * u + 4 * s + m
                    if m < 2:
                        scaled_u(u, s, m + 2)
                    else:
                        scaled_u(u + s, 1 - s, m - 2)
                    act.wait_ge(ded_done, pair + 9)
                    if m == 0:
                        for k in range(TABLES):
                            act.wait_ge(scattered[k][s], 32 * u + 48)
                    act.activation(outm[:, s, 2 * m:2 * m + 2, :],
                                   PS[:, 4 + m % 2, 0:2 * (MSG + 1)].rearrange("p (i d) -> p i d", i=2),
                                   ACT.Copy).then_inc(out_ready, 1)

            def layer1(general):
                scaled_u(0, 0, 0)
                scaled_u(0, 0, 1)
                items(act, item1, general)
            by_input(act, layer1)

            act.wait_ge(l1_done, 1)
            with act.Fori(0, UN) as u:
                for s in range(2):
                    t = 2 * u + s
                    act.wait_ge(n2a_mm, t + 3)
                    act.activation(A1[:, ds(t * D, S_CH)], PS[:, 2 + s, 0:64], ACT.Copy).then_inc(n2a_out, 1)

            def head(t, s):
                act.wait_ge(n2_y, t + 1)
                act.activation(a_s[:, s, :], A1[:, ds(t * D, D)], ACT.Copy)
                normed(X1, 1, t, s).then_inc(n2_h, 1)

            def copies(t, s):
                act.wait_ge(n2_tr, t + 1)
                act.activation(hts[:, s, :], PS[0:64, 0, 0:128], ACT.Copy)
                act.activation(htv[:, s, :], PS[0:96, 0, 128:256], ACT.Copy)
                act.activation(ats[:, s, :], PS[0:64, 0, 256:384], ACT.Copy).then_inc(n2_cp, 1)

            act.wait_ge(n2a_out, NODE_TILES + 2)
            head(0, 0)
            copies(0, 0)
            with act.Fori(0, UN) as u:
                for s in range(2):
                    t = 2 * u + s
                    for e in range(10):
                        if e == 4:
                            head(t + 1, 1 - s)
                        if e == 8:
                            copies(t + 1, 1 - s)
                        act.wait_ge(n2_half, 10 * t + e + 11)
                        act.wait_ge(n2_main, 10 * t + e + 1)
                        act.activation(zt[:, e % 2, :], PS[:, 5 + e % 2, :], ACT.Copy).then_inc(n2_ev, 1)
                    act.wait_ge(n2_main, 10 * t + 12)
                    act.activation(acc[:, s, :], PS[:, 7, 0:D], ACT.Copy).then_inc(n2_acc, 1)

        @block.vector
        def _(dve):
            steps = [0]

            def step(ins):
                steps[0] += 1
                ins.then_inc(setup, 1)
                dve.wait_ge(setup, steps[0])

            def tiles(ap):
                return ap[:, 0:NODE_TILES * D].rearrange("p (t d) -> p t d", d=D)

            def layernorm(x_tiles, layer, eps_sem, std_sem, norm_sem):
                step(dve.tensor_reduce(total[:, :], tiles(x_tiles), AX.X, ALU.add))
                step(dve.tensor_scalar(negmean[:, :], total[:, :], -1.0 / D, None, ALU.mult))
                for h in range(2):
                    mean = negmean[:, UN * h:UN * h + UN].unsqueeze(2).to_broadcast([P, UN, D])
                    dve.tensor_tensor(half_of(centered, h), half_of(x_tiles, h), mean, ALU.add)\
                        .then_inc(centered_ready, 1)
                for h in range(2):
                    dve.wait_ge(squared, 2 * layer + h + 1)
                    last = dve.tensor_reduce(squares[:, UN * h:UN * h + UN], half_of(centered, h), AX.X, ALU.add)
                step(last)
                dve.tensor_scalar(vareps[:, :], squares[:, :], 1.0 / D, EPS, ALU.mult, ALU.add).then_inc(eps_sem, 1)
                dve.wait_ge(std_sem, 1)
                step(dve.reciprocal(rstd[layer][:, 0:NODE_TILES], std[:, :]))
                dve.tensor_tensor(shift[layer][:, 0:NODE_TILES], negmean[:, :], rstd[layer][:, 0:NODE_TILES],
                                  ALU.mult).then_inc(norm_sem, 1)

            for name in ("l0v", "r1v", "fc1"):
                dve.memset(w[name][:, :], 0.0)
            dve.memset(w["lu1"][:, :], 0.0).then_inc(zeroed, 1)
            dve.memset(X[:, NODE_TILES * D:], 0.0)
            dve.memset(X1[:, NODE_TILES * D:], 0.0)
            for l in range(2):
                dve.memset(rstd[l][:, NODE_TILES:], 0.0)
                dve.memset(shift[l][:, NODE_TILES:], 0.0)
            step(dve.memset(ones[:, :], 1.0))
            dve.wait_ge(loaded_x, 16)
            layernorm(X, 0, eps_ready, std_ready, norm_ready)
            dve.wait_ge(loaded_n, 16 * (N_FIRST + 8))
            weights = weights_into(w)
            for ap, factor in weights[:2]:
                last = dve.tensor_scalar(ap, ap, factor, None, ALU.mult)
            last.then_inc(scaled, 1)

            def copies0(u, s):
                t = 2 * u + s
                dve.wait_ge(n0_tr, t + 3)
                dve.wait_ge(n0_mm, t + 1)
                dve.tensor_copy(hts[:, s, :], PS[0:64, s, 0:128])
                dve.tensor_copy(htv[:, s, :], PS[0:96, s, 128:256]).then_inc(n0_cp, 1)

            def projected0(u, s):
                t = 2 * u + s
                dve.wait_ge(n0_mm, t + 3)
                dve.wait_ge(n0_stored[s], 16 * u + 1)
                dve.tensor_scalar(h0s[:, s, :], PS[:, 2 + s, 96:320], attr[:, ds(t, 1)], None, ALU.mult)
                dve.tensor_scalar(Y0[:, ds(t * 2 * V3, 96)], PS[:, 2 + s, 0:96], attr[:, ds(t, 1)], None, ALU.mult)
                dve.tensor_scalar(Y0[:, ds(t * 2 * V3 + 96, 96)], PS[:, 2 + s, 320:416], attr[:, ds(t, 1)], None,
                                  ALU.mult).then_inc(n0_out, 1)

            over_tiles(dve, (1, copies0), (0, projected0))

            dve.wait_ge(loaded, 16 * N_LOADS)
            dve.tensor_copy(dstf[:, :], dsti[:, :]).then_inc(base_mm, 1)
            ap, factor = weights[2]
            dve.tensor_scalar(ap, ap, factor, None, ALU.mult).then_inc(scaled, 1)
            dve.wait_ge(base_mm, 2)
            step(dve.tensor_copy(basef[:, :], PS[:, 4, 0:ITEMS + 1]))
            step(dve.tensor_tensor(rel_all[:, :].rearrange("p (i j) -> p i j", j=EDGE_TILES),
                                   dstf[:, :].rearrange("p (i j) -> p i j", j=EDGE_TILES),
                                   basef[:, :].unsqueeze(2).to_broadcast([P, ITEMS + 1, EDGE_TILES]), ALU.subtract))
            step(dve.tensor_scalar(out_of[:, :], rel_all[:, :], 0.0, None, ALU.is_lt))
            step(dve.scalar_tensor_tensor(out=out_of[:, :], in0=rel_all[:, :], scalar=float(P - 1),
                                          in1=out_of[:, :], op0=ALU.is_gt, op1=ALU.add))
            step(dve.tensor_reduce(far[:, :], out_of[:, :], AX.X, ALU.add))
            dve.sem_inc(far_mm, 1)
            dve.wait_ge(far_mm, 2)
            dve.tensor_copy(flag[0:1, 0:1], PS[0:1, 5, 0:1]).then_inc(flag_ready, 1)

            def item0(u, s, item, window):
                n = 2 * u + s
                dve.wait_ge(l0_loaded[s], 48 * (u + 1))
                base = basef[:, ds(item, 1)] if window is None else win[:, ds(window, 1)]
                dve.tensor_scalar(rel[:, s, :], dstf[:, ds(item * EDGE_TILES, EDGE_TILES)], base, None,
                                  ALU.subtract).then_inc(rel_ready, 1)
                dve.wait_ge(rel_ready, n + 1)
                for m in range(EDGE_TILES // 2):
                    j, b = 2 * m, 2 * (m % 2)
                    tile = 8 * n + j
                    dve.wait_ge(scat_done, tile + 2)
                    for i in range(2):
                        dve.scalar_tensor_tensor(
                            out=sel[:, b + i, :, :], in0=iota[:, :].unsqueeze(1).to_broadcast([P, 4, P]),
                            scalar=rel[:, s, j + i:j + i + 1],
                            in1=ea[:, s, j + i, :].unsqueeze(2).to_broadcast([P, 4, P]),
                            op0=ALU.is_equal, op1=ALU.mult)
                    dve.wait_ge(w_done, tile + 18)
                    for i in range(2):
                        dve.wait_ge(gathered[s][j + i], 16 * (u + 1))
                    wt = PS[:, m % 2, 0:2 * W_COLS].rearrange("p (t w) -> p t w", t=2)
                    x = xw[:, b:b + 2, :].rearrange("p t (k c) -> p t k c", k=5)
                    sc = gath[:, s, j:j + 2, 0:64]
                    dve.tensor_tensor(x[:, :, 0:3, 0:64], wt[:, :, 0:64].unsqueeze(2).to_broadcast([P, 2, 3, 64]),
                                      sc.unsqueeze(2).to_broadcast([P, 2, 3, 64]), ALU.mult)
                    dve.tensor_tensor(x[:, :, 3:5, 160:192], wt[:, :, 64:128].rearrange("p t (i c) -> p t i c", i=2),
                                      sc.rearrange("p t (i c) -> p t i c", i=2), ALU.mult)
                    for i in range(2):
                        v = by3(gath[:, s, j + i, 64:160])
                        dve.tensor_tensor(
                            x[:, i, 0:3, 64:192].rearrange("p k (m c) -> p m k c", m=4)[:, 0:4:3, :, :],
                            wt[:, i, 128:192].rearrange("p (m c) -> p m c", m=2).unsqueeze(2)
                            .to_broadcast([P, 2, 3, V_CH]),
                            v.unsqueeze(1).to_broadcast([P, 2, 3, V_CH]), ALU.mult)
                        dve.tensor_tensor(
                            x[:, i, 0:3, 96:160].rearrange("p k (m c) -> p k m c", m=2),
                            wt[:, i, 192:224].unsqueeze(1).unsqueeze(1).to_broadcast([P, 3, 2, V_CH]),
                            next_two(v), ALU.mult).then_inc(x_ready, 1)

            by_input(dve, lambda general: items(dve, item0, general))

            def mids(u, s):
                t = 2 * u + s
                dve.wait_ge(n1_loaded[s], 16 * (u + 1))
                dve.wait_ge(n1_tr, t + 1)
                q = lambda g, i: aggt[:, s, G0 + GROUP * g + 96 + 32 * i:G0 + GROUP * g + 128 + 32 * i]
                for k in range(3):
                    dve.tensor_tensor(mid[:, s, 96 + P * k + 96:96 + P * k + P], q((k + 2) % 3, 1),
                                      q((k + 1) % 3, 0), ALU.subtract)
                dve.tensor_reduce(mid[:, s, 64:96], aggt[:, s, 64:G0].rearrange("p (k c) -> p c k", k=3),
                                  AX.X, ALU.add).then_inc(n1_mid, 1)

            def copies1(u, s):
                t = 2 * u + s
                dve.wait_ge(n1_tr, t + 3)
                dve.wait_ge(n1_mm, t + 1)
                dve.tensor_copy(midts[:, s, :], PS[0:96, s, 0:128])
                dve.tensor_copy(midtv[:, s, :], PS[:, 2 + s, 0:384]).then_inc(n1_cp, 1)

            def sums1(u, s):
                t = 2 * u + s
                dve.wait_ge(n1_mm, t + 3)
                dve.scalar_tensor_tensor(out=Y0[:, ds(t * 2 * V3, 2 * V3)], in0=PS[:, 4 + s, 0:192],
                                         scalar=attr[:, ds(t, 1)], in1=Y0[:, ds(t * 2 * V3, 2 * V3)],
                                         op0=ALU.mult, op1=ALU.add).then_inc(n1_y, 1)

            dve.wait_ge(loaded_late, 16 * N_LATE)
            for ap, factor in weights[3:]:
                last = dve.tensor_scalar(ap, ap, factor, None, ALU.mult)
            last.then_inc(weighted, 1)
            dve.wait_ge(weighted, 1)
            dve.tensor_tensor(w["lu0"][:, :], w["lu0"][:, :], ident[0:64, 0:64], ALU.add)
            dve.tensor_tensor(w["lu1"][:, :], w["lu1"][:, :], ident[0:96, 0:96], ALU.add).then_inc(scaled, 1)
            dve.wait_ge(l0_done, 1)
            over_tiles(dve, (1, copies1), (2, mids), (0, sums1))

            y = Y0[:, :].rearrange("p (t d) -> p t d", t=NODE_TILES)
            yv = y[:, :, 96:192].rearrange("p t (k c) -> p t k c", k=3)
            dve.wait_ge(n1_y, NODE_TILES + 2)
            dve.wait_ge(n1_sig, 1)
            dve.tensor_tensor(y[:, :, 0:64], y[:, :, 0:64], sig[:, :, 0:64], ALU.mult)
            step(dve.tensor_tensor(yv, yv, sig[:, :, 64:96].unsqueeze(2).to_broadcast([P, NODE_TILES, 3, V_CH]),
                                   ALU.mult))
            dve.tensor_tensor(tiles(X1)[:, :, 0:64], tiles(X)[:, :, 0:64], y[:, :, 0:64], ALU.add)
            step(dve.tensor_tensor(tiles(X1)[:, :, 64:D].rearrange("p t (c k) -> p t k c", k=3),
                                   tiles(X)[:, :, 64:D].rearrange("p t (c k) -> p t k c", k=3), yv, ALU.add))
            layernorm(X1, 1, eps1_ready, std1_ready, norm1_ready)
            dve.memset(A1[:, NODE_TILES * D:], 0.0)
            def copies1b(u, s):
                t = 2 * u + s
                dve.wait_ge(n1b_tr, t + 3)
                dve.wait_ge(n1b_mm, t + 1)
                dve.tensor_copy(hts[:, s, :], PS[0:64, s, 0:128])
                dve.tensor_copy(htv[:, s, :], PS[0:96, s, 128:256]).then_inc(n1b_cp, 1)

            over_tiles(dve, (0, copies1b))

            def base_of(item, window):
                return basef[:, ds(item, 1)] if window is None else win[:, ds(window, 1)]

            def prepare_ids(u, s, base):
                dve.wait_ge(l1_rows[s], 48 * (u + 1))
                dve.tensor_copy(srcf[:, s, :], srci[:, s, :])
                dve.tensor_tensor(nodeid[:, s:s + 1], base, cols[:, 0:1], ALU.add).then_inc(prep_a, 1)

            def prepare_pick(u, s):
                n = 2 * u + s
                dve.wait_ge(prep_a, n + 1)
                dve.wait_ge(gath_mm, 4 * n + 4)
                dve.tensor_scalar(away[:, s, :], srcf[:, s, :], -1.0, cols[:, 3:4], ALU.mult, ALU.add)
                dve.tensor_copy(src_kept[:, s, :], srcf[:, s, :])
                dve.tensor_scalar(pick[:, s, :], dstrow[:, s, :], nodeid[:, s:s + 1], None, ALU.is_equal)\
                    .then_inc(pick_ready, 1)

            def prepare_same(u, s, m):
                j = 2 * m
                dve.wait_ge(ded_done, 8 * u + 4 * s + m + 1)
                dve.tensor_tensor(same[:, s, j * P:(j + 2) * P].rearrange("p (j f) -> p j f", j=2),
                                  srcrow[:, s, j * P:(j + 2) * P].rearrange("p (j f) -> p j f", j=2),
                                  srcf[:, s, j:j + 2].unsqueeze(2).to_broadcast([P, 2, P]), ALU.is_equal)\
                    .then_inc(same_ready, 1)

            def indices(u, s):
                n = 2 * u + s
                dve.wait_ge(pick_ready, n + 1)
                dve.wait_ge(out_ready, 4 * n + 2)
                for k in range(TABLES):
                    dve.wait_ge(scattered[k][1 - s], 32 * (u + s) + 16)
                dve.scalar_tensor_tensor(out=moved[:, :], in0=outm[:, 1 - s, :, MSG], scalar=cols[:, 2:3],
                                         in1=away[:, 1 - s, :], op0=ALU.is_gt, op1=ALU.mult).then_inc(idx_step, 1)
                dve.wait_ge(idx_step, n + 1)
                dve.tensor_tensor(scidx[:, 1 - s, :], moved[:, :], src_kept[:, 1 - s, :], ALU.add)\
                    .then_inc(idx_ready, 1)

            def item1(u, s, item, window):
                for m in range(4):
                    q = m % 2
                    pair = 8 * u + 4 * s + m
                    e = ea[:, s, 2 * m:2 * m + 2, :]
                    g = PS[:, 2 * q:2 * q + 2, :]
                    ek = e[:, :, 0:3].unsqueeze(3).to_broadcast([P, 2, 3, V_CH])
                    if m == 0:
                        dve.wait_ge(l1_loaded[s], 32 * (u + 1))
                    dve.wait_ge(u_ready, pair + 1)
                    dve.tensor_tensor(tx[:, q, :, :, :], g[:, :, 352:448].rearrange("p i (k c) -> p i k c", k=3), ek,
                                      ALU.mult)
                    dve.tensor_tensor(tz[:, q, :, :, :],
                                      g[:, :, 320:352].unsqueeze(2).to_broadcast([P, 2, 3, V_CH]), ek, ALU.mult)
                    dve.tensor_tensor(msg[:, m, :, 0:D], g[:, :, D:2 * D], msg[:, m, :, 0:D], ALU.add)\
                        .then_inc(parts_ready, 1)
                    dve.wait_ge(parts_ready, pair + 9)
                    dve.tensor_reduce(msg[:, m, :, D:MSG], tx[:, q, :, :, :].rearrange("p i k c -> p i c k"),
                                      AX.X, ALU.add)
                    dve.tensor_tensor(msg[:, m, :, 0:V3].rearrange("p i (k c) -> p i k c", k=3),
                                      msg[:, m, :, 0:V3].rearrange("p i (k c) -> p i k c", k=3),
                                      tz[:, q, :, :, :], ALU.add).then_inc(msg_ready, 1)
                    if m == 0:
                        prepare_same(u, s, 3)
                        prepare_ids(u + s, 1 - s, base_of(item + 1, None if window is None else window + 1))
                    elif m == 1:
                        indices(u, s)
                        dve.wait_ge(idx_ready, 2 * u + s + 1)
                        prepare_pick(u + s, 1 - s)
                    elif m == 2:
                        prepare_same(u + s, 1 - s, 0)
                        prepare_same(u + s, 1 - s, 1)
                    else:
                        prepare_same(u + s, 1 - s, 2)

            def layer1(general):
                for k in range(TABLES):
                    for s in range(2):
                        dve.wait_ge(scattered[k][s], 48)
                dve.memset(outm[:, 1, :, MSG], 0.0)
                dve.memset(away[:, 1, :], 0.0)
                dve.memset(src_kept[:, 1, :], 0.0)
                dve.tensor_copy(msg[:, :, :, MSG], cols[:, 1:2].unsqueeze(2).to_broadcast([P, 4, 2]))
                prepare_ids(0, 0, base_of(0, 0 if general else None))
                prepare_pick(0, 0)
                for m in range(3):
                    prepare_same(0, 0, m)
                items(dve, item1, general)
                indices(uses(general) // 2, 0)
            by_input(dve, layer1)

            dve.wait_ge(l1_done, 1)
            def sums2(u, s):
                t = 2 * u + s
                dve.wait_ge(n2_loaded[s], 16 * TABLES * (u + 1))
                dve.tensor_tensor(half[:, s, :, :], tabs[:, s, 0:2, :], tabs[:, s, 2:4, :], ALU.add)\
                    .then_inc(n2a_half, 1)
                dve.wait_ge(n2a_half, t + 3)
                dve.wait_ge(n2a_tr, t + 1)
                dve.tensor_tensor(A1[:, ds(t * D + S_CH, V3)], half[:, s, 0, 0:V3], half[:, s, 1, 0:V3], ALU.add)
                dve.tensor_tensor(mt[:, s, :], half[:, s, 0, V3:MSG], half[:, s, 1, V3:MSG], ALU.add)\
                    .then_inc(n2a_sum, 1)

            def copies2(u, s):
                t = 2 * u + s
                dve.wait_ge(n2a_tr, t + 3)
                dve.wait_ge(n2a_mm, t + 1)
                dve.tensor_copy(mtt[:, s, :], PS[0:96, s, 0:128]).then_inc(n2a_cp, 1)

            over_tiles(dve, (1, copies2), (2, sums2))

            def times(out_ap, half, first_bank, by):
                i0 = 16 * half
                return dve.tensor_tensor(
                    out_ap[:, :, 512 * half:512 * half + 512].rearrange("p k (i w) -> p k i w", w=32),
                    PS[:, first_bank + half, :].rearrange("p (i w) -> p i w", w=32).unsqueeze(1)
                    .to_broadcast([P, 3, 16, 32]),
                    by3(by)[:, :, i0:i0 + 16].unsqueeze(3).to_broadcast([P, 3, 16, 32]), ALU.mult).then_inc(n2_p, 1)

            def outer(t, s, c):
                dve.wait_ge(n2_h, t + 1)
                dve.wait_ge(n2_half, 10 * t + 2 * c + (8 if c >= 2 else 6))
                dve.tensor_tensor(zout[:, c % 2, :].rearrange("p (u v) -> p u v", v=64),
                                  hs[:, s, 16 * c:16 * c + 16].unsqueeze(2).to_broadcast([P, 16, 64]),
                                  a_s[:, s, 0:64].unsqueeze(1).to_broadcast([P, 16, 64]), ALU.mult)\
                    .then_inc(n2_z, 1)

            for c in range(2):
                outer(0, 0, c)
            def products_begin(u, s):
                t = 2 * u + s
                dve.wait_ge(n2_t, 2 * t + 1)
                dve.wait_ge(n2_r, 2 * t + 2)
                times(prod, 0, 1, a_s[:, s, 64:160])

            def products_end(u, s):
                t = 2 * u + s
                outer(t, s, 2)
                times(prod, 1, 1, a_s[:, s, 64:160])
                outer(t, s, 3)
                dve.wait_ge(n2_t, 2 * t + 2)
                times(prod2, 0, 3, hs[:, s, 64:160])
                times(prod2, 1, 3, hs[:, s, 64:160])
                dve.wait_ge(n2_p, 4 * t + 8)
                dve.tensor_reduce(by3(sum2[:, :]), prod2[:, :, :].rearrange("p k (i w) -> p k w i", w=32),
                                  AX.X, ALU.add).then_inc(n2_r, 1)
                for c in range(2):
                    outer(t + 1, 1 - s, c)
                dve.wait_ge(n2_fold, 2 * t + 2)
                dve.tensor_reduce(by3(sum1[:, :]), prod[:, :, 0:256].rearrange("p k (i w) -> p k w i", w=32),
                                  AX.X, ALU.add).then_inc(n2_r, 1)

            def result(u, s):
                t = 2 * u + s
                dve.wait_ge(n2_r, 2 * t + 4)
                dve.tensor_tensor(sum1[:, :], sum1[:, :], sum2[:, :], ALU.add).then_inc(n2_yt, 1)
                dve.wait_ge(n2_acc, t + 3)
                dve.wait_ge(stored[s], 16 * u + 1)
                dve.tensor_tensor(ys[:, s, 0:64], acc[:, s, 0:64], X1[:, ds(t * D, 64)], ALU.add)
                dve.wait_ge(n2_yt, 2 * t + 1)
                dve.tensor_tensor(yt[:, :], acc[:, s, 64:D], sum1[:, :], ALU.add).then_inc(n2_yt, 1)
                dve.wait_ge(n2_yt, 2 * t + 2)
                dve.tensor_tensor(v3(ys[:, s, 64:160]), by3(yt[:, :]), v3(X1[:, ds(t * D + 64, V3)]),
                                  ALU.add).then_inc(n2_y, 1)

            over_tiles(dve, (1, products_begin), (0, result), (1, products_end))

        @block.tensor
        def _(pe):
            def mm(o, l, r, start=True, stop=True):
                return pe.matmul(o, l, r, start=start, stop=stop, skip_group_check=True)

            def turn(o, src):
                return pe.transpose(o, src, ident[:, :])

            pe.wait_ge(scaled, 1)
            pe.wait_ge(loaded_n, 16 * (N_FIRST + 8))

            def turns0(u, s):
                t = 2 * u + s
                pe.wait_ge(n0_h, t + 1)
                pe.wait_ge(n0_cp, t + 1)
                turn(PS[0:96, s, 128:256], hs[:, s, 64:160])
                turn(PS[0:64, s, 0:128], hs[:, s, 0:64]).then_inc(n0_tr, 1)

            def project0(u, s):
                t = 2 * u + s
                pe.wait_ge(n0_cp, t + 3)
                pe.wait_ge(n0_out, t + 1)
                mm(PS[:, 2 + s, 0:160], hts[:, s, :], w["l0s"][:, :])
                mm(PS[:, 2 + s, 160:416], htv[:, s, :], w["l0v"][:, :]).then_inc(n0_mm, 1)

            over_tiles(pe, (0, project0), (2, turns0))

            pe.wait_ge(setup, 1)
            pe.wait_ge(base_mm, 1)
            mm(PS[:, 4, 0:ITEMS + 1], ones[0:1, :],
               dstf[0:1, :].rearrange("p (i j) -> p i j", j=EDGE_TILES)[:, :, 0]).then_inc(base_mm, 1)
            pe.wait_ge(far_mm, 1)
            mm(PS[0:1, 5, 0:1], far[:, :], ones[:, 0:1]).then_inc(far_mm, 1)
            pe.wait_ge(scaled, 2)
            pe.wait_ge(loaded, 16 * N_LOADS)
            pe.wait_ge(flag_ready, 1)

            def hidden(u, s):
                n = 2 * u + s
                pe.wait_ge(l0_loaded[s], 48 * (u + 1))
                pe.wait_ge(hid_ready, n + 1)
                mm(PS[:, 2 + s, :], w["fc1"][:, :], est[:, s, :]).then_inc(hid_mm, 1)

            def radial(u, s, j):
                n = 2 * u + s
                pe.wait_ge(x_ready, 8 * n + j + 14 - j % 2)
                if j == 0:
                    pe.wait_ge(hid_ready, n + 3)
                half = slice(64 * (j // 4), 64 * (j // 4) + 64)
                mm(PS[:, j // 2 % 2, W_COLS * (j % 2):W_COLS * (j % 2 + 1)],
                   hid[half, s, j % 4 * P:j % 4 * P + P], w["fc2"][half, :]).then_inc(w_done, 1)

            def item0(u, s, item, window):
                n = 2 * u + s
                sums = PS[:, 4 + 2 * s:6 + 2 * s, :].rearrange("p b c -> p (b c)")
                for j in range(EDGE_TILES):
                    b = j % 4
                    first, last = j == 0, j == EDGE_TILES - 1
                    if first:
                        pe.wait_ge(agg_evac, n + 1)
                    pe.wait_ge(x_ready, 8 * n + j + 17)
                    x = xw[:, b, :].rearrange("p (k c) -> p k c", k=5)
                    for k in range(3):
                        mm(sums[:, GROUP * k:GROUP * (k + 1)], sel[:, b, 1 + k, :], x[:, k, 0:GROUP],
                           first and k == 0, last)
                    done = mm(sums[:, SUM_0:SUM_0 + 160], sel[:, b, 0, :], x[:, :, 160:192], first, last)
                    done.then_inc(scat_done, 1)
                    for ahead in (j + 3, j + 4) if j % 2 else ():
                        if ahead < 8:
                            radial(u, s, ahead)
                        else:
                            radial(u + s, 1 - s, ahead - 8)
                    if j == 2:
                        hidden(u + s, 1 - s)

            def layer0(general):
                hidden(0, 0)
                for j in range(4):
                    radial(0, 0, j)
                items(pe, item0, general)
            by_input(pe, layer0)

            def turns1(u, s):
                t = 2 * u + s
                pe.wait_ge(n1_copied, t + 3)
                pe.wait_ge(n1_mid, t + 3)
                pe.wait_ge(n1_cp, t + 1)
                turn(PS[0:96, s, 0:128], mid[:, s, 0:96])
                for k in range(3):
                    last = turn(PS[:, 2 + s, P * k:P * k + P], mid[:, s, 96 + P * k:96 + P * k + P])
                last.then_inc(n1_tr, 1)

            def lin2(u, s):
                t = 2 * u + s
                pe.wait_ge(n1_cp, t + 3)
                pe.wait_ge(n1_y, t + 1)
                mm(PS[:, 4 + s, 0:96], midts[:, s, :], w["l2s"][:, :])
                for k in range(3):
                    last = mm(PS[:, 4 + s, 96 + 32 * k:128 + 32 * k], midtv[:, s, P * k:P * k + P], w["l2v"][:, :])
                last.then_inc(n1_mm, 1)

            pe.wait_ge(loaded_late, 16 * N_LATE)
            pe.wait_ge(scaled, 3)
            pe.wait_ge(l0_done, 1)
            over_tiles(pe, (0, lin2), (2, turns1))

            def turns1b(u, s):
                t = 2 * u + s
                pe.wait_ge(n1b_h, t + 1)
                pe.wait_ge(n1b_cp, t + 1)
                turn(PS[0:96, s, 128:256], hs[:, s, 64:160])
                turn(PS[0:64, s, 0:128], hs[:, s, 0:64]).then_inc(n1b_tr, 1)

            def project1(u, s):
                t = 2 * u + s
                pe.wait_ge(n1b_cp, t + 3)
                pe.wait_ge(n1b_out, t + 1)
                mm(PS[:, 2 + s, 0:160], hts[:, s, :], w["r1s"][:, :])
                mm(PS[:, 2 + s, 160:352], htv[:, s, :], w["r1v"][:, :]).then_inc(n1b_mm, 1)

            over_tiles(pe, (0, project1), (2, turns1b))

            def pickup(u, s, m):
                pair = 8 * u + 4 * s + m
                q = m % 2
                if m == 0:
                    pe.wait_ge(l1_loaded[s], 32 * (u + 1))
                    pe.wait_ge(pick_ready, 2 * u + s + 1)
                pe.wait_ge(parts_ready, pair + 7)
                for i in range(2):
                    j = 2 * m + i
                    last = mm(PS[:, 2 * q + i, 0:T1_COLS], pick[:, s, j * P:(j + 1) * P], t1w[:, s, :])
                last.then_inc(gath_mm, 1)

            def item1(u, s, item, window):
                for m in range(4):
                    pair = 8 * u + 4 * s + m
                    q = m % 2
                    if m < 2:
                        pickup(u, s, m + 2)
                    else:
                        pickup(u + s, 1 - s, m - 2)
                    pe.wait_ge(same_ready, pair + 6)
                    pe.wait_ge(msg_ready, pair + 9)
                    pe.wait_ge(out_ready, pair + 1)
                    for i in range(2):
                        j = 2 * m + i
                        last = mm(PS[:, 4 + q, (MSG + 1) * i:(MSG + 1) * (i + 1)], same[:, s, j * P:(j + 1) * P], msg[:, m, i, :])
                    last.then_inc(ded_done, 1)

            def layer1(general):
                pickup(0, 0, 0)
                pickup(0, 0, 1)
                items(pe, item1, general)
            by_input(pe, layer1)

            pe.wait_ge(l1_done, 1)
            def turns2(u, s):
                t = 2 * u + s
                pe.wait_ge(n2a_sum, t + 1)
                pe.wait_ge(n2a_cp, t + 1)
                turn(PS[0:96, s, 0:128], mt[:, s, :]).then_inc(n2a_tr, 1)

            def scalars2(u, s):
                t = 2 * u + s
                pe.wait_ge(n2a_cp, t + 3)
                pe.wait_ge(n2a_out, t + 1)
                mm(PS[:, 2 + s, 0:64], mtt[:, s, :], w["wa"][:, :]).then_inc(n2a_mm, 1)

            over_tiles(pe, (0, scalars2), (2, turns2))

            def head(t, s):
                pe.wait_ge(n2_h, t + 1)
                pe.wait_ge(n2_cp, t + 1)
                turn(PS[0:96, 0, 128:256], hs[:, s, 64:160])
                turn(PS[0:64, 0, 0:128], hs[:, s, 0:64])
                turn(PS[0:64, 0, 256:384], a_s[:, s, 0:64]).then_inc(n2_tr, 1)

            def tables(t, s):
                pe.wait_ge(n2_cp, t + 2)
                for i, (l, r) in enumerate(((hts, "u011"), (ats, "u101"))):
                    pe.wait_ge(n2_p, 4 * t + 2 * i + 2)
                    for h in range(2):
                        last = mm(PS[:, 1 + 2 * i + h, :], l[:, s, :], w[r][:, 512 * h:512 * (h + 1)])
                    last.then_inc(n2_t, 1)

            def turn4(t, s, e):
                c, h = divmod(e, 2)
                if h == 0 and c < 4:
                    pe.wait_ge(n2_z, 4 * t + c + 1)
                if h == 0 and c == 4:
                    pe.wait_ge(n2_g, 5 * t + 5)
                pe.wait_ge(n2_ev, 10 * t + e + 1)
                z = zout[:, c % 2, :] if c < 4 else gsum[:, s, :]
                for i in range(4):
                    last = turn(PS[:, 5 + h, P * i:P * i + P], z[:, 512 * h + P * i:512 * h + P * i + P])
                last.then_inc(n2_half, 1)

            def main4(t, e):
                pe.wait_ge(n2_ev, 10 * t + e + 3)
                wt, b0 = ("u000", 4 * e) if e < 8 else ("u110", 4 * (e - 8))
                for i in range(4):
                    last = mm(PS[:, 7, 0:64], zt[:, e % 2, P * i:P * i + P],
                              w[wt][:, 64 * (b0 + i):64 * (b0 + i + 1)], False, e == 9 and i == 3)
                last.then_inc(n2_main, 1)

            head(0, 0)
            tables(0, 0)
            with pe.Fori(0, UN) as u:
                for s in range(2):
                    t = 2 * u + s
                    turn4(t, s, 0)
                    pe.wait_ge(n2_acc, t + 2)
                    mm(PS[:, 7, 0:64], hts[:, s, :], w["lu0"][:, :], True, False)
                    mm(PS[:, 7, 64:160], htv[:, s, :], w["lu1"][:, :], False, True)
                    for e in range(7):
                        turn4(t, s, e + 1)
                        main4(t, e)
                        if e == 5:
                            head(t + 1, 1 - s)
                    main4(t, 7)
                    turn4(t, s, 8)
                    turn4(t, s, 9)
                    tables(t + 1, 1 - s)
                    main4(t, 8)
                    main4(t, 9)


N_FIRST = 4
N_LATE = 21
N_LOADS = 16


def kernel(**inputs):
    import numpy as np
    import concourse.bacc as bacc
    from concourse.bass_utils import run_bass_kernel_spmd

    src, dst = np.asarray(inputs["src"]), np.asarray(inputs["dst"])
    x, attr = np.asarray(inputs["x"]), np.asarray(inputs["node_vec1"])
    ea, es = np.asarray(inputs["edge_attr_4"]), np.asarray(inputs["edge_attr_64"])

    def padded(a, n, value=0):
        return np.concatenate([a, np.full((n - a.shape[0],) + a.shape[1:], value, a.dtype)])

    src, dst = padded(src, E_PAD, N_NODES), padded(dst, E_PAD, N_NODES)
    ea, es = padded(ea, E_PAD), padded(es, E_PAD)
    n = ITEMS + 1
    p = np.arange(P)
    cols = np.stack([p, 2.0 ** (64 - p), 2.5 * 2.0 ** (64 - p), TRASH + p], 1).astype(np.float32)
    arrays = {
        "x_in": padded(x, N_PAD),
        "a_in": padded(attr, N_PAD).reshape(NODE_TILES, P).T,
        "dst_in": dst.reshape(n * EDGE_TILES, P).T,
        "dstrow_in": dst.reshape(n, ITEM),
        "src_in": src.reshape(n, EDGE_TILES, P).transpose(0, 2, 1),
        "srcrow_in": src.reshape(n, ITEM),
        "ea_in": ea.reshape(n, EDGE_TILES, P, 4).transpose(0, 2, 1, 3).reshape(n, P, EDGE_TILES * 4),
        "es_in": es.reshape(n, 2, ITEM // 2, FC).transpose(0, 1, 3, 2).reshape(n, P, ITEM // 2),
        "ident_in": np.eye(P, dtype=np.float32),
        "iota_in": np.tile(p.astype(np.float32), (P, 1)),
        "cols_in": cols,
        "win_in": np.tile(np.append(P * np.arange(NODE_TILES), 0).astype(np.float32), (P, 1)),
    }
    for name in ("L0_gnn_lin1_ws", "L0_gnn_lin1_wv", "L0_gnn_fc_w1", "L0_gnn_fc_w2", "L0_gnn_sc_ws", "L0_gnn_sc_wv",
                 "L0_gnn_lin2_ws", "L0_gnn_lin2_wv", "L1_gnn_wm000", "L1_gnn_wm011", "L1_gnn_wm101",
                 "L1_gnn_wm110", "L1_gnn_lm0", "L1_gnn_lm1", "L1_gnn_wu000", "L1_gnn_wu011", "L1_gnn_wu101",
                 "L1_gnn_wu110", "L1_gnn_lu0", "L1_gnn_lu1"):
        arrays[name] = np.asarray(inputs[name])
    arrays = {k: np.ascontiguousarray(v) for k, v in arrays.items()}

    nc = bacc.Bacc("TRN2", target_bir_lowering=False, num_devices=1)
    args = [nc.dram_tensor(k, v.shape, mybir.dt.from_np(v.dtype), kind="ExternalInput").ap()
            for k, v in arrays.items()]
    out = nc.dram_tensor("out", (N_PAD, D), mybir.dt.float32, kind="ExternalOutput").ap()
    build(nc, *args, out)
    r = run_bass_kernel_spmd(nc, [arrays], core_ids=[0])
    return r.results[0]["out"][:N_NODES]
```
